# Optimizing a Trainium2 kernel written in Bass

```python
import numpy as np
import jax
import jax.numpy as jnp

def _softmax(x, axis=-1):
    return jax.nn.softmax(x, axis=axis)

def _gelu(x):
    return jax.nn.gelu(x, approximate=True)

def _silu(x):
    return jax.nn.silu(x)

def _sigmoid(x):
    return jax.nn.sigmoid(x)

def _layernorm(x, axis=-1, eps=1e-05):
    m = jnp.mean(x, axis=axis, keepdims=True)
    v = jnp.var(x, axis=axis, keepdims=True)
    return (x - m) / jnp.sqrt(v + eps)

def _scatter_add(tgt, idx, src, axis=0):
    return tgt.at[idx].add(src)

def _segment_sum(src, seg, n):
    return jax.ops.segment_sum(src, seg, n)
kernel_name = 'mk_xattn_ffn_d4_seqx_r8_ef2742'

def setup_inputs(seed: int=0):
    np.random.seed(seed)
    _w = jnp.asarray

    def _rec_inputs():
        import jax
        import jax.numpy as jnp
        _rk = jax.random.key(seed)
        x = -0.0002928 + 1 * jax.random.normal(jax.random.fold_in(_rk, 1), (32, 128, 128), jnp.float32)
        _lenS = 128 - jax.random.randint(jax.random.fold_in(_rk, 7), (32,), 0, max(1, 128 // 4) + 1, jnp.int32)
        _lenS2 = 77 - jax.random.randint(jax.random.fold_in(_rk, 8), (32,), 0, max(1, 77 // 4) + 1, jnp.int32)
        _ctx_1024P = jax.random.normal(jax.random.fold_in(_rk, 11), (32, 16, 128), jnp.float32)
        _ctx_1024c = jax.random.dirichlet(jax.random.fold_in(_rk, 511), 0.3 * jnp.ones((16,), jnp.float32), (32, 77))
        _ctx_1024t = jnp.einsum('bsk,bkd->bsd', _ctx_1024c, _ctx_1024P)
        _ctx_1024t = _ctx_1024t * jax.lax.rsqrt(jnp.mean(jnp.square(_ctx_1024t)) + 1e-12) * 0.953939
        ctx_1024 = -1.39393e-06 + 0.999914 * (_ctx_1024t + 0.3 * jax.random.normal(jax.random.fold_in(_rk, 611), (32, 77, 128), jnp.float32))
        _validS = jnp.arange(128)[None, :] < _lenS[:, None]
        _validS2 = jnp.arange(77)[None, :] < _lenS2[:, None]
        _causal = jnp.tril(jnp.ones((128, 128), dtype=bool))
        mask_1x1xSxS2_ik0 = jnp.where(jnp.broadcast_to(_validS2[0:1, None, None, :], (1, 1, 128, 77)), 0, 1).astype(jnp.int32)
        return (x, ctx_1024, mask_1x1xSxS2_ik0)
    x, ctx_1024, mask_1x1xSxS2_ik0 = _rec_inputs()

    def _L0_xattn_setup():
        import jax, jax.numpy as jnp
        import numpy as np
        EMBED_DIM = 128
        NUM_HEADS = 16
        HEAD_DIM = EMBED_DIM // NUM_HEADS
        key = jax.random.key(seed)
        ks = jax.random.split(key, 7)
        B, S, E = (2, 256, EMBED_DIM)
        bound = float(np.sqrt(6.0 / (E + E)))
        mkw = lambda k: jax.random.uniform(k, (E, E), jnp.float32, -bound, bound)
        return {'query': jax.random.normal(ks[0], (B, S, E), jnp.float32), 'key': jax.random.normal(ks[1], (B, S, E), jnp.float32), 'value': jax.random.normal(ks[2], (B, S, E), jnp.float32), 'Wq': mkw(ks[3]), 'Wk': mkw(ks[4]), 'Wv': mkw(ks[5]), 'Wo': mkw(ks[6])}
    _L0_xattn_all = _L0_xattn_setup()
    _L0_xattn_in = {k: v for k, v in _L0_xattn_all.items() if k in ('Wq', 'Wk', 'Wv', 'Wo')}
    del _L0_xattn_all

    def _L0_ffn_setup():
        import jax, jax.numpy as jnp
        import numpy as np
        NUM_EXPERTS = 8
        TOP_K = 2
        CAPACITY_FACTOR = 1.0

        def _dispatch_compute(xf, top_expert, w1, w2, capacity):
            tokens, hs = xf.shape
            tpe = jnp.bincount(top_expert, length=NUM_EXPERTS)
            indices = jnp.argsort(top_expert)
            offsets = jnp.concatenate([jnp.zeros((1,), tpe.dtype), jnp.cumsum(tpe)[:-1]])
            slot = jnp.arange(capacity)
            pos = offsets[:, None] + slot[None, :]
            valid = slot[None, :] < tpe[:, None]
            tok_idx = indices[jnp.minimum(pos, tokens - 1)]
            xe = jnp.where(valid[..., None], xf[tok_idx], 0.0)
            h = jax.nn.gelu(jnp.einsum('ech,ehf->ecf', xe, w1), approximate=True)
            ye = jnp.einsum('ecf,efh->ech', h, w2)
            tok_safe = jnp.where(valid, tok_idx, tokens)
            out = jnp.zeros((tokens + 1, hs), xf.dtype).at[tok_safe.reshape(-1)].add(ye.reshape(-1, hs))
            return out[:tokens]
        key = jax.random.key(seed)
        k1, k2, k3, k4 = jax.random.split(key, 4)
        hs, ffn = (128, 512)
        x = jax.random.normal(k1, (256, 2, hs), dtype=jnp.float32)
        router_w = jax.random.normal(k2, (hs, NUM_EXPERTS), dtype=jnp.float32) * hs ** (-0.5)
        w1 = jax.random.normal(k3, (NUM_EXPERTS, hs, ffn), dtype=jnp.float32) * 0.02
        w2 = jax.random.normal(k4, (NUM_EXPERTS, ffn, hs), dtype=jnp.float32) * 0.02
        bias = jnp.zeros((1, 1, hs), dtype=jnp.float32)
        return {'x': x, 'router_w': router_w, 'w1': w1, 'w2': w2, 'bias': bias}
    _L0_ffn_all = _L0_ffn_setup()
    _L0_ffn_in = {k: v for k, v in _L0_ffn_all.items() if k in ('router_w', 'w1', 'w2', 'bias')}
    del _L0_ffn_all

    def _L1_xattn_setup():
        import jax, jax.numpy as jnp
        import numpy as np
        key = jax.random.key(seed)
        k1, k2 = jax.random.split(key)
        B, Tq, Tk, D = (8, 256, 256, 128)
        query = jax.random.normal(k1, (B, Tq, D), dtype=jnp.float32)
        key_t = jax.random.normal(k2, (B, Tk, D), dtype=jnp.float32)
        return {'query': query, 'key': key_t}
    _L1_xattn_all = _L1_xattn_setup()
    _L1_xattn_in = {k: v for k, v in _L1_xattn_all.items() if k in ()}
    del _L1_xattn_all

    def _L1_ffn_setup():
        import jax, jax.numpy as jnp
        import numpy as np
        TOP_K = 2

        def _swiglu_mlp(x, wgu, wd, inter):
            gu = x @ wgu
            a = jax.nn.silu(gu[:, :inter]) * gu[:, inter:]
            return a @ wd
        key = jax.random.key(seed)
        ks = jax.random.split(key, 6)
        H, I, E = (128, 352, 8)
        B, S = (2, 128)
        w = 0.02
        return {'x': jax.random.normal(ks[0], (B, S, H), jnp.float32), 'gate_w': jax.random.normal(ks[1], (H, E), jnp.float32) * w, 'base_wgu': jax.random.normal(ks[2], (H, 2 * I), jnp.float32) * w, 'base_wd': jax.random.normal(ks[3], (I, H), jnp.float32) * w, 'exp_wgu': jax.random.normal(ks[4], (E, H, 2 * I), jnp.float32) * w, 'exp_wd': jax.random.normal(ks[5], (E, I, H), jnp.float32) * w}
    _L1_ffn_all = _L1_ffn_setup()
    _L1_ffn_in = {k: v for k, v in _L1_ffn_all.items() if k in ('gate_w', 'base_wgu', 'base_wd', 'exp_wgu', 'exp_wd')}
    del _L1_ffn_all

    def _L2_xattn_setup():
        import jax, jax.numpy as jnp
        import numpy as np
        E, T, H, F = (8, 256, 128, 512)
        key = jax.random.key(seed)
        k1, k2, k3 = jax.random.split(key, 3)
        x = jax.random.normal(k1, (E, T, H), dtype=jnp.float32)
        w1 = jax.random.normal(k2, (E, F, H), dtype=jnp.float32) * 0.02
        w2 = jax.random.normal(k3, (E, F, H), dtype=jnp.float32) * 0.02
        return {'x': x, 'w1': w1, 'w2': w2}
    _L2_xattn_all = _L2_xattn_setup()
    _L2_xattn_in = {k: v for k, v in _L2_xattn_all.items() if k in ()}
    del _L2_xattn_all

    def _L2_ffn_setup():
        import jax, jax.numpy as jnp
        import numpy as np
        B, S, DIM = (2, 256, 128)
        HID = 256
        E, NSH, TOPK = (8, 2, 2)

        def _ffn(x, w1, w2, w3):
            return jax.nn.silu(x @ w1.T) * (x @ w3.T) @ w2.T
        key = jax.random.key(seed)
        ks = jax.random.split(key, 8)
        sc = 0.02
        return {'x': jax.random.normal(ks[0], (B, S, DIM), jnp.float32), 'router_w': jax.random.normal(ks[1], (E, DIM), jnp.float32) * sc, 'expert_bias': jnp.zeros((E,), jnp.float32), 'w1': jax.random.normal(ks[2], (E, HID, DIM), jnp.float32) * sc, 'w3': jax.random.normal(ks[3], (E, HID, DIM), jnp.float32) * sc, 'w2': jax.random.normal(ks[4], (E, DIM, HID), jnp.float32) * sc, 'sw1': jax.random.normal(ks[5], (NSH, HID, DIM), jnp.float32) * sc, 'sw3': jax.random.normal(ks[6], (NSH, HID, DIM), jnp.float32) * sc, 'sw2': jax.random.normal(ks[7], (NSH, DIM, HID), jnp.float32) * sc}
    _L2_ffn_all = _L2_ffn_setup()
    _L2_ffn_in = {k: v for k, v in _L2_ffn_all.items() if k in ('router_w', 'expert_bias', 'w1', 'w3', 'w2', 'sw1', 'sw3', 'sw2')}
    del _L2_ffn_all

    def _L3_xattn_setup():
        import jax, jax.numpy as jnp
        import numpy as np
        D_MODEL = 128
        HEADS = 16
        D_K = D_MODEL // HEADS
        B, S = (4, 256)
        key = jax.random.key(seed)
        ks = jax.random.split(key, 12)
        xav = float(np.sqrt(6.0 / (D_MODEL + D_MODEL)))
        inp = {'query': jax.random.normal(ks[0], (B, S, D_MODEL), jnp.float32), 'key': jax.random.normal(ks[1], (B, S, D_MODEL), jnp.float32), 'value': jax.random.normal(ks[2], (B, S, D_MODEL), jnp.float32), 'mask': jnp.tril(jnp.ones((S, S), jnp.int32))[None, None], 'Wq': jax.random.uniform(ks[3], (D_MODEL, D_MODEL), jnp.float32, -xav, xav), 'bq': jnp.zeros((D_MODEL,), jnp.float32), 'Wk': jax.random.uniform(ks[4], (D_MODEL, D_MODEL), jnp.float32, -xav, xav), 'bk': jnp.zeros((D_MODEL,), jnp.float32), 'Wv': jax.random.uniform(ks[5], (D_MODEL, D_MODEL), jnp.float32, -xav, xav), 'bv': jnp.zeros((D_MODEL,), jnp.float32), 'Wo': jax.random.uniform(ks[6], (D_MODEL, D_MODEL), jnp.float32, -xav, xav), 'bo': jnp.zeros((D_MODEL,), jnp.float32)}
        return inp
    _L3_xattn_all = _L3_xattn_setup()
    _L3_xattn_in = {k: v for k, v in _L3_xattn_all.items() if k in ('Wq', 'bq', 'Wk', 'bk', 'Wv', 'bv', 'Wo', 'bo')}
    del _L3_xattn_all

    def _L3_ffn_setup():
        import jax, jax.numpy as jnp
        import numpy as np
        CAPACITY_FACTOR = 1.25
        key = jax.random.key(seed)
        k1, k2, k3, k4 = jax.random.split(key, 4)
        B, T, D, F, E = (4, 512, 128, 512, 8)
        s = 0.02
        return {'x': jax.random.normal(k1, (B, T, D), dtype=jnp.float32), 'wg': jax.random.normal(k2, (D, E), dtype=jnp.float32) * s, 'W1': jax.random.normal(k3, (E, D, F), dtype=jnp.float32) * s, 'b1': jnp.zeros((E, F), dtype=jnp.float32), 'W2': jax.random.normal(k4, (E, F, D), dtype=jnp.float32) * s, 'b2': jnp.zeros((E, D), dtype=jnp.float32)}
    _L3_ffn_all = _L3_ffn_setup()
    _L3_ffn_in = {k: v for k, v in _L3_ffn_all.items() if k in ('wg', 'W1', 'b1', 'W2', 'b2')}
    del _L3_ffn_all
    return {'x': x, 'ctx_1024': ctx_1024, 'mask_1x1xSxS2_ik0': mask_1x1xSxS2_ik0, 'L0_xattn_Wq': _L0_xattn_in['Wq'], 'L0_xattn_Wk': _L0_xattn_in['Wk'], 'L0_xattn_Wv': _L0_xattn_in['Wv'], 'L0_xattn_Wo': _L0_xattn_in['Wo'], 'L0_ffn_router_w': _L0_ffn_in['router_w'], 'L0_ffn_w1': _L0_ffn_in['w1'], 'L0_ffn_w2': _L0_ffn_in['w2'], 'L0_ffn_bias': _L0_ffn_in['bias'], 'L1_ffn_gate_w': _L1_ffn_in['gate_w'], 'L1_ffn_base_wgu': _L1_ffn_in['base_wgu'], 'L1_ffn_base_wd': _L1_ffn_in['base_wd'], 'L1_ffn_exp_wgu': _L1_ffn_in['exp_wgu'], 'L1_ffn_exp_wd': _L1_ffn_in['exp_wd'], 'L2_ffn_router_w': _L2_ffn_in['router_w'], 'L2_ffn_expert_bias': _L2_ffn_in['expert_bias'], 'L2_ffn_w1': _L2_ffn_in['w1'], 'L2_ffn_w3': _L2_ffn_in['w3'], 'L2_ffn_w2': _L2_ffn_in['w2'], 'L2_ffn_sw1': _L2_ffn_in['sw1'], 'L2_ffn_sw3': _L2_ffn_in['sw3'], 'L2_ffn_sw2': _L2_ffn_in['sw2'], 'L3_xattn_Wq': _L3_xattn_in['Wq'], 'L3_xattn_bq': _L3_xattn_in['bq'], 'L3_xattn_Wk': _L3_xattn_in['Wk'], 'L3_xattn_bk': _L3_xattn_in['bk'], 'L3_xattn_Wv': _L3_xattn_in['Wv'], 'L3_xattn_bv': _L3_xattn_in['bv'], 'L3_xattn_Wo': _L3_xattn_in['Wo'], 'L3_xattn_bo': _L3_xattn_in['bo'], 'L3_ffn_wg': _L3_ffn_in['wg'], 'L3_ffn_W1': _L3_ffn_in['W1'], 'L3_ffn_b1': _L3_ffn_in['b1'], 'L3_ffn_W2': _L3_ffn_in['W2'], 'L3_ffn_b2': _L3_ffn_in['b2']}

def reference(x, ctx_1024, mask_1x1xSxS2_ik0, L0_xattn_Wq, L0_xattn_Wk, L0_xattn_Wv, L0_xattn_Wo, L0_ffn_router_w, L0_ffn_w1, L0_ffn_w2, L0_ffn_bias, L1_ffn_gate_w, L1_ffn_base_wgu, L1_ffn_base_wd, L1_ffn_exp_wgu, L1_ffn_exp_wd, L2_ffn_router_w, L2_ffn_expert_bias, L2_ffn_w1, L2_ffn_w3, L2_ffn_w2, L2_ffn_sw1, L2_ffn_sw3, L2_ffn_sw2, L3_xattn_Wq, L3_xattn_bq, L3_xattn_Wk, L3_xattn_bk, L3_xattn_Wv, L3_xattn_bv, L3_xattn_Wo, L3_xattn_bo, L3_ffn_wg, L3_ffn_W1, L3_ffn_b1, L3_ffn_W2, L3_ffn_b2):
    import jax
    import jax.numpy as jnp

    def _L0_xattn_ref(query, key, value, Wq, Wk, Wv, Wo):
        import jax, jax.numpy as jnp
        import numpy as np
        EMBED_DIM = 128
        NUM_HEADS = 16
        HEAD_DIM = EMBED_DIM // NUM_HEADS
        B, L, E = query.shape
        H, D = (NUM_HEADS, HEAD_DIM)
        scale = D ** (-0.5)
        q = (query @ Wq.T).reshape(B, L, H, D) * scale
        k = (key @ Wk.T).reshape(B, -1, H, D)
        v = (value @ Wv.T).reshape(B, -1, H, D)
        scores = jax.nn.sigmoid(jnp.einsum('blhd,bshd->bhls', q, k))
        o = jnp.einsum('bhls,bshd->blhd', scores, v).reshape(B, L, E)
        return o @ Wo.T

    def _L0_ffn_ref(x, router_w, w1, w2, bias):
        import jax, jax.numpy as jnp
        import numpy as np
        NUM_EXPERTS = 8
        TOP_K = 2
        CAPACITY_FACTOR = 1.0

        def _dispatch_compute(xf, top_expert, w1, w2, capacity):
            tokens, hs = xf.shape
            tpe = jnp.bincount(top_expert, length=NUM_EXPERTS)
            indices = jnp.argsort(top_expert)
            offsets = jnp.concatenate([jnp.zeros((1,), tpe.dtype), jnp.cumsum(tpe)[:-1]])
            slot = jnp.arange(capacity)
            pos = offsets[:, None] + slot[None, :]
            valid = slot[None, :] < tpe[:, None]
            tok_idx = indices[jnp.minimum(pos, tokens - 1)]
            xe = jnp.where(valid[..., None], xf[tok_idx], 0.0)
            h = jax.nn.gelu(jnp.einsum('ech,ehf->ecf', xe, w1), approximate=True)
            ye = jnp.einsum('ecf,efh->ech', h, w2)
            tok_safe = jnp.where(valid, tok_idx, tokens)
            out = jnp.zeros((tokens + 1, hs), xf.dtype).at[tok_safe.reshape(-1)].add(ye.reshape(-1, hs))
            return out[:tokens]
        sl, bs, hs = x.shape
        tokens = sl * bs
        capacity = int(CAPACITY_FACTOR * tokens / NUM_EXPERTS)
        xf = x.reshape(tokens, hs)
        scores = jax.nn.softmax(xf @ router_w, axis=-1)
        expert_weights, top_experts = jax.lax.top_k(scores, TOP_K)
        out = jnp.zeros_like(xf)
        for k in range(TOP_K):
            y = _dispatch_compute(xf, top_experts[:, k].astype(jnp.int32), w1, w2, capacity)
            out = out + y * expert_weights[:, k][:, None]
        return out.reshape(sl, bs, hs) + bias

    def _L1_xattn_ref(query, key):
        import jax, jax.numpy as jnp
        import numpy as np
        energy = jnp.einsum('bqd,bkd->bqk', query, key)
        attention = jax.nn.softmax(energy, axis=-1)
        return jnp.einsum('bqk,bkd->bqd', attention, key)

    def _L1_ffn_ref(x, gate_w, base_wgu, base_wd, exp_wgu, exp_wd):
        import jax, jax.numpy as jnp
        import numpy as np
        TOP_K = 2

        def _swiglu_mlp(x, wgu, wd, inter):
            gu = x @ wgu
            a = jax.nn.silu(gu[:, :inter]) * gu[:, inter:]
            return a @ wd
        orig_shape = x.shape
        H = orig_shape[-1]
        I = base_wd.shape[0]
        E = gate_w.shape[1]
        xt = x.reshape(-1, H)
        T = xt.shape[0]
        base_y = _swiglu_mlp(xt, base_wgu, base_wd, I)
        logits = xt @ gate_w
        probs = jax.nn.softmax(logits.astype(jnp.float32), axis=-1)
        topw, topi = jax.lax.top_k(probs, TOP_K)
        topw = topw / jnp.sum(topw, axis=-1, keepdims=True)
        topw = topw.astype(x.dtype)
        cw = jnp.zeros((T, E), x.dtype).at[jnp.arange(T)[:, None], topi].add(topw)
        out = base_y
        for e in range(E):
            ye = _swiglu_mlp(xt, exp_wgu[e], exp_wd[e], I)
            out = out + cw[:, e:e + 1] * ye
        return out.reshape(orig_shape)

    def _L2_xattn_ref(x, w1, w2):
        import jax, jax.numpy as jnp
        import numpy as np
        E, T, H, F = (8, 256, 128, 512)
        h = jnp.einsum('eth,efh->etf', x, w1)
        a = jax.nn.gelu(h, approximate=True)
        return jnp.einsum('etf,efh->eth', a, w2)

    def _L2_ffn_ref(x, router_w, expert_bias, w1, w3, w2, sw1, sw3, sw2):
        import jax, jax.numpy as jnp
        import numpy as np
        B, S, DIM = (2, 256, 128)
        HID = 256
        E, NSH, TOPK = (8, 2, 2)

        def _ffn(x, w1, w2, w3):
            return jax.nn.silu(x @ w1.T) * (x @ w3.T) @ w2.T
        bs, sl, d = x.shape
        xf = x.reshape(-1, d)
        shared = jnp.zeros_like(xf)
        for i in range(sw1.shape[0]):
            shared = shared + _ffn(xf, sw1[i], sw2[i], sw3[i])
        logits = xf @ router_w.T + expert_bias
        rw, sel = jax.lax.top_k(logits, TOPK)
        rw = jax.nn.softmax(rw.astype(jnp.float32), axis=-1).astype(x.dtype)
        onehot = jax.nn.one_hot(sel, E, dtype=x.dtype)
        combine = jnp.einsum('tk,tke->te', rw, onehot)

        def body(acc, ew):
            e1, e3, e2, cw = ew
            acc = acc + cw[:, None] * _ffn(xf, e1, e2, e3)
            return (acc, None)
        out, _ = jax.lax.scan(body, jnp.zeros_like(xf), (w1, w3, w2, combine.T))
        out = out + shared
        return out.reshape(bs, sl, -1)

    def _L3_xattn_ref(query, key, value, mask, Wq, bq, Wk, bk, Wv, bv, Wo, bo):
        import jax, jax.numpy as jnp
        import numpy as np
        D_MODEL = 128
        HEADS = 16
        D_K = D_MODEL // HEADS
        B, S = (4, 256)
        b, s, d = query.shape
        Q = (jnp.einsum('bsd,ed->bse', query, Wq) + bq).reshape(b, s, HEADS, D_K).transpose(0, 2, 1, 3)
        K = (jnp.einsum('bsd,ed->bse', key, Wk) + bk).reshape(b, -1, HEADS, D_K).transpose(0, 2, 1, 3)
        V = (jnp.einsum('bsd,ed->bse', value, Wv) + bv).reshape(b, -1, HEADS, D_K).transpose(0, 2, 1, 3)
        scale = 1.0 / jnp.sqrt(jnp.asarray(D_K, query.dtype))
        scores = jnp.einsum('bhqd,bhkd->bhqk', Q, K) * scale
        scores = jnp.where(mask == 0, -jnp.inf, scores)
        attn = jax.nn.softmax(scores, axis=-1)
        attn = jnp.where(jnp.isnan(attn), jnp.zeros_like(attn), attn)
        out = jnp.einsum('bhqk,bhkd->bhqd', attn, V)
        out = out.transpose(0, 2, 1, 3).reshape(b, s, d)
        return jnp.einsum('bsd,ed->bse', out, Wo) + bo

    def _L3_ffn_ref(x, wg, W1, b1, W2, b2):
        import jax, jax.numpy as jnp
        import numpy as np
        CAPACITY_FACTOR = 1.25
        B, T, D = x.shape
        E = wg.shape[1]
        N = B * T
        capacity = int(N / E * CAPACITY_FACTOR) + 1
        xf = x.reshape(N, D)
        logits = xf @ wg
        scores = jax.nn.softmax(logits, axis=-1)
        top1 = jnp.argmax(scores, axis=-1)
        combine_w = jnp.take_along_axis(scores, top1[:, None], axis=1)[:, 0]
        oh = jax.nn.one_hot(top1, E, dtype=jnp.int32)
        rank = jnp.take_along_axis(jnp.cumsum(oh, axis=0), top1[:, None], axis=1)[:, 0] - 1
        valid = rank < capacity
        trash = E * capacity
        slot = jnp.where(valid, top1 * capacity + rank, trash)
        buf = jnp.zeros((E * capacity + 1, D), dtype=x.dtype).at[slot].set(xf)
        eb = buf[:E * capacity].reshape(E, capacity, D)
        h = jax.nn.gelu(jnp.einsum('ecd,edf->ecf', eb, W1) + b1[:, None, :], approximate=False)
        y = jnp.einsum('ecf,efd->ecd', h, W2) + b2[:, None, :]
        yf = y.reshape(E * capacity, D)
        gathered = yf[jnp.minimum(slot, E * capacity - 1)]
        out_flat = jnp.where(valid[:, None], gathered, 0.0) * combine_w[:, None]
        return out_flat.reshape(B, T, D)
    x = x + _L0_xattn_ref(_layernorm(x, axis=-1), ctx_1024, ctx_1024, L0_xattn_Wq, L0_xattn_Wk, L0_xattn_Wv, L0_xattn_Wo)
    x = x + _L0_ffn_ref(_layernorm(x, axis=-1), L0_ffn_router_w, L0_ffn_w1, L0_ffn_w2, L0_ffn_bias)
    x = x + _L1_xattn_ref(_layernorm(x, axis=-1), ctx_1024)
    x = x + _L1_ffn_ref(_layernorm(x, axis=-1), L1_ffn_gate_w, L1_ffn_base_wgu, L1_ffn_base_wd, L1_ffn_exp_wgu, L1_ffn_exp_wd)
    x = x + _L2_xattn_ref(_layernorm(x, axis=-1), ctx_1024, ctx_1024)
    x = x + _L2_ffn_ref(_layernorm(x, axis=-1), L2_ffn_router_w, L2_ffn_expert_bias, L2_ffn_w1, L2_ffn_w3, L2_ffn_w2, L2_ffn_sw1, L2_ffn_sw3, L2_ffn_sw2)
    x = x + _L3_xattn_ref(_layernorm(x, axis=-1), ctx_1024, ctx_1024, mask_1x1xSxS2_ik0, L3_xattn_Wq, L3_xattn_bq, L3_xattn_Wk, L3_xattn_bk, L3_xattn_Wv, L3_xattn_bv, L3_xattn_Wo, L3_xattn_bo)
    x = x + _L3_ffn_ref(_layernorm(x, axis=-1), L3_ffn_wg, L3_ffn_W1, L3_ffn_b1, L3_ffn_W2, L3_ffn_b2)
    return x

_drawn_inputs = setup_inputs


def setup_inputs(seed=0):
    import zlib

    import numpy as np

    out = dict(_drawn_inputs(seed))
    spreads = {'L0_ffn_bias': (0.0, 0.8),
     'L2_ffn_expert_bias': (0.0, 2.0),
     'L3_xattn_bq': (0.0, 0.8),
     'L3_xattn_bk': (0.0, 2.0),
     'L3_xattn_bv': (0.0, 2.0),
     'L3_xattn_bo': (0.0, 2.0),
     'L3_ffn_b1': (0.0, 2.0),
     'L3_ffn_b2': (0.0, 2.0)}
    factors = {'L0_ffn_router_w': 8.0,
     'L0_ffn_w1': 8.0,
     'L0_ffn_w2': 8.0,
     'L1_ffn_gate_w': 8.0,
     'L1_ffn_base_wgu': 8.0,
     'L1_ffn_base_wd': 8.0,
     'L1_ffn_exp_wgu': 8.0,
     'L1_ffn_exp_wd': 8.0,
     'L2_ffn_router_w': 27.99,
     'L2_ffn_w1': 28.375,
     'L2_ffn_w3': 25.266,
     'L2_ffn_w2': 24.974,
     'L2_ffn_sw1': 8.0,
     'L2_ffn_sw3': 8.0,
     'L2_ffn_sw2': 8.0,
     'L3_xattn_Wq': 8.0,
     'L3_xattn_Wk': 8.0,
     'L3_xattn_Wv': 8.0,
     'L3_xattn_Wo': 8.0,
     'L3_ffn_wg': 54.79,
     'L3_ffn_W1': 64.0,
     'L3_ffn_W2': 60.338}
    for name, (base, spread) in spreads.items():
        noise = np.random.default_rng([zlib.crc32(name.encode()), seed]).standard_normal(out[name].shape)
        drawn = base * np.exp(spread * noise) if base else spread * noise
        out[name] = jnp.asarray(drawn.astype(out[name].dtype))
    for name, factor in factors.items():
        out[name] = (out[name] * factor).astype(out[name].dtype)
    return out
```

```python
from contextlib import ExitStack

import concourse.bass as bass
from concourse import mybir

F32 = mybir.dt.float32
BF16 = mybir.dt.bfloat16
I32 = mybir.dt.int32
U32 = mybir.dt.uint32
ALU = mybir.AluOpType
ACT = mybir.ActivationFunctionType
AX = mybir.AxisListType

P = 128
B, D, KV = 32, 128, 77
TG = 4
NG = B // TG
GT = TG * P
GK = TG * KV
NH, HD = 16, 8
HQ = 32 // HD
NE = 8
EPS = 1e-5
MASKED = -1e30
CAP0 = B * P // NE
CAP3 = int(B * P / NE * 1.25) + 1

C_ID, C_TRI, C_HM, C_IOTA, C_ONE, C_ZERO = 0, 128, 256, 260, 268, 269
C_N = 272
SMALL = {}
_at = 0
for _n, _w in (("bq3", 1), ("bk3", 1), ("bv3", D), ("bo3", D), ("bias0", D), ("ebias2", NE),
               ("rw0", NE), ("rw1", NE), ("rw2", NE), ("rw3", NE), ("b1", NE * 4), ("b2", TG * D)):
    SMALL[_n] = (_at, _w)
    _at += _w
SMALL_N = _at
AW = ("q0", "k0", "v0", "o0", "q3", "k3", "v3", "o3")


class Steps:

    def __init__(self, eng, sem, base):
        self.eng, self.sem, self.base, self.n = eng, sem, base, 0

    def do(self, ins):
        ins.then_inc(self.sem, 1)
        self.n += 1

    def settle(self, apart=False):
        self.eng.wait_ge(self.sem, self.base + self.n)
        if apart:
            self.eng.nop(nofuse=True)


def moe_plan(kind):
    if kind == "l1":
        f = 352
        chunks = [(0, 128), (128, 128), (256, 96)]
        return dict(f=f, chunks=chunks, experts=NE + 1, plain=1, glu=True, banks=3, slots=3)
    if kind == "l2":
        return dict(f=256, chunks=[(0, 128), (128, 128)], experts=NE + 2, plain=2, glu=True, banks=4, slots=4)
    return dict(f=512, chunks=[(128 * c, 128) for c in range(4)], experts=NE, plain=0, glu=False, banks=4, slots=4)


def build(nc, ins, out):
    ctx = ExitStack()
    with ctx:
        def sb(name, shape, dt=F32):
            return ctx.enter_context(nc.sbuf_tensor(name, shape, dt))

        def sem(name):
            return ctx.enter_context(nc.semaphore(name))

        x = sb("x", [P, B * D])
        ctxT = sb("ctxT", [P, B * KV])
        ctxk = sb("ctxk", [KV, B * D])
        const = sb("const", [P, C_N])
        small = sb("small", [P, SMALL_N])
        aw = sb("aw", [P, len(AW) * D])
        w_even = sb("w_even", [P, 8192])
        w_odd = sb("w_odd", [P, 9 * 704 + 9 * 3 * 128])
        z = sb("z", [P, GT])
        zT = sb("zT", [P, GT])
        bn = sb("bn", [P, TG, 6])
        mv = sb("mv", [P, TG, 2])
        ve = sb("ve", [P, TG])
        rstd = sb("rstd", [P, TG])
        mhalf = sb("mhalf", [P, TG])
        id_bf = sb("id_bf", [P, P], BF16)
        tri_bf = sb("tri_bf", [P, P], BF16)
        one_bf = sb("one_bf", [P, P], BF16)
        mask_i = sb("mask_i", [P, KV], I32)
        mask_b = sb("mask_b", [P, KV], BF16)
        mask_v = sb("mask_v", [P, KV])
        rowok = sb("rowok", [P, 1])
        hid = sb("hid", [P, 2, 4, GT])
        aux = sb("aux", [P, 4, GT])
        qT = sb("qT", [P, GT])
        kmask = sb("kmask", [P, TG, HQ, KV])
        vS = sb("vS", [KV, TG, NH, HD + 1])
        ctxg = sb("ctxg", [P, GK])
        oS = sb("oS", [P, 2, D])
        oT = sb("oT", [P, 2, D])
        mx = sb("mx", [P, NH])
        rs = sb("rs", [P, NH])
        tmp = sb("tmp", [P, D])
        pt = sb("pt", [KV, 2, NH, P])
        lg = sb("lg", [P, TG, NE])
        ls = sb("ls", [P, TG, NE])
        el = sb("el", [P, TG, NE])
        mx8 = sb("mx8", [P, TG, 8])
        ix8 = sb("ix8", [P, TG, 8], U32)
        ixf = sb("ixf", [P, TG, 2])
        oh = sb("oh", [P, TG, 2, NE], BF16)
        rank = sb("rank", [P, TG, 2 * NE])
        ohv = sb("ohv", [P, TG, 2, NE])
        count = sb("count", [P, 2 * NE])
        sel = sb("sel", [P, TG, NE])
        den = sb("den", [P, TG])
        rden = sb("rden", [P, TG])
        cw = sb("cw", [P, TG, 32])
        cwT = sb("cwT", [P, P])
        banks = ctx.enter_context(nc.psum_tensor("banks", [P, 8, 512], F32))

        ident = const[:, C_ID:C_ID + P]
        hm = const[:, C_HM:C_HM + HQ]
        iota8 = const[:, C_IOTA:C_IOTA + NE]
        zero1 = const[:, C_ZERO:C_ZERO + 1]

        def sm(name):
            a, w = SMALL[name]
            return small[:, a:a + w]

        def weight(name):
            i = AW.index(name)
            return aw[:, i * D:(i + 1) * D]

        loaded = sem("loaded")
        w_loaded = [sem(f"w_loaded{i}") for i in range(4)]
        var_ready = sem("var_ready")
        rstd_ready = sem("rstd_ready")
        z_ready = sem("z_ready")
        zt_ready = sem("zt_ready")
        zT_ready = sem("zT_ready")
        dve_step = sem("dve_step")
        pool_step = sem("pool_step")
        stored = sem("stored")

        def psum_copy_of(bank):
            return banks[:, bank, :]

        def norm_stats(dve, st, at):
            for i in range(TG):
                st.do(nc.vector.bn_stats(bn[:, i, :], x[:, bass.ds(at + i * D, D)]))
            st.settle(apart=True)
            for i in range(TG):
                st.do(nc.vector.bn_aggr(mv[:, i, :], bn[:, i, :]))
            st.settle()
            nc.vector.tensor_scalar(ve[:, :], mv[:, :, 1], EPS, None, ALU.add).then_inc(var_ready, 1)

        def norm_apply(dve, n, at, first=False):
            dve.wait_ge(rstd_ready, n)
            if not first:
                dve.wait_ge(zt_ready, n - 1)
            for i in range(TG):
                r = nc.vector.tensor_scalar(z[:, i * D:(i + 1) * D], x[:, bass.ds(at + i * D, D)],
                                            mv[:, i, 0:1], rstd[:, i:i + 1], ALU.subtract, ALU.mult)
            r.then_inc(z_ready, 1)

        def norm_power(pool, n):
            pool.wait_ge(var_ready, n)
            nc.gpsimd.tensor_tensor(rstd[:, :], ve[:, :], mhalf[:, :], ALU.pow).then_inc(rstd_ready, 1)

        def norm_transpose(pe, n, bank):
            pe.wait_ge(z_ready, n)
            for i in range(TG):
                r = nc.tensor.transpose(banks[:, bank, i * P:(i + 1) * P], z[:, i * D:(i + 1) * D], ident)
            r.then_inc(zt_ready, 1)

        def norm_store(act, n, bank):
            act.wait_ge(zt_ready, n)
            nc.scalar.copy(zT[:, :], banks[:, bank, :]).then_inc(zT_ready, 1)

        dve_base = [0]

        with nc.Block() as block:
            @block.sync
            def _(sp):
                sp.dma_start(x[:, 0:GT], ins["x"][:, 0:GT]).then_inc(loaded, 16)
                sp.dma_start(const[:], ins["const"]).then_inc(loaded, 16)
                sp.dma_start(aw[:], ins["aw"]).then_inc(loaded, 16)
                sp.dma_start(ctxT[:], ins["ctxT"]).then_inc(loaded, 16)
                sp.dma_start(mask_i[:], ins["mask"]).then_inc(loaded, 16)
                sp.dma_start(x[:, GT:], ins["x"][:, GT:]).then_inc(loaded, 16)
                sp.dma_start(small[:], ins["small"]).then_inc(loaded, 16)
                sp.dma_start(ctxk[:], ins["ctxk"]).then_inc(loaded, 16)
                sp.dma_start(w_even[:, :], ins["w0"]).then_inc(w_loaded[0], 16)
                sp.dma_start(w_odd[:, :], ins["w1"]).then_inc(w_loaded[1], 16)
                sp.wait_ge(loaded, 16 * 8)

            @block.gpsimd
            def _(pool):
                nc.gpsimd.memset(mhalf[:], -0.5).then_inc(pool_step, 1)
                nc.gpsimd.memset(one_bf[:], 1.0).then_inc(pool_step, 1)
                nc.gpsimd.memset(count[:], 0.0).then_inc(pool_step, 1)
                nc.gpsimd.memset(cw[:], 0.0).then_inc(pool_step, 1)
                nc.gpsimd.memset(vS[:], 1.0).then_inc(pool_step, 1)
                pool.wait_ge(pool_step, 5)
                norm_power(pool, 1)

            @block.vector
            def _(dve):
                dve.wait_ge(loaded, 16 * 8)
                st = Steps(dve, dve_step, 0)
                norm_stats(dve, st, 0)
                st.do(nc.vector.tensor_copy(id_bf[:], const[:, C_ID:C_ID + P]))
                st.do(nc.vector.tensor_copy(tri_bf[:], const[:, C_TRI:C_TRI + P]))
                st.do(nc.vector.tensor_scalar(mask_b[:], mask_i[:], 0.0, MASKED, ALU.is_equal, ALU.mult))
                st.do(nc.vector.tensor_scalar(mask_v[:], mask_i[:], 0.0, None, ALU.not_equal))
                st.settle()
                st.do(nc.vector.tensor_reduce(rowok[:], mask_v[:], AX.X, ALU.max))
                norm_apply(dve, 1, 0, first=True)
                st.settle()
                dve_base[0] = st.n

            @block.tensor
            def _(pe):
                pe.wait_ge(loaded, 16 * 8)
                norm_transpose(pe, 1, 7)

            @block.scalar
            def _(act):
                norm_store(act, 1, 7)

        def heads_phase(phase, tag, softmax, prefetch):
            q_mm, k_mm, v_mm = sem(f"{tag}_q_mm"), sem(f"{tag}_k_mm"), sem(f"{tag}_v_mm")
            q_done, k_done, v_done = sem(f"{tag}_q_done"), sem(f"{tag}_k_done"), sem(f"{tag}_v_done")
            ctx_ready = sem(f"{tag}_ctx")
            s_mm = sem(f"{tag}_s_mm")
            s_free = sem(f"{tag}_s_free")
            p_done = sem(f"{tag}_p_done")
            pt_mm = sem(f"{tag}_pt_mm")
            pt_act, pt_dve = sem(f"{tag}_pt_act"), sem(f"{tag}_pt_dve")
            o_mm = sem(f"{tag}_o_mm")
            o_used = sem(f"{tag}_o_used")
            ot_mm = sem(f"{tag}_ot_mm")
            ot_done = sem(f"{tag}_ot_done")
            out_mm = sem(f"{tag}_out_mm")
            x_added = sem(f"{tag}_x_added")
            wq, wk, wv, wo = (weight(c + ("3" if softmax else "0")) for c in "qkvo")
            W = HD + 1 if softmax else HD
            scale = float(HD) ** -0.5
            LN0 = NG * phase
            cen = aux[:, :, :].rearrange("p a b -> p (a b)")[:, 0:NH * KV].rearrange("p (h k) -> p h k", k=KV)
            prob = hid[:, :, :, :].rearrange("p s a b -> p s (a b)")[:, :, 0:NH * KV]\
                .rearrange("p s (h k) -> p s h k", k=KV)
            base = dve_base[0]
            per = [0]

            with nc.Block() as block:
                @block.sync
                def _(sp):
                    prefetch(sp)

                @block.gpsimd
                def _(pool):
                    with pool.Fori(0, NG) as g:
                        pool.wait_ge(v_mm, g + 1)
                        nc.gpsimd.tensor_copy(ctxg[:, :], ctxT[:, bass.ds(g * GK, GK)]).then_inc(ctx_ready, 1)
                        norm_power(pool, g + (LN0 + 2))

                @block.tensor
                def _(pe):
                    pe.sem_inc(v_mm, 1)
                    pe.sem_inc(o_mm, 2)
                    pe.sem_inc(ot_mm, 2)
                    pe.sem_inc(out_mm, 2)
                    if softmax:
                        pe.sem_inc(pt_mm, 8)

                    def scores(g, b):
                        for half in range(2):
                            pe.wait_ge(s_free, g * 8 + (2 * b + half + 1))
                            for q in (2 * half, 2 * half + 1):
                                rows = slice(32 * q, 32 * q + 32)
                                if softmax:
                                    nc.tensor.matmul(banks[:, q, 0:HQ * KV], qT[rows, b * P:(b + 1) * P],
                                                     kmask[rows, b, :, :].rearrange("p j k -> p (j k)"), start=True, stop=False)
                                    r = nc.tensor.matmul(banks[:, q, 0:HQ * KV], id_bf[:, :],
                                                         mask_b[:, :].unsqueeze(1).to_broadcast([P, HQ, KV]),
                                                         start=False, stop=True)
                                else:
                                    for j in range(HQ):
                                        r = nc.tensor.matmul(banks[0:KV, q, j * P:(j + 1) * P], kmask[rows, b, j, :],
                                                             qT[rows, b * P:(b + 1) * P], start=True, stop=True)
                            r.then_inc(s_mm, 1)

                    def turn_probs(g, b):
                        for quad in range(4):
                            if quad % 2 == 0:
                                pe.wait_ge(p_done, g * 8 + (2 * b + quad // 2 + 1))
                            pe.wait_ge((pt_act, pt_dve)[quad % 2], g * 8 + (2 * b + quad // 2 + 1))
                            for j in range(4):
                                r = nc.tensor.transpose(banks[0:KV, 4 + quad % 2, j * P:(j + 1) * P],
                                                        prob[:, b % 2, 4 * quad + j, :], ident)
                            r.then_inc(pt_mm, 1)

                    def values(g, b):
                        if softmax:
                            pe.wait_ge(pt_act, g * 8 + (2 * b + 3))
                            pe.wait_ge(pt_dve, g * 8 + (2 * b + 3))
                        else:
                            pe.wait_ge(s_free, g * 8 + (2 * b + 4))
                        pe.wait_ge(o_used, g * 4 + (b + 2))
                        for h in range(NH):
                            c = h * W
                            r = nc.tensor.matmul(banks[:, 6, c:c + W], pt[:, b % 2, h, :], vS[:, b, h, 0:W],
                                                 start=True, stop=True)
                        r.then_inc(o_mm, 1)

                    def turn_outputs(g, b):
                        pe.wait_ge(o_used, g * 4 + (b + 3))
                        pe.wait_ge(x_added, g * 4 + (b + 2))
                        nc.tensor.transpose(banks[:, 7, 0:P], oS[:, b % 2, :], ident).then_inc(ot_mm, 1)

                    def project(g, b):
                        pe.wait_ge(ot_done, g * 4 + (b + 3))
                        nc.tensor.matmul(banks[:, 7, P:2 * P], oT[:, b % 2, :], wo,
                                         start=True, stop=True).then_inc(out_mm, 1)

                    with pe.Fori(0, NG) as g:
                        pe.wait_ge(zT_ready, g + (LN0 + 1))
                        nc.tensor.matmul(banks[:, 6, :], wq, zT[:, :], start=True, stop=True).then_inc(q_mm, 1)
                        pe.wait_ge(ctx_ready, g + 1)
                        pe.wait_ge(x_added, g * 4 + 2)
                        nc.tensor.matmul(banks[:, 7, 0:GK], wk, ctxg[:, :], start=True, stop=True).then_inc(k_mm, 1)
                        pe.wait_ge(q_done, g + 1)
                        for b in range(TG):
                            r = nc.tensor.matmul(banks[0:KV, 6, b * P:(b + 1) * P], ctxg[:, b * KV:(b + 1) * KV], wv,
                                                 start=True, stop=True)
                        r.then_inc(v_mm, 1)
                        pe.wait_ge(k_done, g + 1)
                        scores(g, 0)
                        pe.wait_ge(v_done, g + 1)
                        for b in range(TG):
                            if b + 1 < TG:
                                scores(g, b + 1)
                            if softmax:
                                turn_probs(g, b)
                            if b >= 1:
                                turn_outputs(g, b - 1)
                            values(g, b)
                            if b >= 1:
                                project(g, b - 1)
                        turn_outputs(g, TG - 1)
                        project(g, TG - 1)
                        norm_transpose(pe, g + (LN0 + 2), 6)

                @block.scalar
                def _(act):
                    act.sem_inc(ot_done, 2)
                    if softmax:
                        act.sem_inc(pt_act, 1)
                    else:
                        act.sem_inc(s_free, 2)

                    def weigh(g, b):
                        for half in range(2):
                            if softmax:
                                act.wait_ge(s_free, g * 8 + (2 * b + half + 3))
                                if half == 0:
                                    act.wait_ge(pt_mm, g * 16 + (4 * b + 4))
                                nc.scalar.activation(prob[:, b % 2, 8 * half:8 * half + 8, :], cen[:, 8 * half:8 * half + 8, :],
                                                     ACT.Exp, scale=scale).then_inc(p_done, 1)
                            else:
                                act.wait_ge(s_mm, g * 8 + (2 * b + half + 1))
                                if half == 0:
                                    act.wait_ge(o_mm, g * 4 + (b + 1))
                                nc.scalar.activation(pt[:, b % 2, 8 * half:8 * half + 8, :].rearrange("p h k -> p (h k)"),
                                                     banks[0:KV, 2 * half:2 * half + 2, :].rearrange("p h k -> p (h k)"),
                                                     ACT.Sigmoid, scale=scale).then_inc(s_free, 1)

                    def probs_copy(g, b):
                        act.wait_ge(o_mm, g * 4 + (b + 1))
                        for quad in (0, 2):
                            act.wait_ge(pt_mm, g * 16 + (4 * b + quad + 9))
                            nc.scalar.copy(pt[:, b % 2, 4 * quad:4 * quad + 4, :].rearrange("p h k -> p (h k)"),
                                           banks[0:KV, 4, :]).then_inc(pt_act, 1)

                    def turned(g, b):
                        act.wait_ge(ot_mm, g * 4 + (b + 3))
                        act.wait_ge(out_mm, g * 4 + (b + 1))
                        nc.scalar.copy(oT[:, b % 2, :], banks[:, 7, 0:P]).then_inc(ot_done, 1)

                    with act.Fori(0, NG) as g:
                        act.wait_ge(q_mm, g + 1)
                        nc.scalar.activation(qT[:, :], banks[:, 6, :], ACT.Identity,
                                             bias=sm("bq3") if softmax else zero1).then_inc(q_done, 1)
                        weigh(g, 0)
                        for b in range(TG):
                            if b + 1 < TG:
                                weigh(g, b + 1)
                            if softmax:
                                probs_copy(g, b)
                            if b >= 1:
                                turned(g, b - 1)
                        turned(g, TG - 1)
                        norm_store(act, g + (LN0 + 2), 6)

                @block.vector
                def _(dve):
                    dve.sem_inc(o_used, 2)
                    dve.sem_inc(x_added, 2)
                    if softmax:
                        dve.sem_inc(pt_dve, 1)
                        dve.sem_inc(s_free, 2)

                    def centre(st, g, b):
                        for half in range(2):
                            s = banks[:, 2 * half:2 * half + 2, 0:HQ * KV].rearrange("p q (j k) -> p q j k", k=KV)
                            m = mx[:, 8 * half:8 * half + 8].rearrange("p (q j) -> p q j", j=HQ)
                            dve.wait_ge(s_mm, g * 8 + (2 * b + half + 1))
                            st.do(nc.vector.tensor_reduce(m, s, AX.X, ALU.max))
                            st.settle()
                            if not (b == 0):
                                dve.wait_ge(p_done, g * 8 + (2 * b + half - 1))
                            nc.vector.tensor_tensor(cen[:, 8 * half:8 * half + 8, :].rearrange("p (q j) k -> p q j k", j=HQ),
                                                    s, m.unsqueeze(3).to_broadcast([P, 2, HQ, KV]),
                                                    ALU.subtract).then_inc(s_free, 1)

                    def probs_copy(g, b):
                        dve.wait_ge(o_mm, g * 4 + (b + 1))
                        for quad in (1, 3):
                            dve.wait_ge(pt_mm, g * 16 + (4 * b + quad + 9))
                            nc.vector.tensor_copy(pt[:, b % 2, 4 * quad:4 * quad + 4, :].rearrange("p h k -> p (h k)"),
                                                  banks[0:KV, 5, :]).then_inc(pt_dve, 1)

                    def gather(st, g, b):
                        o = banks[:, 6, 0:NH * W].rearrange("p (h w) -> p h w", w=W)
                        dve.wait_ge(o_mm, g * 4 + (b + 3))
                        dve.wait_ge(ot_mm, g * 4 + (b + 1))
                        dst = oS[:, b % 2, :].rearrange("p (h w) -> p h w", w=HD)
                        if softmax:
                            st.do(nc.vector.reciprocal(rs[:, :], o[:, :, HD]))
                            st.settle()
                            st.do(nc.vector.tensor_scalar(rs[:, :], rs[:, :], rowok[:, 0:1], None, ALU.mult))
                            st.settle()
                            nc.vector.tensor_tensor(dst, o[:, :, 0:HD], rs[:, :].unsqueeze(2).to_broadcast([P, NH, HD]),
                                                    ALU.mult).then_inc(o_used, 1)
                        else:
                            nc.vector.tensor_copy(dst, o).then_inc(o_used, 1)

                    def add(st, g, b):
                        at = bass.ds(g * GT + b * P, P)
                        c = P
                        dve.wait_ge(out_mm, g * 4 + (b + 3))
                        if softmax:
                            st.do(nc.vector.tensor_tensor(tmp[:, :], banks[:, 7, c:c + P], sm("bo3"), ALU.add))
                            st.settle()
                            nc.vector.tensor_tensor(x[:, at], x[:, at], tmp[:, :], ALU.add).then_inc(x_added, 1)
                        else:
                            nc.vector.tensor_tensor(x[:, at], x[:, at], banks[:, 7, c:c + P], ALU.add).then_inc(x_added, 1)

                    PER = 28 if softmax else 8
                    with dve.Fori(0, NG) as g:
                        st = Steps(dve, dve_step, g * PER + base)
                        nxt = ((g + 1) % NG) * GT
                        dve.wait_ge(k_mm, g + 1)
                        for b in range(TG):
                            r = nc.vector.scalar_tensor_tensor(
                                out=kmask[:, b, :, :], in0=banks[:, 7, b * KV:(b + 1) * KV].unsqueeze(1).to_broadcast([P, HQ, KV]),
                                scalar=sm("bk3") if softmax else zero1,
                                in1=hm.unsqueeze(2).to_broadcast([P, HQ, KV]), op0=ALU.add, op1=ALU.mult)
                        r.then_inc(k_done, 1)
                        dve.wait_ge(v_mm, g + 2)
                        vin = banks[0:KV, 6, :].rearrange("p (b h w) -> p b h w", b=TG, w=HD)
                        vout = vS[:, :, :, 0:HD]
                        if softmax:
                            bv = sm("bv3")[0:KV, :].rearrange("p (h w) -> p h w", w=HD)
                            for b in range(TG):
                                r = nc.vector.tensor_tensor(vout[:, b], vin[:, b], bv, ALU.add)
                            r.then_inc(v_done, 1)
                            centre(st, g, 0)
                        else:
                            nc.vector.tensor_copy(vout, vin).then_inc(v_done, 1)
                        for b in range(TG):
                            if softmax:
                                if b + 1 < TG:
                                    centre(st, g, b + 1)
                                probs_copy(g, b)
                            gather(st, g, b)
                            if b >= 1:
                                add(st, g, b - 1)
                            if b == 1:
                                norm_stats(dve, st, nxt)
                            if b == 2:
                                norm_apply(dve, g + (LN0 + 2), nxt)
                        add(st, g, TG - 1)
                        per[0] = st.n
                        assert st.n == PER, st.n
            dve_base[0] = base + NG * per[0]

        def plain_phase(phase, tag, prefetch):
            e_mm, cen_done, p_done = sem(f"{tag}_e_mm"), sem(f"{tag}_cen"), sem(f"{tag}_p")
            pt_mm, pt_done, out_mm = sem(f"{tag}_pt_mm"), sem(f"{tag}_pt"), sem(f"{tag}_out_mm")
            x_added = sem(f"{tag}_x")
            LN0 = NG * phase
            base = dve_base[0]
            per = [0]
            cen = aux[:, 0, 0:GK].rearrange("p (b k) -> p b k", k=KV)
            prob = aux[:, 1, 0:GK].rearrange("p (b k) -> p b k", k=KV)
            pT = aux[0:KV, 2, :]

            with nc.Block() as block:
                @block.sync
                def _(sp):
                    prefetch(sp)

                @block.gpsimd
                def _(pool):
                    with pool.Fori(0, NG) as g:
                        norm_power(pool, g + (LN0 + 2))

                @block.tensor
                def _(pe):
                    with pe.Fori(0, NG) as g:
                        pe.wait_ge(zT_ready, g + (LN0 + 1))
                        for b in range(TG):
                            r = nc.tensor.matmul(banks[:, 0, b * KV:(b + 1) * KV], zT[:, b * P:(b + 1) * P],
                                                 ctxT[:, bass.ds(g * GK + b * KV, KV)], start=True, stop=True)
                        r.then_inc(e_mm, 1)
                        norm_transpose(pe, g + (LN0 + 2), 3)
                        pe.wait_ge(p_done, g + 1)
                        for b in range(TG):
                            r = nc.tensor.transpose(banks[0:KV, 1, b * P:(b + 1) * P], prob[:, b, :], ident)
                        r.then_inc(pt_mm, 1)
                        pe.wait_ge(pt_done, g + 1)
                        pe.wait_ge(x_added, g + 1)
                        for b in range(TG):
                            r = nc.tensor.matmul(banks[:, 2, b * P:(b + 1) * P], pT[:, b * P:(b + 1) * P],
                                                 ctxk[:, bass.ds(g * GT + b * D, D)], start=True, stop=True)
                        r.then_inc(out_mm, 1)

                @block.scalar
                def _(act):
                    with act.Fori(0, NG) as g:
                        act.wait_ge(cen_done, g + 1)
                        nc.scalar.activation(prob, cen, ACT.Exp).then_inc(p_done, 1)
                        act.wait_ge(pt_mm, g + 1)
                        nc.scalar.copy(pT, banks[0:KV, 1, :]).then_inc(pt_done, 1)
                        norm_store(act, g + (LN0 + 2), 3)

                @block.vector
                def _(dve):
                    dve.sem_inc(x_added, 1)
                    PER = 11
                    with dve.Fori(0, NG) as g:
                        st = Steps(dve, dve_step, g * PER + base)
                        nxt = ((g + 1) % NG) * GT
                        s = banks[:, 0, 0:GK].rearrange("p (b k) -> p b k", k=KV)
                        dve.wait_ge(e_mm, g + 1)
                        st.do(nc.vector.tensor_reduce(mx[:, 0:TG], s, AX.X, ALU.max))
                        st.settle()
                        nc.vector.tensor_tensor(cen, s, mx[:, 0:TG].unsqueeze(2).to_broadcast([P, TG, KV]),
                                                ALU.subtract).then_inc(cen_done, 1)
                        norm_stats(dve, st, nxt)
                        norm_apply(dve, g + (LN0 + 2), nxt)
                        dve.wait_ge(p_done, g + 1)
                        st.do(nc.vector.tensor_reduce(den[:, :], prob, AX.X, ALU.add))
                        st.settle()
                        st.do(nc.vector.reciprocal(rden[:, :], den[:, :]))
                        st.settle()
                        dve.wait_ge(out_mm, g + 1)
                        for b in range(TG):
                            at = bass.ds(g * GT + b * P, P)
                            r = nc.vector.scalar_tensor_tensor(out=x[:, at], in0=banks[:, 2, b * P:(b + 1) * P],
                                                               scalar=rden[:, b:b + 1], in1=x[:, at],
                                                               op0=ALU.mult, op1=ALU.add)
                        r.then_inc(x_added, 1)
                        per[0] = st.n
                        assert st.n == PER, st.n
            dve_base[0] = base + NG * per[0]

        def gelu_phase(phase, tag, prefetch):
            ctx_ready, h_mm, g_done = sem(f"{tag}_ctx"), sem(f"{tag}_h_mm"), sem(f"{tag}_g")
            out_mm, x_added = sem(f"{tag}_out_mm"), sem(f"{tag}_x")
            LN0 = NG * phase
            base = dve_base[0]
            per = [0]
            gT = aux[0:KV, 0, :]

            with nc.Block() as block:
                @block.sync
                def _(sp):
                    prefetch(sp)

                @block.gpsimd
                def _(pool):
                    with pool.Fori(0, NG) as g:
                        pool.wait_ge(h_mm, g + 1)
                        nc.gpsimd.tensor_copy(ctxg[:, :], ctxT[:, bass.ds(g * GK, GK)]).then_inc(ctx_ready, 1)
                        norm_power(pool, g + (LN0 + 2))

                @block.tensor
                def _(pe):
                    pe.sem_inc(h_mm, 1)
                    with pe.Fori(0, NG) as g:
                        pe.wait_ge(zT_ready, g + (LN0 + 1))
                        pe.wait_ge(ctx_ready, g + 1)
                        for b in range(TG):
                            r = nc.tensor.matmul(banks[0:KV, 0, b * P:(b + 1) * P], ctxg[:, b * KV:(b + 1) * KV],
                                                 zT[:, b * P:(b + 1) * P], start=True, stop=True)
                        r.then_inc(h_mm, 1)
                        norm_transpose(pe, g + (LN0 + 2), 3)
                        pe.wait_ge(g_done, g + 1)
                        pe.wait_ge(x_added, g + 1)
                        for b in range(TG):
                            r = nc.tensor.matmul(banks[:, 2, b * P:(b + 1) * P], gT[:, b * P:(b + 1) * P],
                                                 ctxk[:, bass.ds(g * GT + b * D, D)], start=True, stop=True)
                        r.then_inc(out_mm, 1)

                @block.scalar
                def _(act):
                    with act.Fori(0, NG) as g:
                        act.wait_ge(h_mm, g + 2)
                        nc.scalar.activation(gT, banks[0:KV, 0, :], ACT.Gelu_apprx_tanh).then_inc(g_done, 1)
                        norm_store(act, g + (LN0 + 2), 3)

                @block.vector
                def _(dve):
                    dve.sem_inc(x_added, 1)
                    PER = 8
                    with dve.Fori(0, NG) as g:
                        st = Steps(dve, dve_step, g * PER + base)
                        nxt = ((g + 1) % NG) * GT
                        norm_stats(dve, st, nxt)
                        norm_apply(dve, g + (LN0 + 2), nxt)
                        dve.wait_ge(out_mm, g + 1)
                        at = bass.ds(g * GT, GT)
                        nc.vector.tensor_tensor(x[:, at], x[:, at], banks[:, 2, :], ALU.add).then_inc(x_added, 1)
                        per[0] = st.n
                        assert st.n == PER, st.n
            dve_base[0] = base + NG * per[0]

        def moe_phase(phase, tag, kind, wbuf, w_sem, act_fn, topk, cap, renorm, store=False):
            plan = moe_plan(kind)
            f, chunks, EX, plain, glu = plan["f"], plan["chunks"], plan["experts"], plan["plain"], plan["glu"]
            NB, SL = plan["banks"], plan["slots"]
            C = len(chunks)
            UPW = 2 * f if glu else f
            up = wbuf[:, 0:EX * UPW].rearrange("p (e f) -> p e f", f=UPW)
            down = wbuf[:, EX * UPW:EX * (UPW + C * D)].rearrange("p (e c d) -> p e c d", c=C, d=D)
            NC = EX * C
            NU = NC * 2 if glu else NC
            CR = 4
            Y0, RT, TP = 4, 6, 7
            if NB == 3:
                assert NU % 3 == 0 and NC % SL == 0
            l_mm = sem(f"{tag}_l_mm")
            sub_done = sem(f"{tag}_sub")
            e_done = sem(f"{tag}_exp")
            oh_done = sem(f"{tag}_oh")
            r_mm = sem(f"{tag}_r_mm")
            cw_done = sem(f"{tag}_cw")
            ct_mm, ct_done, b_mm = sem(f"{tag}_ct_mm"), sem(f"{tag}_ct"), sem(f"{tag}_b_mm")
            b_used = sem(f"{tag}_b_used")
            h_mm = sem(f"{tag}_h_mm")
            a_done = sem(f"{tag}_a_done")
            m_done = sem(f"{tag}_m_done")
            y_mm = sem(f"{tag}_y_mm")
            y_used = sem(f"{tag}_y_used")
            hid_done = m_done if glu else a_done
            LN0 = NG * phase
            base = dve_base[0]
            per = [0]
            odd = EX % 2

            with nc.Block() as block:
                @block.sync
                def _(sp):
                    if store:
                        with sp.Fori(0, NG) as g:
                            sp.wait_ge(y_used, (g + 1) * EX + 2)
                            sp.dma_start(out[:, bass.ds(g * GT, GT)], x[:, bass.ds(g * GT, GT)]).then_inc(stored, 16)
                        sp.wait_ge(stored, 16 * NG)

                @block.gpsimd
                def _(pool):
                    with pool.Fori(0, NG) as g:
                        norm_power(pool, g + (LN0 + 2))

                @block.tensor
                def _(pe):
                    pe.sem_inc(y_mm, 2)
                    pe.wait_ge(w_sem, 16)

                    def bank_free(g, n):
                        q = n - NB
                        if not glu:
                            pe.wait_ge(a_done, g * NC + (q + 1 + CR))
                        elif q % 2 == 0:
                            pe.wait_ge(a_done, g * NC + (q // 2 + 1 + CR))
                        else:
                            pe.wait_ge(m_done, g * NC + (q // 2 + 1 + CR))

                    def rise(g, e):
                        n = e * C * (2 if glu else 1)
                        for c, (at, w) in enumerate(chunks):
                            for part in range(2 if glu else 1):
                                bank_free(g, n)
                                nc.tensor.matmul(banks[0:w, n % NB, :], up[:, e, part * f + at:part * f + at + w], zT[:, :],
                                                 start=True, stop=True).then_inc(h_mm, 1)
                                n += 1

                    def fall(g, e):
                        pe.wait_ge(hid_done, g * NC + ((e + 1) * C + CR))
                        pe.wait_ge(y_used, g * EX + (e + 1 + (odd if e == 0 else 0)))
                        for i in range(TG):
                            for c, (_, w) in enumerate(chunks):
                                r = nc.tensor.matmul(banks[:, Y0 + e % 2, i * D:(i + 1) * D],
                                                     hid[0:w, e % 2, c, i * P:(i + 1) * P], down[0:w, e, c, :],
                                                     start=(c == 0), stop=(c == C - 1))
                        r.then_inc(y_mm, 1)

                    with pe.Fori(0, NG) as g:
                        pe.wait_ge(zT_ready, g + (LN0 + 1))
                        if True:
                            for i in range(TG):
                                r = nc.tensor.matmul(banks[:, RT, i * NE:(i + 1) * NE], zT[:, i * P:(i + 1) * P],
                                                     sm("rw" + kind[1]), start=True, stop=True)
                            r.then_inc(l_mm, 1)
                        rise(g, 0)
                        if cap:
                            pe.wait_ge(oh_done, g + 1)
                            nk = topk * NE
                            R = banks[:, RT, 64:64 + TG * nk].rearrange("p (i n) -> p i n", n=nk)
                            T = banks[:, RT, 160:160 + nk]
                            nc.tensor.matmul(R, tri_bf[:, :], oh[:, :, 0:topk, :], start=True, stop=False)
                            for i in range(TG - 1):
                                nc.tensor.matmul(R[:, i + 1:TG, :], one_bf[:, :],
                                                 oh[:, i:i + 1, 0:topk, :].rearrange("p i k n -> p i (k n)")
                                                 .to_broadcast([P, TG - 1 - i, nk]),
                                                 start=False, stop=(i == TG - 2))
                            for i in range(TG):
                                r = nc.tensor.matmul(T, one_bf[:, :], oh[:, i, 0:topk, :].rearrange("p k n -> p (k n)"),
                                                     start=(i == 0), stop=(i == TG - 1))
                            r.then_inc(r_mm, 1)
                        for e in range(EX):
                            if e + 1 < EX:
                                rise(g, e + 1)
                            if e == 0 and kind == "l3":
                                pe.wait_ge(cw_done, g + 1)
                                nc.tensor.transpose(banks[:, RT, 256:384], cw[:, :, :].rearrange("p i n -> p (i n)"),
                                                    ident).then_inc(ct_mm, 1)
                                pe.wait_ge(ct_done, g + 1)
                                nc.tensor.matmul(banks[:, TP, :], cwT[:, :], sm("b2"), start=True,
                                                 stop=True).then_inc(b_mm, 1)
                            if e == EX - 2:
                                if kind == "l3":
                                    pe.wait_ge(b_used, g + 1)
                                norm_transpose(pe, g + (LN0 + 2), TP)
                            fall(g, e)

                @block.scalar
                def _(act):
                    act.sem_inc(a_done, CR)
                    with act.Fori(0, NG) as g:
                        act.wait_ge(sub_done, g + 1)
                        nc.scalar.activation(el[:, :, :], ls[:, :, :], ACT.Exp).then_inc(e_done, 1)
                        for e in range(EX):
                            for c, (_, w) in enumerate(chunks):
                                n = e * C + c
                                if glu:
                                    act.wait_ge(h_mm, g * NU + (2 * n + 1))
                                    act.wait_ge(m_done, g * NC + (n - SL + 1 + CR))
                                    nc.scalar.activation(aux[0:w, n % SL, :], banks[0:w, (2 * n) % NB, :],
                                                         act_fn).then_inc(a_done, 1)
                                else:
                                    act.wait_ge(h_mm, g * NU + (n + 1))
                                    if c == 0:
                                        act.wait_ge(y_mm, g * EX + (e + 1 + (odd if e == 0 else 0)))
                                    bias = sm("b1")[:, e * C + c:e * C + c + 1] if kind == "l3" else zero1
                                    nc.scalar.activation(hid[0:w, e % 2, c, :], banks[0:w, n % NB, :], act_fn,
                                                         bias=bias).then_inc(a_done, 1)
                            if e == 1 and kind == "l3":
                                act.wait_ge(ct_mm, g + 1)
                                nc.scalar.copy(cwT[:, :], banks[:, RT, 256:384]).then_inc(ct_done, 1)
                        norm_store(act, g + (LN0 + 2), TP)

                @block.vector
                def _(dve):
                    dve.sem_inc(y_used, 2)
                    if glu:
                        dve.sem_inc(m_done, CR)

                    def gate(g, e):
                        dve.wait_ge(y_mm, g * EX + (e + 1 + (odd if e == 0 else 0)))
                        for c, (_, w) in enumerate(chunks):
                            n = e * C + c
                            dve.wait_ge(a_done, g * NC + (n + 1 + CR))
                            dve.wait_ge(h_mm, g * NU + (2 * n + 2))
                            nc.vector.tensor_tensor(hid[0:w, e % 2, c, :], aux[0:w, n % SL, :],
                                                    banks[0:w, (2 * n + 1) % NB, :], ALU.mult).then_inc(m_done, 1)

                    def route_first(st, g):
                        dve.wait_ge(l_mm, g + 1)
                        L = banks[:, RT, 0:TG * NE].rearrange("p (i n) -> p i n", n=NE)
                        if kind == "l2":
                            st.do(nc.vector.tensor_tensor(lg[:, :, :], L, sm("ebias2").unsqueeze(1).to_broadcast([P, TG, NE]), ALU.add))
                        else:
                            st.do(nc.vector.tensor_copy(lg[:, :, :], L))
                        st.settle(apart=True)
                        for i in range(TG):
                            st.do(nc.vector.max(mx8[:, i, :], lg[:, i, :]))
                        st.settle()
                        nc.vector.tensor_tensor(ls[:, :, :], lg[:, :, :], mx8[:, :, 0:1].to_broadcast([P, TG, NE]),
                                                ALU.subtract).then_inc(sub_done, 1)
                        for i in range(TG):
                            st.do(nc.vector.max_index(ix8[:, i, :], mx8[:, i, :], lg[:, i, :]))
                        st.settle()
                        st.do(nc.vector.tensor_copy(ixf[:, :, :], ix8[:, :, 0:2]))
                        st.settle()
                        for k in range(topk):
                            r = nc.vector.tensor_tensor(oh[:, :, k, :], iota8.unsqueeze(1).to_broadcast([P, TG, NE]),
                                                        ixf[:, :, k:k + 1].to_broadcast([P, TG, NE]), ALU.is_equal)
                        r.then_inc(oh_done, 1)

                    def route_last(st, g):
                        nk = topk * NE
                        if cap:
                            R = banks[:, RT, 64:64 + TG * nk].rearrange("p (i n) -> p i n", n=nk)
                            dve.wait_ge(r_mm, g + 1)
                            st.do(nc.vector.tensor_tensor(rank[:, :, 0:nk], R, count[:, 0:nk].unsqueeze(1).to_broadcast([P, TG, nk]), ALU.add))
                            st.settle()
                            for k in range(topk):
                                st.do(nc.vector.scalar_tensor_tensor(out=ohv[:, :, k, :], in0=rank[:, :, k * NE:(k + 1) * NE],
                                                                     scalar=float(cap), in1=oh[:, :, k, :],
                                                                     op0=ALU.is_le, op1=ALU.mult))
                            st.do(nc.vector.tensor_tensor(count[:, 0:nk], count[:, 0:nk], banks[:, RT, 160:160 + nk], ALU.add))
                            st.settle()
                            picks = ohv
                        else:
                            dve.wait_ge(oh_done, g + 1)
                            picks = oh
                        if topk == 2:
                            st.do(nc.vector.tensor_tensor(sel[:, :, :], picks[:, :, 0, :], picks[:, :, 1, :], ALU.add))
                            st.settle()
                            chosen = sel[:, :, :]
                        else:
                            chosen = picks[:, :, 0, :]
                        dve.wait_ge(e_done, g + 1)
                        st.do(nc.vector.tensor_tensor(sel[:, :, :], chosen, el[:, :, :], ALU.mult))
                        st.settle()
                        st.do(nc.vector.tensor_reduce(den[:, :], sel[:, :, :] if renorm else el[:, :, :], AX.X, ALU.add))
                        st.settle()
                        st.do(nc.vector.reciprocal(rden[:, :], den[:, :]))
                        st.settle()
                        nc.vector.tensor_tensor(cw[:, :, 0:NE], sel[:, :, :], rden[:, :].unsqueeze(2).to_broadcast([P, TG, NE]),
                                                ALU.mult).then_inc(cw_done, 1)

                    def combine(g, e):
                        dve.wait_ge(y_mm, g * EX + (e + 3))
                        if e == plain:
                            dve.wait_ge(cw_done, g + 1)
                        dve.wait_ge(y_used, g * EX + (e + 2))
                        if e < plain:
                            at = bass.ds(g * GT, GT)
                            r = nc.vector.tensor_tensor(x[:, at], x[:, at], banks[:, Y0 + e % 2, :], ALU.add)
                        else:
                            for i in range(TG):
                                at = bass.ds(g * GT + i * P, P)
                                r = nc.vector.scalar_tensor_tensor(out=x[:, at], in0=banks[:, Y0 + e % 2, i * D:(i + 1) * D],
                                                                   scalar=cw[:, i, e - plain:e - plain + 1], in1=x[:, at],
                                                                   op0=ALU.mult, op1=ALU.add)
                        r.then_inc(y_used, 1)

                    PER = {"l0": 27, "l1": 22, "l2": 22, "l3": 25}[kind]
                    with dve.Fori(0, NG) as g:
                        st = Steps(dve, dve_step, g * PER + base)
                        nxt = ((g + 1) % NG) * GT
                        if glu:
                            pass
                        route_first(st, g)
                        if glu:
                            gate(g, 0)
                        route_last(st, g)
                        if kind == "l0":
                            at = bass.ds(g * GT, GT)
                            xv = x[:, at].rearrange("p (i d) -> p i d", d=D)
                            st.do(nc.vector.tensor_tensor(xv, xv, sm("bias0").unsqueeze(1).to_broadcast([P, TG, D]), ALU.add))
                            st.settle()
                        for e in range(EX):
                            if glu and e + 1 < EX:
                                gate(g, e + 1)
                            combine(g, e)
                            if e == 1 and kind == "l3":
                                at = bass.ds(g * GT, GT)
                                dve.wait_ge(b_mm, g + 1)
                                dve.wait_ge(y_used, g * EX + (e + 3))
                                st.do(nc.vector.tensor_tensor(x[:, at], x[:, at], banks[:, TP, :], ALU.add))
                                st.settle()
                                dve.sem_inc(b_used, 1)
                            if e == 2:
                                norm_stats(dve, st, nxt)
                            if e == 3:
                                norm_apply(dve, g + (LN0 + 2), nxt)
                        per[0] = st.n
                        assert st.n == PER, (kind, st.n)
            dve_base[0] = base + NG * per[0]

        def nothing(sp):
            pass

        def load_layer2(sp):
            sp.dma_start(w_even[:, 0:ins["w2"].shape[1]], ins["w2"]).then_inc(w_loaded[2], 16)

        def load_layer3(sp):
            sp.dma_start(w_odd[:, 0:ins["w3"].shape[1]], ins["w3"]).then_inc(w_loaded[3], 16)

        def clear_count():
            with nc.Block() as block:
                @block.gpsimd
                def _(pool):
                    nc.gpsimd.memset(count[:], 0.0).then_inc(pool_step, 1)
                    pool.wait_ge(pool_step, 6)

        heads_phase(0, "a0", False, nothing)
        moe_phase(1, "f0", "l0", w_even, w_loaded[0], ACT.Gelu_apprx_tanh, 2, CAP0, False)
        plain_phase(2, "a1", load_layer2)
        moe_phase(3, "f1", "l1", w_odd, w_loaded[1], ACT.Silu, 2, 0, True)
        gelu_phase(4, "a2", load_layer3)
        moe_phase(5, "f2", "l2", w_even, w_loaded[2], ACT.Silu, 2, 0, True)
        clear_count()
        heads_phase(6, "a3", True, nothing)
        moe_phase(7, "f3", "l3", w_odd, w_loaded[3], ACT.Gelu, 1, CAP3, False, store=True)


def lay_out(inputs):
    import numpy as np

    def f32(name):
        return np.ascontiguousarray(inputs[name])

    a = {}
    xs, cs = f32("x"), f32("ctx_1024")
    a["x"] = xs.transpose(1, 0, 2).reshape(P, B * D)
    a["ctxT"] = cs.transpose(2, 0, 1).reshape(D, B * KV)
    a["ctxk"] = cs.transpose(1, 0, 2).reshape(KV, B * D)
    a["mask"] = f32("mask_1x1xSxS2_ik0").reshape(P, KV)
    const = np.zeros((P, C_N), np.float32)
    const[:, C_ID:C_ID + P] = np.eye(P)
    const[:, C_TRI:C_TRI + P] = np.triu(np.ones((P, P)))
    const[:, C_HM:C_HM + HQ] = (np.arange(P)[:, None] % 32 // HD == np.arange(HQ)[None])
    const[:, C_IOTA:C_IOTA + NE] = np.arange(NE)
    const[:, C_ONE] = 1.0
    a["const"] = const
    small = np.zeros((P, SMALL_N), np.float32)

    def put(name, v):
        o, w = SMALL[name]
        small[0:v.shape[0], o:o + w] = v
    put("bq3", f32("L3_xattn_bq")[:, None])
    put("bk3", f32("L3_xattn_bk")[:, None])
    put("bv3", np.broadcast_to(f32("L3_xattn_bv")[None], (P, D)))
    put("bo3", np.broadcast_to(f32("L3_xattn_bo")[None], (P, D)))
    put("bias0", np.broadcast_to(f32("L0_ffn_bias").reshape(1, D), (P, D)))
    put("ebias2", np.broadcast_to(f32("L2_ffn_expert_bias")[None], (P, NE)))
    put("rw0", f32("L0_ffn_router_w"))
    put("rw1", f32("L1_ffn_gate_w"))
    put("rw2", f32("L2_ffn_router_w").T)
    put("rw3", f32("L3_ffn_wg"))
    put("b1", f32("L3_ffn_b1").reshape(NE * 4, P).T)
    b2 = np.zeros((P, TG * D), np.float32)
    for i in range(TG):
        b2[32 * i:32 * i + NE, i * D:(i + 1) * D] = f32("L3_ffn_b2")
    put("b2", b2)
    a["small"] = small
    a["aw"] = np.concatenate([f32(f"L{n[1]}_xattn_W{n[0]}").T for n in AW], axis=1)

    def packed(up, down):
        e, h = down.shape[0], down.shape[1]
        c = -(-h // P)
        dn = np.zeros((e, c * P, D), np.float32)
        dn[:, :h] = down
        return np.concatenate([up.transpose(1, 0, 2).reshape(D, -1),
                               dn.reshape(e, c, P, D).transpose(2, 0, 1, 3).reshape(P, -1)], axis=1)

    a["w0"] = packed(f32("L0_ffn_w1"), f32("L0_ffn_w2"))
    a["w1"] = packed(np.concatenate([f32("L1_ffn_base_wgu")[None], f32("L1_ffn_exp_wgu")]),
                     np.concatenate([f32("L1_ffn_base_wd")[None], f32("L1_ffn_exp_wd")]))
    up = [np.concatenate([f32("L2_ffn_s" + w if s else "L2_ffn_" + w).transpose(0, 2, 1) for w in ("w1", "w3")], axis=2)
          for s in (True, False)]
    dn = [f32(n).transpose(0, 2, 1) for n in ("L2_ffn_sw2", "L2_ffn_w2")]
    a["w2"] = packed(np.concatenate(up), np.concatenate(dn))
    a["w3"] = packed(f32("L3_ffn_W1"), f32("L3_ffn_W2"))
    return {k: np.ascontiguousarray(v) for k, v in a.items()}


def kernel(**inputs):
    import concourse.bacc as _bacc
    from concourse.bass_utils import run_bass_kernel_spmd as _run

    arrays = lay_out(inputs)
    nc = _bacc.Bacc("TRN2", target_bir_lowering=False, num_devices=1)
    ins = {k: nc.dram_tensor(f"in_{k}", v.shape, mybir.dt.from_np(v.dtype), kind="ExternalInput").ap()
           for k, v in arrays.items()}
    out = nc.dram_tensor("out_0", (P, B * D), F32, kind="ExternalOutput").ap()
    build(nc, ins, out)
    r = _run(nc, [{f"in_{k}": v for k, v in arrays.items()}], core_ids=[0])
    return r.results[0]["out_0"].reshape(P, B, D).transpose(1, 0, 2)
```

```python
from contextlib import ExitStack

import concourse.bass as bass
from concourse import mybir

F32 = mybir.dt.float32
F32R = mybir.dt.float32r
BF16 = mybir.dt.bfloat16
I32 = mybir.dt.int32
U32 = mybir.dt.uint32
ALU = mybir.AluOpType
ACT = mybir.ActivationFunctionType
AX = mybir.AxisListType

P = 128
B, D, KV = 32, 128, 77
KE = 78
TG = 4
NG = B // TG
GT = TG * P
GK = TG * KV
NH, HD = 16, 8
HQ = 32 // HD
NE = 8
EPS = 1e-5
MASKED = -1e30
CAP0 = B * P // NE
CAP3 = int(B * P / NE * 1.25) + 1

C_ID, C_TRI, C_IOTA, C_ZERO, C_STEP, C_BLK, C_TRASH = 0, 128, 256, 264, 265, 281, 321
C_N = C_TRASH + 2 * B

BLK = 256
NBLK = 2 * B * P // BLK + NE
WS = 4
R_ALL = B * P + BLK
R_CAP3 = -(-CAP3 // BLK) * BLK
X_ROWS = NE * R_ALL
Y_ROWS = NBLK * BLK
TRASH = Y_ROWS - P
assert 2 * NE * CAP0 <= TRASH and NE * R_CAP3 <= TRASH and Y_ROWS + 2 * B * P <= X_ROWS
SMALL = {}
_at = 0
for _n, _w in (("bq3", 1), ("bk3", 1), ("bv3", D), ("bo3", D), ("bias0", D), ("ebias2", NE),
               ("rw0", NE), ("rw1", NE), ("rw2", NE), ("rw3", NE)):
    SMALL[_n] = (_at, _w)
    _at += _w
SMALL_N = _at
AW = ("q0", "k0", "v0", "o0", "q3", "k3", "v3", "o3")


STEPS = {"a0": 8, "r0": 36, "a1": 17, "r1": 33, "a2": 13, "r2": 33, "a3": 33, "r3": 34, "end": 1}


class Steps:

    def __init__(self, eng, sem, base):
        self.eng, self.sem, self.base, self.n = eng, sem, base, 0

    def do(self, ins):
        ins.then_inc(self.sem, 1)
        self.n += 1

    def settle(self, apart=False):
        self.eng.wait_ge(self.sem, self.base + self.n)
        if apart:
            self.eng.nop(nofuse=True)


class Mixture:

    def __init__(self, layer, hidden, glu, plain, topk, cap, region, rows, blocks, renorm, act_fn):
        self.layer, self.hidden, self.glu, self.plain = layer, hidden, glu, plain
        self.topk, self.cap, self.region, self.rows, self.blocks = topk, cap, region, rows, blocks
        self.renorm, self.act_fn = renorm, act_fn
        self.chunks = [(at, min(P, hidden - at)) for at in range(0, hidden, P)]
        self.C = len(self.chunks)
        self.up = hidden * (2 if glu else 1)
        self.down = self.C * D
        self.parts = 2 if glu else 1
        self.U = self.C * self.parts
        self.banks = 3 if self.U % 4 else 4
        self.bias = layer == 3
        self.width = self.up + self.down + (self.C + D if self.bias else 0)


MIX = (Mixture(0, 512, False, 0, 2, CAP0, 2 * CAP0, 2 * BLK, 2 * NE * CAP0 // (2 * BLK), False, ACT.Gelu_apprx_tanh),
       Mixture(1, 352, True, 1, 2, 0, R_ALL, BLK, NBLK, True, ACT.Silu),
       Mixture(2, 256, True, 2, 2, 0, R_ALL, BLK, NBLK, True, ACT.Silu),
       Mixture(3, 512, False, 0, 1, CAP3, R_CAP3, BLK, NE * R_CAP3 // BLK, False, ACT.Gelu))
W_MAX = max(m.width for m in MIX)
PLAIN = [m.plain * (m.up + m.down) for m in MIX]


def build(nc, ins, out):
    ctx = ExitStack()
    with ctx:
        def sb(name, shape, dt=F32):
            return ctx.enter_context(nc.sbuf_tensor(name, shape, dt))

        def sem(name):
            return ctx.enter_context(nc.semaphore(name))

        def signal(name):
            return nc.alloc_semaphore(name)

        x = sb("x", [P, B * D])
        ctxT = sb("ctxT", [P, B * KV])
        ctxk = sb("ctxk", [KV, B * D])
        const = sb("const", [P, C_N])
        small = sb("small", [P, SMALL_N])
        aw = sb("aw", [P, len(AW) * D])
        w_plain = sb("w_plain", [P, sum(PLAIN)])
        w_exp = sb("w_exp", [P, WS, W_MAX])
        z = sb("z", [P, GT])
        z_out = sb("z_out", [P, GT])
        xin = sb("xin", [P, WS, 2 * BLK])
        xT = sb("xT", [P, 2, 2 * BLK])
        y_out = sb("y_out", [P, 2, 2 * BLK])
        y_in = sb("y_in", [P, 2 * TG, D])
        zT = sb("zT", [P, GT])
        bn = sb("bn", [P, TG, 6])
        mv = sb("mv", [P, TG, 2])
        ve = sb("ve", [P, TG])
        rstd = sb("rstd", [P, TG])
        mhalf = sb("mhalf", [P, TG])
        id_bf = sb("id_bf", [P, P], BF16)
        tri_bf = sb("tri_bf", [P, P], BF16)
        one_bf = sb("one_bf", [P, P], BF16)
        mask_i = sb("mask_i", [P, KV], I32)
        mask_b = sb("mask_b", [P, KE], BF16)
        mask_v = sb("mask_v", [P, KV])
        rowok = sb("rowok", [P, 1])
        hid = sb("hid", [P, 2, 4, GT])
        aux = sb("aux", [P, 4, GT])
        spread = sb("spread", [P, 2, 2, HQ, P], F32R)
        q_hi, q_lo = sb("q_hi", [P, GT], F32R), sb("q_lo", [P, GT], F32R)
        k_hi, k_lo = sb("k_hi", [P, GK], F32R), sb("k_lo", [P, GK], F32R)
        qR = sb("qR", [P, HQ, GT], F32R)
        kR = sb("kR", [P, HQ, TG, KE], F32R)
        vS = sb("vS", [KV, TG, HQ, HQ, 32])
        ctxg = sb("ctxg", [P, GK])
        oS = sb("oS", [P, 2, D])
        oW = hid[:, 0, 3, :]
        oT = sb("oT", [P, 2, D])
        mx = sb("mx", [P, NH])
        rs = sb("rs", [P, NH])
        tmp = sb("tmp", [P, D])
        pt = sb("pt", [KV, 2, NH, P])
        lg = sb("lg", [P, TG, NE])
        ls = sb("ls", [P, TG, NE])
        el = sb("el", [P, TG, NE])
        mx8 = sb("mx8", [P, TG, 8])
        ix8 = sb("ix8", [P, TG, 8], U32)
        ixf = sb("ixf", [P, TG, 2])
        oh = sb("oh", [P, TG, 2, NE], BF16)
        ohc = sb("ohc", [P, TG, NE], BF16)
        rank = sb("rank", [P, TG, 2 * NE])
        picked = sb("picked", [P, TG, 2, NE])
        rk = sb("rk", [P, TG, 2])
        row = sb("row", [P, TG, 2])
        within = sb("within", [P, TG, 2])
        wt = sb("wt", [P, TG, 2])
        count = sb("count", [P, 2 * NE])
        den = sb("den", [P, TG])
        rden = sb("rden", [P, TG])
        idx_out = sb("idx_out", [P, 2 * TG], U32)
        idx_in = sb("idx_in", [P, 2 * TG], U32)
        wt_in = sb("wt_in", [P, 2 * TG])
        idx_all = sb("idx_all", [P, 2 * B], U32)
        wt_all = sb("wt_all", [P, 2 * B])
        rk_all = sb("rk_all", [P, 2 * B])
        ix_all = sb("ix_all", [P, 2 * B])
        pos = sb("pos", [P, 2 * B])
        ok_all = sb("ok_all", [P, 2 * B])
        nblk = sb("nblk", [P, 3, NE])
        first = sb("first", [P, NE])
        tab = sb("tab", [1, 3, NBLK])
        tab_e = sb("tab_e", [1, NBLK], I32)
        tab_r = sb("tab_r", [1, NBLK], I32)
        x_rows = nc.dram_tensor("x_rows", (X_ROWS, D), F32, kind="Internal").ap()
        y_rows = nc.dram_tensor("y_rows", (Y_ROWS, D), F32, kind="Internal").ap()
        banks = ctx.enter_context(nc.psum_tensor("banks", [P, 8, 512], F32))

        ident = const[:, C_ID:C_ID + P]
        iota8 = const[:, C_IOTA:C_IOTA + NE]
        zero1 = const[:, C_ZERO:C_ZERO + 1]

        def sm(name):
            a, w = SMALL[name]
            return small[:, a:a + w]

        def weight(name):
            i = AW.index(name)
            return aw[:, i * D:(i + 1) * D]

        loaded = sem("loaded")
        zeros_ready = sem("zeros_ready")
        cleared = sem("cleared")
        var_ready = sem("var_ready")
        rstd_ready = sem("rstd_ready")
        z_ready = sem("z_ready")
        zt_ready = sem("zt_ready")
        zT_ready = sem("zT_ready")
        dve_step = sem("dve_step")
        pool_step = sem("pool_step")
        stored = sem("stored")

        def psum_copy_of(bank):
            return banks[:, bank, :]

        def norm_stats(dve, st, at):
            dve.nop(nofuse=True)
            for i in range(TG):
                st.do(nc.vector.bn_stats(bn[:, i, :], x[:, bass.ds(at + i * D, D)]))
            st.settle(apart=True)
            for i in range(TG):
                st.do(nc.vector.bn_aggr(mv[:, i, :], bn[:, i, :]))
            st.settle()
            nc.vector.tensor_scalar(ve[:, :], mv[:, :, 1], EPS, None, ALU.add).then_inc(var_ready, 1)

        def norm_apply(dve, n, at, first=False):
            dve.wait_ge(rstd_ready, n)
            if not first:
                dve.wait_ge(zt_ready, n - 1)
            for i in range(TG):
                r = nc.vector.tensor_scalar(z[:, i * D:(i + 1) * D], x[:, bass.ds(at + i * D, D)],
                                            mv[:, i, 0:1], rstd[:, i:i + 1], ALU.subtract, ALU.mult)
            r.then_inc(z_ready, 1)

        def norm_power(pool, n):
            pool.wait_ge(var_ready, n)
            nc.gpsimd.tensor_tensor(rstd[:, :], ve[:, :], mhalf[:, :], ALU.pow).then_inc(rstd_ready, 1)

        def norm_transpose(pe, n, bank):
            pe.wait_ge(z_ready, n)
            for i in range(TG):
                r = nc.tensor.transpose(banks[:, bank, i * P:(i + 1) * P], z[:, i * D:(i + 1) * D], ident)
            r.then_inc(zt_ready, 1)

        def norm_store(act, n, bank):
            act.wait_ge(zt_ready, n)
            nc.scalar.copy(zT[:, :], banks[:, bank, :]).then_inc(zT_ready, 1)

        dve_base = [0]
        pool_base = [4]
        norms = [1]
        clears = 16 * (-(-X_ROWS // 4096) - (-Y_ROWS // 4096))

        with nc.Block() as block:
            @block.sync
            def _(sp):
                sp.dma_start(x[:, 0:GT], ins["x"][:, 0:GT]).then_inc(loaded, 16)
                sp.dma_start(const[:], ins["const"]).then_inc(loaded, 16)
                sp.dma_start(aux[:, :, :].rearrange("p a b -> p (a b)"), ins["spread"]).then_inc(loaded, 16)
                sp.dma_start(aw[:], ins["aw"]).then_inc(loaded, 16)
                sp.dma_start(ctxT[:], ins["ctxT"]).then_inc(loaded, 16)
                sp.dma_start(mask_i[:], ins["mask"]).then_inc(loaded, 16)
                sp.dma_start(x[:, GT:], ins["x"][:, GT:]).then_inc(loaded, 16)
                sp.dma_start(small[:], ins["small"]).then_inc(loaded, 16)
                sp.dma_start(ctxk[:], ins["ctxk"]).then_inc(loaded, 16)
                sp.dma_start(w_plain[:], ins["plain"]).then_inc(loaded, 16)
                sp.wait_ge(zeros_ready, 1)
                zero_rows = hid[:, :, :, :].rearrange("p s a b -> p (s a b)")
                per_dma = 4096 // D * P
                for rows, total in ((x_rows, X_ROWS), (y_rows, Y_ROWS)):
                    for r0 in range(0, total, per_dma):
                        n = min(per_dma, total - r0)
                        sp.dma_start(rows[r0:r0 + n, :].rearrange("(p a) d -> p (a d)", p=P),
                                     zero_rows[:, 0:n // P * D]).then_inc(cleared, 16)
                sp.wait_ge(loaded, 16 * 10)

            @block.gpsimd
            def _(pool):
                nc.gpsimd.memset(hid[:], 0.0).then_inc(zeros_ready, 1)
                nc.gpsimd.memset(mhalf[:], -0.5).then_inc(pool_step, 1)
                nc.gpsimd.memset(one_bf[:], 1.0).then_inc(pool_step, 1)
                nc.gpsimd.memset(count[:], 0.0).then_inc(pool_step, 1)
                nc.gpsimd.memset(vS[:], 0.0).then_inc(pool_step, 1)
                pool.wait_ge(pool_step, 4)
                norm_power(pool, 1)

            @block.vector
            def _(dve):
                dve.wait_ge(loaded, 16 * 10)
                st = Steps(dve, dve_step, 0)
                norm_stats(dve, st, 0)
                st.do(nc.vector.tensor_copy(id_bf[:], const[:, C_ID:C_ID + P]))
                st.do(nc.vector.tensor_copy(tri_bf[:], const[:, C_TRI:C_TRI + P]))
                st.do(nc.vector.memset(mask_b[:, KV:KE], 0.0))
                st.do(nc.vector.tensor_scalar(mask_b[:, 0:KV], mask_i[:], 0.0, MASKED, ALU.is_equal, ALU.mult))
                st.do(nc.vector.tensor_copy(spread[:].rearrange("p a b c d -> p (a b c d)"), aux[:, :, :].rearrange("p a b -> p (a b)")))
                st.do(nc.vector.tensor_copy(kR[:, :, :, KV:KE], const[:, C_ZERO:C_ZERO + 1].unsqueeze(1).unsqueeze(1)
                                            .to_broadcast([P, HQ, TG, 1])))
                st.do(nc.vector.tensor_scalar(mask_v[:], mask_i[:], 0.0, None, ALU.not_equal))
                st.settle()
                st.do(nc.vector.tensor_reduce(rowok[:], mask_v[:], AX.X, ALU.max))
                norm_apply(dve, 1, 0, first=True)
                st.settle()
                dve_base[0] = st.n

            @block.tensor
            def _(pe):
                pe.wait_ge(loaded, 16 * 10)
                norm_transpose(pe, 1, 7)

            @block.scalar
            def _(act):
                norm_store(act, 1, 7)

        class Combine:

            def __init__(self, tag, mix):
                self.mix = mix
                if mix is not None:
                    self.K = mix.topk
                    self.landed = [signal(f"{tag}_landed{i}") for i in range(TG)]
                    self.added = signal(f"{tag}_added")
                    self.idx = signal(f"{tag}_idx")

            def start(self, dve):
                if self.mix is not None:
                    dve.sem_inc(self.added, 1)

            def gather(self, pool, g):
                if self.mix is None:
                    return
                n = TG * self.K
                pool.wait_ge(self.added, g * TG + 1)
                nc.gpsimd.tensor_copy(idx_in[:, 0:n], idx_all[:, bass.ds(g * n, n)]).then_inc(self.idx, 1)
                pool.wait_ge(self.idx, g + 1)
                pool.nop(nofuse=True)
                for i in range(TG):
                    for k in range(self.K):
                        c = i * self.K + k
                        pool.indirect_dma_start(y_in[:, c, :], None, y_rows[:, :],
                                                bass.IndirectOffsetOnAxis(ap=idx_in[:, c:c + 1], axis=0))\
                            .then_inc(self.landed[i], 16)

            def add(self, dve, st, g):
                if self.mix is None:
                    return
                K = self.K
                n = TG * K
                st.do(nc.vector.tensor_copy(wt_in[:, 0:n], wt_all[:, bass.ds(g * n, n)]))
                st.settle()
                for k in range(K):
                    for i in range(TG):
                        at = bass.ds(g * GT + i * D, D)
                        if k == 0:
                            dve.wait_ge(self.landed[i], (g + 1) * (16 * K))
                        r = nc.vector.scalar_tensor_tensor(out=x[:, at], in0=y_in[:, i * K + k, :],
                                                           scalar=wt_in[:, i * K + k:i * K + k + 1], in1=x[:, at],
                                                           op0=ALU.mult, op1=ALU.add)
                        if k == K - 1:
                            r.then_inc(self.added, 1)
                        else:
                            st.do(r)
                    if k < K - 1:
                        st.settle()
                dve.wait_ge(self.added, g * TG + (TG + 1))

            def first_norm(self, dve, st):
                if self.mix is not None:
                    self.add(dve, st, 0)
                    if self.mix.layer == 0:
                        add_bias0(st, 0)
                    norm_stats(dve, st, 0)

        def add_bias0(st, g):
            at = bass.ds(g * GT, GT)
            xv = x[:, at].rearrange("p (i d) -> p i d", d=D)
            st.do(nc.vector.tensor_tensor(xv, xv, sm("bias0").unsqueeze(1).to_broadcast([P, TG, D]), ALU.add))
            st.settle()

        def over_groups(eng, body):
            with eng.Fori(0, NG - 1) as g:
                body(g, False)
            body(NG - 1, True)

        def next_group(dve, st, comb, g, last):
            nxt = 0 if last else (g + 1) * GT
            if not last:
                comb.add(dve, st, g + 1)
                if comb.mix is not None and comb.mix.layer == 0:
                    add_bias0(st, g + 1)
            norm_stats(dve, st, nxt)
            return nxt

        def heads_phase(tag, softmax, comb_mix):
            q_mm, k_mm, v_mm = signal(f"{tag}_q_mm"), signal(f"{tag}_k_mm"), signal(f"{tag}_v_mm")
            hi_done = signal(f"{tag}_hi")
            lo_done = signal(f"{tag}_lo")
            sp_mm = signal(f"{tag}_sp_mm")
            sp_act, sp_dve = signal(f"{tag}_sp_act"), signal(f"{tag}_sp_dve")
            v_done = signal(f"{tag}_v_done")
            ctx_ready = signal(f"{tag}_ctx")
            s_mm = signal(f"{tag}_s_mm")
            s_free = signal(f"{tag}_s_free")
            p_done = signal(f"{tag}_p_done")
            pt_mm = signal(f"{tag}_pt_mm")
            pt_act, pt_dve = signal(f"{tag}_pt_act"), signal(f"{tag}_pt_dve")
            o_mm = signal(f"{tag}_o_mm")
            ow_done = signal(f"{tag}_ow")
            ow_mm = signal(f"{tag}_ow_mm")
            o_used = signal(f"{tag}_o_used")
            ot_mm = signal(f"{tag}_ot_mm")
            ot_done = signal(f"{tag}_ot_done")
            out_mm = signal(f"{tag}_out_mm")
            x_added = signal(f"{tag}_x_added")
            wq, wk, wv, wo = (weight(c + ("3" if softmax else "0")) for c in "qkvo")
            bq, bk = (sm("bq3"), sm("bk3")) if softmax else (zero1, zero1)
            scale = float(HD) ** -0.5
            comb = Combine(tag, comb_mix)
            LN0 = norms[0] - (0 if comb_mix is not None else 1)
            norms[0] = LN0 + 1 + NG
            cen = aux[:, :, :].rearrange("p a b -> p (a b)")[:, 0:NH * KV].rearrange("p (h k) -> p h k", k=KV)
            prob = hid[:, :, :, :].rearrange("p s a b -> p s (a b)")[:, :, 0:NH * KV]\
                .rearrange("p s (h k) -> p s h k", k=KV)
            base = dve_base[0]

            with nc.Block() as block:
                @block.gpsimd
                def _(pool):
                    if softmax:
                        nc.gpsimd.memset(vS[:], 0.0).then_inc(pool_step, 1)
                        pool.wait_ge(pool_step, pool_base[0] + 1)
                        nc.gpsimd.memset(vS[:, :, :, :, HD:HD + 1].rearrange("p a b c w -> p (a b c) w"), 1.0)\
                            .then_inc(pool_step, 1)
                        pool.wait_ge(pool_step, pool_base[0] + 2)
                        pool_base[0] += 2
                    if comb_mix is not None:
                        comb.gather(pool, 0)
                        norm_power(pool, LN0 + 1)

                    def body(g, last):
                        pool.wait_ge(v_mm, g + 1)
                        nc.gpsimd.tensor_copy(ctxg[:, :], ctxT[:, bass.ds(g * GK, GK)]).then_inc(ctx_ready, 1)
                        if not last:
                            comb.gather(pool, g + 1)
                        norm_power(pool, g + (LN0 + 2))
                    over_groups(pool, body)

                @block.tensor
                def _(pe):
                    pe.sem_inc(v_mm, 1)
                    pe.sem_inc(o_mm, 2)
                    pe.sem_inc(out_mm, 2)
                    if softmax:
                        pe.sem_inc(ot_mm, 2)
                        pe.sem_inc(pt_mm, 8)
                        pe.sem_inc(ow_mm, 1)

                    def spread_side(g, side, hi, lo, width):
                        for t in range(HQ):
                            if side:
                                pe.wait_ge((sp_act, sp_dve)[t // 2], g * 4 + (t % 2 + 1))
                            nc.tensor.matmul(banks[:, t, 0:width], spread[:, side, 0, t, :], hi, start=True, stop=False)
                            nc.tensor.matmul(banks[:, t, 0:width], spread[:, side, 1, t, :], lo, start=False,
                                             stop=True).then_inc(sp_mm, 1)

                    def scores(g, b):
                        for half in range(2):
                            pe.wait_ge(s_free, g * 8 + (2 * b + half + 1))
                            for j in (2 * half, 2 * half + 1):
                                rows = slice(32 * j, 32 * j + 32)
                                if softmax:
                                    nc.tensor.matmul(banks[:, j, 0:HQ * KE], id_bf[:, :],
                                                     mask_b[:, :].unsqueeze(1).to_broadcast([P, HQ, KE]),
                                                     start=True, stop=False)
                                for t in range(HQ):
                                    if softmax:
                                        r = nc.tensor.matmul(banks[:, j, t * KE:(t + 1) * KE], qR[rows, t, b * P:(b + 1) * P],
                                                             kR[rows, t, b, :], start=False, stop=(t == HQ - 1))
                                    else:
                                        r = nc.tensor.matmul(banks[0:KV, j, t * P:(t + 1) * P], kR[rows, t, b, 0:KV],
                                                             qR[rows, t, b * P:(b + 1) * P], start=True, stop=True)
                            r.then_inc(s_mm, 1)

                    def turn_probs(g, b):
                        for quad in range(4):
                            if quad % 2 == 0:
                                pe.wait_ge(p_done, g * 8 + (2 * b + quad // 2 + 1))
                            pe.wait_ge((pt_act, pt_dve)[quad % 2], g * 8 + (2 * b + quad // 2 + 1))
                            for n in range(4):
                                r = nc.tensor.transpose(banks[0:KV, 4 + quad % 2, n * P:(n + 1) * P],
                                                        prob[:, b % 2, 4 * quad + n, :], ident)
                            r.then_inc(pt_mm, 1)

                    def values(g, b):
                        if softmax:
                            pe.wait_ge(pt_act, g * 8 + (2 * b + 3))
                            pe.wait_ge(pt_dve, g * 8 + (2 * b + 3))
                            pe.wait_ge(ow_done, g * 4 + (b + 1))
                            for t in range(HQ):
                                for j in range(HQ):
                                    r = nc.tensor.matmul(banks[32 * j:32 * j + 32, 6, t * P:(t + 1) * P],
                                                         vS[:, b, t, j, :], pt[:, b % 2, HQ * j + t, :], start=True, stop=True)
                        else:
                            pe.wait_ge(s_free, g * 8 + (2 * b + 4))
                            pe.wait_ge(ot_done, g * 4 + (b + 1))
                            for t in range(HQ):
                                for j in range(HQ):
                                    r = nc.tensor.matmul(banks[32 * t:32 * t + 32, 4 + b % 2, 0:P], vS[:, b, t, j, :],
                                                         pt[:, b % 2, HQ * j + t, :], start=(j == 0), stop=(j == HQ - 1))
                        r.then_inc(o_mm, 1)

                    def turn_back(g, b):
                        pe.wait_ge(ow_done, g * 4 + (b + 2))
                        pe.wait_ge(x_added, g * 4 + (b + 2))
                        for t in range(HQ):
                            r = nc.tensor.transpose(banks[:, 7, t * P:(t + 1) * P], oW[:, t * P:(t + 1) * P], ident)
                        r.then_inc(ow_mm, 1)

                    def turn_outputs(g, b):
                        pe.wait_ge(o_used, g * 4 + (b + 3))
                        nc.tensor.transpose(banks[:, 7, 0:P], oS[:, b % 2, :], ident).then_inc(ot_mm, 1)

                    def project(g, b):
                        pe.wait_ge(ot_done, g * 4 + (b + 3))
                        if not softmax:
                            pe.wait_ge(x_added, g * 4 + (b + 2))
                        nc.tensor.matmul(banks[:, 7, P:2 * P], oT[:, b % 2, :], wo,
                                         start=True, stop=True).then_inc(out_mm, 1)

                    if comb_mix is not None:
                        norm_transpose(pe, LN0 + 1, 6)
                    with pe.Fori(0, NG) as g:
                        pe.wait_ge(zT_ready, g + (LN0 + 1))
                        nc.tensor.matmul(banks[:, 6, :], wq, zT[:, :], start=True, stop=True).then_inc(q_mm, 1)
                        pe.wait_ge(ctx_ready, g + 1)
                        pe.wait_ge(x_added, g * 4 + 2)
                        nc.tensor.matmul(banks[:, 7, 0:GK], wk, ctxg[:, :], start=True, stop=True).then_inc(k_mm, 1)
                        pe.wait_ge(s_free, g * 8 + 2)
                        pe.wait_ge(lo_done, g * 2 + 1)
                        spread_side(g, 0, q_hi[:, :], q_lo[:, :], GT)
                        for b in range(TG):
                            r = nc.tensor.matmul(banks[0:KV, 6, b * P:(b + 1) * P], ctxg[:, b * KV:(b + 1) * KV], wv,
                                                 start=True, stop=True)
                        r.then_inc(v_mm, 1)
                        pe.wait_ge(lo_done, g * 2 + 2)
                        spread_side(g, 1, k_hi[:, :], k_lo[:, :], GK)
                        pe.wait_ge(sp_act, g * 4 + 4)
                        pe.wait_ge(sp_dve, g * 4 + 4)
                        scores(g, 0)
                        pe.wait_ge(v_done, g + 1)
                        for b in range(TG):
                            if b + 1 < TG:
                                scores(g, b + 1)
                            if softmax:
                                if b >= 1:
                                    turn_back(g, b - 1)
                                turn_probs(g, b)
                                if b >= 1:
                                    turn_outputs(g, b - 1)
                            values(g, b)
                            if b >= 1:
                                project(g, b - 1)
                        if softmax:
                            turn_back(g, TG - 1)
                            turn_outputs(g, TG - 1)
                        norm_transpose(pe, g + (LN0 + 2), 6)
                        project(g, TG - 1)

                @block.scalar
                def _(act):
                    act.sem_inc(ot_done, 2)
                    if softmax:
                        act.sem_inc(pt_act, 1)
                        act.sem_inc(ow_done, 1)
                    else:
                        act.sem_inc(s_free, 2)

                    def weigh(g, b):
                        for half in range(2):
                            if softmax:
                                act.wait_ge(s_free, g * 8 + (2 * b + half + 3))
                                if half == 0:
                                    act.wait_ge(pt_mm, g * 16 + (4 * b + 4))
                                nc.scalar.activation(prob[:, b % 2, 8 * half:8 * half + 8, :], cen[:, 8 * half:8 * half + 8, :],
                                                     ACT.Exp, scale=scale).then_inc(p_done, 1)
                            else:
                                act.wait_ge(s_mm, g * 8 + (2 * b + half + 1))
                                if half == 0:
                                    act.wait_ge(o_mm, g * 4 + (b + 1))
                                nc.scalar.activation(pt[:, b % 2, 8 * half:8 * half + 8, :].rearrange("p h k -> p (h k)"),
                                                     banks[0:KV, 2 * half:2 * half + 2, :].rearrange("p h k -> p (h k)"),
                                                     ACT.Sigmoid, scale=scale).then_inc(s_free, 1)

                    def probs_copy(g, b):
                        act.wait_ge(o_mm, g * 4 + (b + 1))
                        for quad in (0, 2):
                            act.wait_ge(pt_mm, g * 16 + (4 * b + quad + 9))
                            nc.scalar.copy(pt[:, b % 2, 4 * quad:4 * quad + 4, :].rearrange("p h k -> p (h k)"),
                                           banks[0:KV, 4, :]).then_inc(pt_act, 1)

                    def wide_copy(g, b):
                        act.wait_ge(o_mm, g * 4 + (b + 3))
                        act.wait_ge(ow_mm, g * 4 + (b + 1))
                        nc.scalar.copy(oW[:, :], banks[:, 6, :]).then_inc(ow_done, 1)

                    def turned(g, b):
                        act.wait_ge(out_mm, g * 4 + (b + 1))
                        if softmax:
                            act.wait_ge(ot_mm, g * 4 + (b + 3))
                            nc.scalar.copy(oT[:, b % 2, :], banks[:, 7, 0:P]).then_inc(ot_done, 1)
                        else:
                            act.wait_ge(o_mm, g * 4 + (b + 3))
                            nc.scalar.copy(oT[:, b % 2, :], banks[:, 4 + b % 2, 0:P]).then_inc(ot_done, 1)

                    if comb_mix is not None:
                        norm_store(act, LN0 + 1, 6)
                    with act.Fori(0, NG) as g:
                        act.wait_ge(q_mm, g + 1)
                        nc.scalar.activation(q_hi[:, :], banks[:, 6, :], ACT.Identity, bias=bq).then_inc(hi_done, 1)
                        act.wait_ge(k_mm, g + 1)
                        nc.scalar.activation(k_hi[:, :], banks[:, 7, 0:GK], ACT.Identity, bias=bk).then_inc(hi_done, 1)
                        for t in range(2):
                            act.wait_ge(sp_mm, g * 8 + (t + 1))
                            nc.scalar.copy(qR[:, t, :], banks[:, t, :]).then_inc(sp_act, 1)
                        for t in range(2):
                            act.wait_ge(sp_mm, g * 8 + (t + 5))
                            nc.scalar.copy(kR[:, t, :, 0:KV], banks[:, t, 0:GK].rearrange("p (b k) -> p b k", k=KV))\
                                .then_inc(sp_act, 1)
                        weigh(g, 0)
                        for b in range(TG):
                            if b + 1 < TG:
                                weigh(g, b + 1)
                            if softmax:
                                probs_copy(g, b)
                                if b >= 1:
                                    turned(g, b - 1)
                                wide_copy(g, b)
                            else:
                                turned(g, b)
                        if softmax:
                            turned(g, TG - 1)
                        norm_store(act, g + (LN0 + 2), 6)

                @block.vector
                def _(dve):
                    dve.sem_inc(x_added, 2)
                    if softmax:
                        dve.sem_inc(o_used, 2)
                        dve.sem_inc(pt_dve, 1)
                        dve.sem_inc(s_free, 2)

                    def centre(st, g, b):
                        for half in range(2):
                            s = banks[:, 2 * half:2 * half + 2, 0:HQ * KE].rearrange("p q (j k) -> p q j k", k=KE)[:, :, :, 0:KV]
                            m = mx[:, 8 * half:8 * half + 8].rearrange("p (q j) -> p q j", j=HQ)
                            dve.wait_ge(s_mm, g * 8 + (2 * b + half + 1))
                            st.do(nc.vector.tensor_reduce(m, s, AX.X, ALU.max))
                            st.settle()
                            if not (b == 0):
                                dve.wait_ge(p_done, g * 8 + (2 * b + half - 1))
                            nc.vector.tensor_tensor(cen[:, 8 * half:8 * half + 8, :].rearrange("p (q j) k -> p q j k", j=HQ),
                                                    s, m.unsqueeze(3).to_broadcast([P, 2, HQ, KV]),
                                                    ALU.subtract).then_inc(s_free, 1)

                    def probs_copy(g, b):
                        dve.wait_ge(o_mm, g * 4 + (b + 1))
                        for quad in (1, 3):
                            dve.wait_ge(pt_mm, g * 16 + (4 * b + quad + 9))
                            nc.vector.tensor_copy(pt[:, b % 2, 4 * quad:4 * quad + 4, :].rearrange("p h k -> p (h k)"),
                                                  banks[0:KV, 5, :]).then_inc(pt_dve, 1)

                    def normalise(st, g, b):
                        o = banks[:, 7, :].rearrange("p (h w) -> p h w", w=32)
                        dve.wait_ge(ow_mm, g * 4 + (b + 2))
                        st.do(nc.vector.reciprocal(rs[:, :], o[:, :, HD]))
                        st.settle()
                        st.do(nc.vector.tensor_scalar(rs[:, :], rs[:, :], rowok[:, 0:1], None, ALU.mult))
                        st.settle()
                        dve.wait_ge(ot_mm, g * 4 + (b + 1))
                        nc.vector.tensor_tensor(oS[:, b % 2, :].rearrange("p (h w) -> p h w", w=HD), o[:, :, 0:HD],
                                                rs[:, :].unsqueeze(2).to_broadcast([P, NH, HD]),
                                                ALU.mult).then_inc(o_used, 1)

                    def add(st, g, b):
                        at = bass.ds(g * GT + b * P, P)
                        dve.wait_ge(out_mm, g * 4 + (b + 3))
                        if softmax:
                            st.do(nc.vector.tensor_tensor(tmp[:, :], banks[:, 7, P:2 * P], sm("bo3"), ALU.add))
                            st.settle()
                            nc.vector.tensor_tensor(x[:, at], x[:, at], tmp[:, :], ALU.add).then_inc(x_added, 1)
                        else:
                            nc.vector.tensor_tensor(x[:, at], x[:, at], banks[:, 7, P:2 * P], ALU.add).then_inc(x_added, 1)

                    comb.start(dve)
                    pre = Steps(dve, dve_step, base)
                    if comb_mix is not None:
                        comb.first_norm(dve, pre)
                        norm_apply(dve, LN0 + 1, 0)

                    def body(g, last):
                        st = Steps(dve, dve_step, g * PER + (base + pre.n))
                        dve.wait_ge(hi_done, g * 2 + 1)
                        nc.vector.scalar_tensor_tensor(out=q_lo[:, :], in0=banks[:, 6, :], scalar=bq, in1=q_hi[:, :].bitcast(F32),
                                                       op0=ALU.add, op1=ALU.subtract).then_inc(lo_done, 1)
                        dve.wait_ge(hi_done, g * 2 + 2)
                        nc.vector.scalar_tensor_tensor(out=k_lo[:, :], in0=banks[:, 7, 0:GK], scalar=bk,
                                                       in1=k_hi[:, :].bitcast(F32),
                                                       op0=ALU.add, op1=ALU.subtract).then_inc(lo_done, 1)
                        for t in range(2, 4):
                            dve.wait_ge(sp_mm, g * 8 + (t + 1))
                            nc.vector.tensor_copy(qR[:, t, :], banks[:, t, :]).then_inc(sp_dve, 1)
                        dve.wait_ge(v_mm, g + 2)
                        vin = banks[0:KV, 6, :].rearrange("p (b c i w) -> p b c i w", b=TG, c=HQ, w=HD)
                        for t in range(2, 4):
                            dve.wait_ge(sp_mm, g * 8 + (t + 5))
                            nc.vector.tensor_copy(kR[:, t, :, 0:KV], banks[:, t, 0:GK].rearrange("p (b k) -> p b k", k=KV))\
                                .then_inc(sp_dve, 1)
                        if softmax:
                            bv = sm("bv3")[0:KV, :].rearrange("p (c i w) -> p c i w", c=HQ, w=HD)
                            for b in range(TG):
                                r = nc.vector.tensor_tensor(vS[:, b, :, :, 0:HD], vin[:, b], bv, ALU.add)
                            r.then_inc(v_done, 1)
                            centre(st, g, 0)
                        else:
                            for i in range(HQ):
                                r = nc.vector.tensor_copy(vS[:, :, :, i, HD * i:HD * i + HD], vin[:, :, :, i, :])
                            r.then_inc(v_done, 1)
                        for b in range(TG):
                            if softmax:
                                if b + 1 < TG:
                                    centre(st, g, b + 1)
                                if b >= 1:
                                    normalise(st, g, b - 1)
                                probs_copy(g, b)
                            if b >= 1:
                                add(st, g, b - 1)
                            if b == 1:
                                nxt = next_group(dve, st, comb, g, last)
                            if b == 2:
                                norm_apply(dve, g + (LN0 + 2), nxt)
                        if softmax:
                            normalise(st, g, TG - 1)
                        add(st, g, TG - 1)
                        assert last or st.n == PER, (tag, st.n)
                        dve_base[0] = base + pre.n + (NG - 1) * PER + st.n
                    PER = STEPS[tag]
                    over_groups(dve, body)

        def plain_phase(tag, comb_mix):
            e_mm, cen_done, p_done = signal(f"{tag}_e_mm"), signal(f"{tag}_cen"), signal(f"{tag}_p")
            pt_mm, pt_done, out_mm = signal(f"{tag}_pt_mm"), signal(f"{tag}_pt"), signal(f"{tag}_out_mm")
            x_added = signal(f"{tag}_x")
            comb = Combine(tag, comb_mix)
            LN0 = norms[0]
            norms[0] = LN0 + 1 + NG
            base = dve_base[0]
            cen = aux[:, 0, 0:GK].rearrange("p (b k) -> p b k", k=KV)
            prob = aux[:, 1, 0:GK].rearrange("p (b k) -> p b k", k=KV)
            pT = aux[0:KV, 2, :]

            with nc.Block() as block:
                @block.gpsimd
                def _(pool):
                    comb.gather(pool, 0)
                    norm_power(pool, LN0 + 1)

                    def body(g, last):
                        if not last:
                            comb.gather(pool, g + 1)
                        norm_power(pool, g + (LN0 + 2))
                    over_groups(pool, body)

                @block.tensor
                def _(pe):
                    norm_transpose(pe, LN0 + 1, 3)
                    with pe.Fori(0, NG) as g:
                        pe.wait_ge(zT_ready, g + (LN0 + 1))
                        for b in range(TG):
                            r = nc.tensor.matmul(banks[:, 0, b * KV:(b + 1) * KV], zT[:, b * P:(b + 1) * P],
                                                 ctxT[:, bass.ds(g * GK + b * KV, KV)], start=True, stop=True)
                        r.then_inc(e_mm, 1)
                        pe.wait_ge(p_done, g + 1)
                        for b in range(TG):
                            r = nc.tensor.transpose(banks[0:KV, 1, b * P:(b + 1) * P], prob[:, b, :], ident)
                        r.then_inc(pt_mm, 1)
                        pe.wait_ge(pt_done, g + 1)
                        pe.wait_ge(x_added, g + 1)
                        for b in range(TG):
                            r = nc.tensor.matmul(banks[:, 2, b * P:(b + 1) * P], pT[:, b * P:(b + 1) * P],
                                                 ctxk[:, bass.ds(g * GT + b * D, D)], start=True, stop=True)
                        r.then_inc(out_mm, 1)
                        norm_transpose(pe, g + (LN0 + 2), 3)

                @block.scalar
                def _(act):
                    norm_store(act, LN0 + 1, 3)
                    with act.Fori(0, NG) as g:
                        act.wait_ge(cen_done, g + 1)
                        nc.scalar.activation(prob, cen, ACT.Exp).then_inc(p_done, 1)
                        act.wait_ge(pt_mm, g + 1)
                        nc.scalar.copy(pT, banks[0:KV, 1, :]).then_inc(pt_done, 1)
                        norm_store(act, g + (LN0 + 2), 3)

                @block.vector
                def _(dve):
                    dve.sem_inc(x_added, 1)
                    comb.start(dve)
                    pre = Steps(dve, dve_step, base)
                    comb.first_norm(dve, pre)
                    norm_apply(dve, LN0 + 1, 0)
                    PER = STEPS[tag]

                    def body(g, last):
                        st = Steps(dve, dve_step, g * PER + (base + pre.n))
                        s = banks[:, 0, 0:GK].rearrange("p (b k) -> p b k", k=KV)
                        dve.wait_ge(e_mm, g + 1)
                        st.do(nc.vector.tensor_reduce(mx[:, 0:TG], s, AX.X, ALU.max))
                        st.settle()
                        nc.vector.tensor_tensor(cen, s, mx[:, 0:TG].unsqueeze(2).to_broadcast([P, TG, KV]),
                                                ALU.subtract).then_inc(cen_done, 1)
                        dve.wait_ge(p_done, g + 1)
                        st.do(nc.vector.tensor_reduce(den[:, :], prob, AX.X, ALU.add))
                        st.settle()
                        st.do(nc.vector.reciprocal(rden[:, :], den[:, :]))
                        st.settle()
                        dve.wait_ge(out_mm, g + 1)
                        for b in range(TG):
                            at = bass.ds(g * GT + b * P, P)
                            r = nc.vector.scalar_tensor_tensor(out=x[:, at], in0=banks[:, 2, b * P:(b + 1) * P],
                                                               scalar=rden[:, b:b + 1], in1=x[:, at],
                                                               op0=ALU.mult, op1=ALU.add)
                        r.then_inc(x_added, 1)
                        nxt = next_group(dve, st, comb, g, last)
                        norm_apply(dve, g + (LN0 + 2), nxt)
                        assert last or st.n == PER, (tag, st.n)
                        dve_base[0] = base + pre.n + (NG - 1) * PER + st.n
                    over_groups(dve, body)

        def gelu_phase(tag, comb_mix):
            ctx_ready, h_mm, g_done = signal(f"{tag}_ctx"), signal(f"{tag}_h_mm"), signal(f"{tag}_g")
            out_mm, x_added = signal(f"{tag}_out_mm"), signal(f"{tag}_x")
            comb = Combine(tag, comb_mix)
            LN0 = norms[0]
            norms[0] = LN0 + 1 + NG
            base = dve_base[0]
            gT = aux[0:KV, 0, :]

            with nc.Block() as block:
                @block.gpsimd
                def _(pool):
                    comb.gather(pool, 0)
                    norm_power(pool, LN0 + 1)

                    def body(g, last):
                        pool.wait_ge(h_mm, g + 1)
                        nc.gpsimd.tensor_copy(ctxg[:, :], ctxT[:, bass.ds(g * GK, GK)]).then_inc(ctx_ready, 1)
                        if not last:
                            comb.gather(pool, g + 1)
                        norm_power(pool, g + (LN0 + 2))
                    over_groups(pool, body)

                @block.tensor
                def _(pe):
                    pe.sem_inc(h_mm, 1)
                    norm_transpose(pe, LN0 + 1, 3)
                    with pe.Fori(0, NG) as g:
                        pe.wait_ge(zT_ready, g + (LN0 + 1))
                        pe.wait_ge(ctx_ready, g + 1)
                        for b in range(TG):
                            r = nc.tensor.matmul(banks[0:KV, 0, b * P:(b + 1) * P], ctxg[:, b * KV:(b + 1) * KV],
                                                 zT[:, b * P:(b + 1) * P], start=True, stop=True)
                        r.then_inc(h_mm, 1)
                        pe.wait_ge(g_done, g + 1)
                        pe.wait_ge(x_added, g + 1)
                        for b in range(TG):
                            r = nc.tensor.matmul(banks[:, 2, b * P:(b + 1) * P], gT[:, b * P:(b + 1) * P],
                                                 ctxk[:, bass.ds(g * GT + b * D, D)], start=True, stop=True)
                        r.then_inc(out_mm, 1)
                        norm_transpose(pe, g + (LN0 + 2), 3)

                @block.scalar
                def _(act):
                    norm_store(act, LN0 + 1, 3)
                    with act.Fori(0, NG) as g:
                        act.wait_ge(h_mm, g + 2)
                        nc.scalar.activation(gT, banks[0:KV, 0, :], ACT.Gelu_apprx_tanh).then_inc(g_done, 1)
                        norm_store(act, g + (LN0 + 2), 3)

                @block.vector
                def _(dve):
                    dve.sem_inc(x_added, 1)
                    comb.start(dve)
                    pre = Steps(dve, dve_step, base)
                    comb.first_norm(dve, pre)
                    norm_apply(dve, LN0 + 1, 0)
                    PER = STEPS[tag]

                    def body(g, last):
                        st = Steps(dve, dve_step, g * PER + (base + pre.n))
                        dve.wait_ge(out_mm, g + 1)
                        at = bass.ds(g * GT, GT)
                        nc.vector.tensor_tensor(x[:, at], x[:, at], banks[:, 2, :], ALU.add).then_inc(x_added, 1)
                        nxt = next_group(dve, st, comb, g, last)
                        norm_apply(dve, g + (LN0 + 2), nxt)
                        assert last or st.n == PER, (tag, st.n)
                        dve_base[0] = base + pre.n + (NG - 1) * PER + st.n
                    over_groups(dve, body)

        def route_phase(tag, mix):
            chunks, C, EX, hidden = mix.chunks, mix.C, mix.plain, mix.hidden
            K, cap = mix.topk, mix.cap
            NB, NU, NC = mix.banks, EX * mix.U, EX * mix.C
            per_choice = mix.layer == 0
            nk = K * NE if per_choice else NE
            CR = 4
            Y0, RT, TP = 4, 6, 7
            w0 = sum(PLAIN[0:mix.layer])
            wide = mix.up + mix.down
            plain_w = [w_plain[:, w0 + e * wide:w0 + (e + 1) * wide] for e in range(EX)]
            l_mm = signal(f"{tag}_l_mm")
            sub_done = signal(f"{tag}_sub")
            e_done = signal(f"{tag}_exp")
            oh_done = signal(f"{tag}_oh")
            r_mm = signal(f"{tag}_r_mm")
            h_mm = signal(f"{tag}_h_mm")
            a_done = signal(f"{tag}_a_done")
            m_done = signal(f"{tag}_m_done")
            y_mm = signal(f"{tag}_y_mm")
            y_used = signal(f"{tag}_y_used")
            idx_ready = signal(f"{tag}_idx")
            z_copied = signal(f"{tag}_z")
            sent = signal(f"{tag}_sent")
            LN0 = norms[0] - 1
            norms[0] += NG - 1
            base = dve_base[0]
            odd = EX % 2
            out_free = signal(f"{tag}_out_free")
            SENT = 16 * TG * K

            with nc.Block() as block:
                @block.gpsimd
                def _(pool):
                    pool.sem_inc(out_free, 1)
                    pool.wait_ge(cleared, clears)
                    if mix.layer:
                        nc.gpsimd.memset(count[:], 0.0).then_inc(pool_step, 1)
                        pool_base[0] += 1
                        pool.wait_ge(pool_step, pool_base[0])

                    def body(g, last):
                        if not last:
                            norm_power(pool, g + (LN0 + 2))
                        pool.wait_ge(idx_ready, g + 2)
                        pool.wait_ge(z_copied, g + 1)
                        pool.nop(nofuse=True)
                        for i in range(TG):
                            for k in range(K):
                                c = i * K + k
                                pool.indirect_dma_start(x_rows[:, :], bass.IndirectOffsetOnAxis(ap=idx_out[:, c:c + 1], axis=0),
                                                        z_out[:, i * D:(i + 1) * D], None).then_inc(sent, 16)
                        pool.wait_ge(sent, g * SENT + SENT)
                        pool.sem_inc(out_free, 1)
                    over_groups(pool, body)

                @block.tensor
                def _(pe):
                    if EX:
                        pe.sem_inc(y_mm, 2)

                    def rise(g, e):
                        n = e * mix.U
                        for c, (at, w) in enumerate(chunks):
                            for part in range(2):
                                q = n - NB
                                pe.wait_ge(m_done if q % 2 else a_done, g * NC + (q // 2 + 1 + CR))
                                up = plain_w[e][:, part * hidden + at:part * hidden + at + w]
                                nc.tensor.matmul(banks[0:w, n % NB, :], up, zT[:, :], start=True, stop=True).then_inc(h_mm, 1)
                                n += 1

                    def fall(g, e):
                        pe.wait_ge(m_done, g * NC + ((e + 1) * C + CR))
                        pe.wait_ge(y_used, g * EX + (e + 1 + (odd if e == 0 else 0)))
                        for i in range(TG):
                            for c, (_, w) in enumerate(chunks):
                                r = nc.tensor.matmul(banks[:, Y0 + e % 2, i * D:(i + 1) * D],
                                                     hid[0:w, e % 2, c, i * P:(i + 1) * P],
                                                     plain_w[e][0:w, mix.up + c * D:mix.up + (c + 1) * D],
                                                     start=(c == 0), stop=(c == C - 1))
                        r.then_inc(y_mm, 1)

                    def body(g, last):
                        pe.wait_ge(zT_ready, g + (LN0 + 1))
                        pe.wait_ge(idx_ready, g + 1)
                        for i in range(TG):
                            r = nc.tensor.matmul(banks[:, RT, i * NE:(i + 1) * NE], zT[:, i * P:(i + 1) * P],
                                                 sm(f"rw{mix.layer}"), start=True, stop=True)
                        r.then_inc(l_mm, 1)
                        if EX:
                            rise(g, 0)
                        pe.wait_ge(oh_done, g + 1)
                        chosen = oh[:, :, 0:K, :].rearrange("p i k n -> p i (k n)") if per_choice or K == 1 else ohc[:, :, :]
                        R = banks[:, RT, 64:64 + TG * nk].rearrange("p (i n) -> p i n", n=nk)
                        T = banks[:, RT, 160:160 + nk]
                        nc.tensor.matmul(R, tri_bf[:, :], chosen, start=True, stop=False)
                        for i in range(TG - 1):
                            nc.tensor.matmul(R[:, i + 1:TG, :], one_bf[:, :],
                                             chosen[:, i:i + 1, :].to_broadcast([P, TG - 1 - i, nk]),
                                             start=False, stop=(i == TG - 2))
                        for i in range(TG):
                            r = nc.tensor.matmul(T, one_bf[:, :], chosen[:, i, :], start=(i == 0), stop=(i == TG - 1))
                        r.then_inc(r_mm, 1)
                        for e in range(EX):
                            if e + 1 < EX:
                                rise(g, e + 1)
                            fall(g, e)
                        if not last:
                            norm_transpose(pe, g + (LN0 + 2), TP)
                    over_groups(pe, body)

                @block.scalar
                def _(act):
                    act.sem_inc(a_done, CR)

                    def body(g, last):
                        act.wait_ge(z_ready, g + (LN0 + 1))
                        act.wait_ge(out_free, g + 1)
                        nc.scalar.copy(z_out[:, :], z[:, :]).then_inc(z_copied, 1)
                        act.wait_ge(sub_done, g + 1)
                        nc.scalar.activation(el[:, :, :], ls[:, :, :], ACT.Exp).then_inc(e_done, 1)
                        for e in range(EX):
                            for c, (_, w) in enumerate(chunks):
                                n = e * C + c
                                act.wait_ge(h_mm, g * NU + (2 * n + 1))
                                act.wait_ge(m_done, g * NC + (n - NC + 1 + CR))
                                nc.scalar.activation(aux[0:w, n, :], banks[0:w, (2 * n) % NB, :],
                                                     mix.act_fn).then_inc(a_done, 1)
                        if not last:
                            norm_store(act, g + (LN0 + 2), TP)
                    over_groups(act, body)

                @block.vector
                def _(dve):
                    dve.sem_inc(idx_ready, 1)
                    if EX:
                        dve.sem_inc(y_used, 2)
                        dve.sem_inc(m_done, CR)
                    dve.wait_ge(pool_step, pool_base[0])
                    PER = STEPS[tag]

                    def gate(g, e):
                        dve.wait_ge(y_mm, g * EX + (e + 1 + (odd if e == 0 else 0)))
                        for c, (_, w) in enumerate(chunks):
                            n = e * C + c
                            dve.wait_ge(a_done, g * NC + (n + 1 + CR))
                            dve.wait_ge(h_mm, g * NU + (2 * n + 2))
                            nc.vector.tensor_tensor(hid[0:w, e % 2, c, :], aux[0:w, n, :],
                                                    banks[0:w, (2 * n + 1) % NB, :], ALU.mult).then_inc(m_done, 1)

                    def choose(st, g):
                        dve.wait_ge(l_mm, g + 1)
                        L = banks[:, RT, 0:TG * NE].rearrange("p (i n) -> p i n", n=NE)
                        if mix.layer == 2:
                            st.do(nc.vector.tensor_tensor(lg[:, :, :], L, sm("ebias2").unsqueeze(1).to_broadcast([P, TG, NE]), ALU.add))
                        else:
                            st.do(nc.vector.tensor_copy(lg[:, :, :], L))
                        st.settle(apart=True)
                        for i in range(TG):
                            st.do(nc.vector.max(mx8[:, i, :], lg[:, i, :]))
                        st.settle()
                        nc.vector.tensor_tensor(ls[:, :, :], mx8[:, :, :], mx8[:, :, 0:1].to_broadcast([P, TG, NE]),
                                                ALU.subtract).then_inc(sub_done, 1)
                        for i in range(TG):
                            st.do(nc.vector.max_index(ix8[:, i, :], mx8[:, i, :], lg[:, i, :]))
                        st.settle()
                        st.do(nc.vector.tensor_copy(ixf[:, :, :], ix8[:, :, 0:2]))
                        st.settle()
                        for k in range(K):
                            r = nc.vector.tensor_tensor(oh[:, :, k, :], iota8.unsqueeze(1).to_broadcast([P, TG, NE]),
                                                        ixf[:, :, k:k + 1].to_broadcast([P, TG, NE]), ALU.is_equal)
                            if k < K - 1 or not (per_choice or K == 1):
                                st.do(r)
                        if not (per_choice or K == 1):
                            st.settle()
                            r = nc.vector.tensor_tensor(ohc[:, :, :], oh[:, :, 0, :], oh[:, :, 1, :], ALU.add)
                        r.then_inc(oh_done, 1)

                    def place(st, g):
                        n = TG * K
                        R = banks[:, RT, 64:64 + TG * nk].rearrange("p (i n) -> p i n", n=nk)
                        dve.wait_ge(r_mm, g + 1)
                        st.do(nc.vector.tensor_tensor(rank[:, :, 0:nk], R, count[:, 0:nk].unsqueeze(1).to_broadcast([P, TG, nk]), ALU.add))
                        st.settle()
                        st.do(nc.vector.tensor_tensor(count[:, 0:nk], count[:, 0:nk], banks[:, RT, 160:160 + nk], ALU.add))
                        for k in range(K):
                            a = k * NE if per_choice else 0
                            st.do(nc.vector.tensor_tensor(picked[:, :, k, :], oh[:, :, k, :], rank[:, :, a:a + NE], ALU.mult))
                        st.settle()
                        st.do(nc.vector.tensor_reduce(rk[:, :, 0:K], picked[:, :, 0:K, :], AX.X, ALU.add))
                        st.settle()
                        for k in range(K):
                            st.do(nc.vector.tensor_scalar(row[:, :, k], ixf[:, :, k], float(mix.region),
                                                          float((k * CAP0 if per_choice else 0) - 1), ALU.mult, ALU.add))
                        st.settle()
                        st.do(nc.vector.tensor_tensor(row[:, :, 0:K], row[:, :, 0:K], rk[:, :, 0:K], ALU.add))
                        st.settle()
                        if cap:
                            st.do(nc.vector.tensor_scalar(within[:, :, 0:K], rk[:, :, 0:K], float(cap), None, ALU.is_le))
                            st.settle()
                            aside = const[:, bass.ds(g * n + C_TRASH, n)].rearrange("p (i k) -> p i k", k=K)
                            for other, op in ((aside, ALU.subtract), (within[:, :, 0:K], ALU.mult), (aside, ALU.add)):
                                st.do(nc.vector.tensor_tensor(row[:, :, 0:K], row[:, :, 0:K], other, op))
                                st.settle()
                        here = bass.ds(g * n, n)
                        dve.wait_ge(out_free, g + 1)
                        if per_choice:
                            st.do(nc.vector.tensor_scalar(idx_all[:, here].rearrange("p (i k) -> p i k", k=K), row[:, :, 0:K],
                                                          float(TRASH), None, ALU.min))
                        else:
                            st.do(nc.vector.tensor_copy(rk_all[:, here].rearrange("p (i k) -> p i k", k=K), rk[:, :, 0:K]))
                            st.do(nc.vector.tensor_copy(ix_all[:, here].rearrange("p (i k) -> p i k", k=K), ixf[:, :, 0:K]))
                        nc.vector.tensor_copy(idx_out[:, 0:n].rearrange("p (i k) -> p i k", k=K), row[:, :, 0:K])\
                            .then_inc(idx_ready, 1)
                        dve.wait_ge(e_done, g + 1)
                        st.do(nc.vector.tensor_reduce(den[:, :], el[:, :, 0:2] if mix.renorm else el[:, :, :], AX.X, ALU.add))
                        st.settle()
                        st.do(nc.vector.reciprocal(rden[:, :], den[:, :]))
                        st.settle()
                        dst = wt if cap else wt_all[:, here].rearrange("p (i k) -> p i k", k=K)
                        st.do(nc.vector.tensor_tensor(dst[:, :, 0:K], el[:, :, 0:K], rden[:, :].unsqueeze(2).to_broadcast([P, TG, K]), ALU.mult))
                        if cap:
                            st.settle()
                            st.do(nc.vector.tensor_tensor(wt_all[:, here].rearrange("p (i k) -> p i k", k=K),
                                                          wt[:, :, 0:K], within[:, :, 0:K], ALU.mult))

                    def body(g, last):
                        st = Steps(dve, dve_step, g * PER + base)
                        choose(st, g)
                        if EX:
                            gate(g, 0)
                        if not last:
                            norm_stats(dve, st, (g + 1) * GT)
                        place(st, g)
                        if not last:
                            dve.wait_ge(z_copied, g + 1)
                            norm_apply(dve, g + (LN0 + 2), (g + 1) * GT)
                        for e in range(EX):
                            if e + 1 < EX:
                                gate(g, e + 1)
                            dve.wait_ge(y_mm, g * EX + (e + 3))
                            dve.wait_ge(y_used, g * EX + (e + 2))
                            at = bass.ds(g * GT, GT)
                            nc.vector.tensor_tensor(x[:, at], x[:, at], banks[:, Y0 + e % 2, :], ALU.add).then_inc(y_used, 1)
                        assert last or st.n == PER, (tag, st.n)
                        dve_base[0] = base + (NG - 1) * PER + st.n
                    over_groups(dve, body)
                    if not per_choice:
                        st = Steps(dve, dve_step, dve_base[0])
                        st.settle()
                        plan_blocks(st, mix)
                        dve_base[0] += st.n

        def plan_blocks(st, mix):
            v, K, NBK = nc.vector, mix.topk, mix.blocks
            if mix.cap:
                st.do(v.tensor_scalar(count[:, 0:NE], count[:, 0:NE], float(mix.cap), None, ALU.min))
                st.settle()
            over = hid[:, 0, 0, 0:NE * 16].rearrange("p (e m) -> p e m", m=16)
            st.do(v.tensor_tensor(over, count[:, 0:NE].unsqueeze(2).to_broadcast([P, NE, 16]),
                                  const[:, C_STEP:C_STEP + 16].unsqueeze(1).to_broadcast([P, NE, 16]), ALU.is_gt))
            st.settle()
            st.do(v.tensor_reduce(nblk[:, 0, :], over, AX.X, ALU.add))
            st.settle()
            src = 0
            for d, dst in ((1, 1), (2, 2), (4, 1)):
                st.do(v.tensor_copy(nblk[:, dst, 0:d], nblk[:, src, 0:d]))
                st.do(v.tensor_tensor(nblk[:, dst, d:NE], nblk[:, src, d:NE], nblk[:, src, 0:NE - d], ALU.add))
                st.settle()
                src = dst
            ends = nblk[:, src, :]
            st.do(v.tensor_tensor(first[:, :], ends, nblk[:, 0, :], ALU.subtract))
            st.settle()
            blk = const[0:1, C_BLK:C_BLK + NBK]
            past = hid[0:1, 1, 0, 0:NBK * NE].rearrange("p (j e) -> p j e", e=NE)
            held = hid[0:1, 1, 1, 0:NBK * NE].rearrange("p (j e) -> p j e", e=NE)
            st.do(v.tensor_tensor(past, ends[0:1].unsqueeze(1).to_broadcast([1, NBK, NE]),
                                  blk.unsqueeze(2).to_broadcast([1, NBK, NE]), ALU.is_le))
            st.settle()
            st.do(v.tensor_tensor(held, past, nblk[0:1, 0, :].unsqueeze(1).to_broadcast([1, NBK, NE]), ALU.mult))
            st.do(v.tensor_reduce(tab[:, 0, 0:NBK], past, AX.X, ALU.add))
            st.settle()
            st.do(v.tensor_reduce(tab[:, 1, 0:NBK], held, AX.X, ALU.add))
            st.do(v.tensor_scalar(tab_e[:, 0:NBK], tab[:, 0, 0:NBK], float(NE - 1), None, ALU.min))
            st.settle()
            st.do(v.tensor_tensor(tab[:, 1, 0:NBK], blk, tab[:, 1, 0:NBK], ALU.subtract))
            st.do(v.tensor_scalar(tab[:, 2, 0:NBK], tab[:, 0, 0:NBK], float(mix.region), None, ALU.mult))
            st.settle()
            st.do(v.scalar_tensor_tensor(out=tab[:, 0, 0:NBK], in0=tab[:, 1, 0:NBK], scalar=float(BLK), in1=tab[:, 2, 0:NBK],
                                         op0=ALU.mult, op1=ALU.add))
            st.settle()
            st.do(v.tensor_scalar(tab_r[:, 0:NBK], tab[:, 0, 0:NBK], float(NE * mix.region - BLK), None, ALU.min))
            n = B * K
            eq = hid[:, 0, 1, 0:n * NE].rearrange("p (n e) -> p n e", e=NE)
            st.do(v.tensor_tensor(eq, iota8.unsqueeze(1).to_broadcast([P, n, NE]),
                                  ix_all[:, 0:n].unsqueeze(2).to_broadcast([P, n, NE]), ALU.is_equal))
            st.settle()
            st.do(v.tensor_tensor(eq, eq, first[:, :].unsqueeze(1).to_broadcast([P, n, NE]), ALU.mult))
            st.settle()
            st.do(v.tensor_reduce(pos[:, 0:n], eq, AX.X, ALU.add))
            st.settle()
            st.do(v.tensor_scalar(pos[:, 0:n], pos[:, 0:n], float(BLK), -1.0, ALU.mult, ALU.add))
            st.settle()
            st.do(v.tensor_tensor(pos[:, 0:n], pos[:, 0:n], rk_all[:, 0:n], ALU.add))
            st.settle()
            if mix.cap:
                st.do(v.tensor_scalar(ok_all[:, 0:n], rk_all[:, 0:n], float(mix.cap), None, ALU.is_le))
                st.settle()
                st.do(v.scalar_tensor_tensor(out=pos[:, 0:n], in0=pos[:, 0:n], scalar=float(TRASH), in1=ok_all[:, 0:n],
                                             op0=ALU.subtract, op1=ALU.mult))
                st.settle()
                st.do(v.tensor_scalar(pos[:, 0:n], pos[:, 0:n], float(TRASH), None, ALU.add))
                st.settle()
            st.do(v.tensor_copy(idx_all[:, 0:n], pos[:, 0:n]))
            st.settle()

        def block_phase(tag, mix):
            chunks, C, U, NB, N = mix.chunks, mix.C, mix.U, mix.banks, mix.rows
            T, QUADS = N // P, mix.blocks // WS
            CR = 2 * C
            w_in = [signal(f"{tag}_w_in{q}") for q in range(WS)]
            x_in = [signal(f"{tag}_x_in{q}") for q in range(WS)]
            y_st = [signal(f"{tag}_y_st{s}") for s in range(2)]
            t_mm = signal(f"{tag}_t_mm")
            xt_done = signal(f"{tag}_xt")
            h_mm = signal(f"{tag}_h_mm")
            a_done = signal(f"{tag}_a_done")
            m_done = signal(f"{tag}_m_done")
            y_mm = signal(f"{tag}_y_mm")
            y_used = signal(f"{tag}_y_used")
            hid_done = m_done if mix.glu else a_done
            w = ins[f"w{mix.layer}"]
            aux8 = aux[:, :, :].rearrange("p a (h b) -> p (a h) b", h=2)

            def over_quads(eng, body):
                with eng.Fori(0, QUADS - 1) as i:
                    body(i, False)
                body(QUADS - 1, True)

            def at_block(i, q):
                return (i + 1, q - WS) if q >= WS else (i, q)

            with nc.Block() as block:
                @block.sync
                def _(sp):
                    def load(i, q):
                        n = i * WS + q
                        if mix.layer == 0:
                            e, r0 = i * (WS // 2) + q // 2, n * N
                        else:
                            e = sp.value_load(tab_e[0:1, bass.ds(n, 1)], min_val=0, max_val=NE - 1)
                            r0 = sp.value_load(tab_r[0:1, bass.ds(n, 1)], min_val=0, max_val=X_ROWS - N)
                        sp.dma_start(xin[:, q, 0:N].rearrange("p (t d) -> p t d", d=D),
                                     x_rows[bass.ds(r0, N), :].rearrange("(t p) d -> p t d", p=P)).then_inc(x_in[q], 16)
                        sp.dma_start(w_exp[:, q, 0:mix.width].unsqueeze(1),
                                     w[bass.ds(e, 1), :, :].rearrange("e p w -> p e w")).then_inc(w_in[q], 16)

                    for q in range(WS):
                        load(0, q)

                    def body(i, last):
                        for q in range(WS):
                            s, n = q % 2, i * WS + q
                            sp.wait_ge(y_used, n + 3)
                            sp.dma_start(y_rows[bass.ds(n * N, N), :].rearrange("(t p) d -> p t d", p=P),
                                         y_out[:, s, 0:N].rearrange("p (t d) -> p t d", d=D)).then_inc(y_st[s], 16)
                            if not last:
                                load(i + 1, q)
                    over_quads(sp, body)
                    for s in range(2):
                        sp.wait_ge(y_st[s], 16 * (QUADS * WS // 2 + 1))

                @block.tensor
                def _(pe):
                    pe.sem_inc(t_mm, 2)
                    pe.sem_inc(h_mm, 2 * U)
                    pe.sem_inc(y_mm, 2)

                    def turn(i, q):
                        i, q = at_block(i, q)
                        pe.wait_ge(x_in[q], i * 16 + 16)
                        pe.wait_ge(xt_done, i * WS + (q + 1))
                        for t in range(T):
                            r = nc.tensor.transpose(banks[:, 7, t * P:(t + 1) * P], xin[:, q, t * D:(t + 1) * D], ident)
                        r.then_inc(t_mm, 1)

                    def rise(i, q):
                        i, q = at_block(i, q)
                        n = i * WS + q
                        pe.wait_ge(xt_done, n + 2)
                        pe.wait_ge(w_in[q], i * 16 + 16)
                        for u in range(U):
                            c, part = u // mix.parts, u % mix.parts
                            at, wd = chunks[c]
                            at += part * mix.hidden
                            b = u - NB
                            if not mix.glu:
                                pe.wait_ge(a_done, n * C + (b + 1 + CR))
                            else:
                                pe.wait_ge(m_done if b % 2 else a_done, n * C + (b // 2 + 1 + CR))
                            nc.tensor.matmul(banks[0:wd, u % NB, 0:N], w_exp[:, q, at:at + wd], xT[:, q % 2, 0:N],
                                             start=True, stop=True).then_inc(h_mm, 1)

                    def fall(i, q):
                        s, n = q % 2, i * WS + q
                        pe.wait_ge(hid_done, n * C + (C + CR))
                        pe.wait_ge(y_used, n + 1)
                        for t in range(T):
                            for c, (_, wd) in enumerate(chunks):
                                at = mix.up + c * D
                                r = nc.tensor.matmul(banks[:, 5 + s, t * D:(t + 1) * D], hid[0:wd, s, c, t * P:(t + 1) * P],
                                                     w_exp[0:wd, q, at:at + D], start=(c == 0), stop=(c == C - 1))
                        r.then_inc(y_mm, 1)

                    turn(0, 0)
                    turn(0, 1)
                    rise(0, 0)

                    def body(i, last):
                        for q in range(WS):
                            if not last or q + 1 < WS:
                                rise(i, q + 1)
                            if not last or q + 2 < WS:
                                turn(i, q + 2)
                            fall(i, q)
                    over_quads(pe, body)

                @block.scalar
                def _(act):
                    act.sem_inc(a_done, CR)
                    with act.Fori(0, QUADS) as i:
                        for q in range(WS):
                            s, n = q % 2, i * WS + q
                            for c, (_, wd) in enumerate(chunks):
                                act.wait_ge(h_mm, n * U + (c * mix.parts + 1 + 2 * U))
                                src = banks[0:wd, (c * mix.parts) % NB, 0:N]
                                if mix.glu:
                                    act.wait_ge(m_done, n * C + (c + 1))
                                    nc.scalar.activation(aux8[0:wd, s * C + c, 0:N], src, mix.act_fn).then_inc(a_done, 1)
                                else:
                                    if c == 0:
                                        act.wait_ge(y_mm, n + 1)
                                    at = mix.up + mix.down + c
                                    bias = w_exp[:, q, at:at + 1] if mix.bias else zero1
                                    nc.scalar.activation(hid[0:wd, s, c, 0:N], src, mix.act_fn, bias=bias).then_inc(a_done, 1)

                @block.vector
                def _(dve):
                    dve.sem_inc(xt_done, 1)
                    dve.sem_inc(y_used, 2)
                    dve.sem_inc(m_done, CR)
                    for s in range(2):
                        dve.sem_inc(y_st[s], 16)

                    def keep_xT(i, q):
                        i, q = at_block(i, q)
                        n = i * WS + q
                        dve.wait_ge(t_mm, n + 3)
                        dve.wait_ge(h_mm, n * U + U)
                        nc.vector.tensor_copy(xT[:, q % 2, 0:N], banks[:, 7, 0:N]).then_inc(xt_done, 1)

                    def gate(i, q):
                        if not mix.glu:
                            return
                        i, q = at_block(i, q)
                        s, n = q % 2, i * WS + q
                        dve.wait_ge(y_mm, n + 1)
                        for c, (_, wd) in enumerate(chunks):
                            dve.wait_ge(a_done, n * C + (c + 1 + CR))
                            dve.wait_ge(h_mm, n * U + (2 * c + 2 + 2 * U))
                            nc.vector.tensor_tensor(hid[0:wd, s, c, 0:N], aux8[0:wd, s * C + c, 0:N],
                                                    banks[0:wd, (2 * c + 1) % NB, 0:N], ALU.mult).then_inc(m_done, 1)

                    def take(i, q):
                        s, n = q % 2, i * WS + q
                        dve.wait_ge(y_mm, n + 3)
                        dve.wait_ge(y_st[s], i * (WS // 2 * 16) + 16 * (q // 2 + 1))
                        yb = banks[:, 5 + s, 0:N]
                        if mix.bias:
                            at = mix.up + mix.down + C
                            r = nc.vector.tensor_tensor(y_out[:, s, 0:N].rearrange("p (t d) -> p t d", d=D),
                                                        yb.rearrange("p (t d) -> p t d", d=D),
                                                        w_exp[:, q, at:at + D].unsqueeze(1).to_broadcast([P, T, D]), ALU.add)
                        else:
                            r = nc.vector.tensor_copy(y_out[:, s, 0:N], yb)
                        r.then_inc(y_used, 1)

                    keep_xT(0, 0)
                    keep_xT(0, 1)
                    gate(0, 0)

                    def body(i, last):
                        for q in range(WS):
                            if not last or q + 1 < WS:
                                gate(i, q + 1)
                            if not last or q + 2 < WS:
                                keep_xT(i, q + 2)
                            take(i, q)
                    over_quads(dve, body)

        def end_phase(tag, comb_mix):
            comb = Combine(tag, comb_mix)
            base = dve_base[0]
            PER = STEPS[tag]
            with nc.Block() as block:
                @block.gpsimd
                def _(pool):
                    with pool.Fori(0, NG) as g:
                        comb.gather(pool, g)

                @block.vector
                def _(dve):
                    comb.start(dve)
                    with dve.Fori(0, NG) as g:
                        st = Steps(dve, dve_step, g * PER + base)
                        comb.add(dve, st, g)
                        assert st.n == PER, (tag, st.n)

                @block.sync
                def _(sp):
                    with sp.Fori(0, NG) as g:
                        sp.wait_ge(comb.added, g * TG + (TG + 1))
                        sp.dma_start(out[:, bass.ds(g * GT, GT)], x[:, bass.ds(g * GT, GT)]).then_inc(stored, 16)
                    sp.wait_ge(stored, 16 * NG)

        for phase, *args in ((heads_phase, "a0", False, None), (route_phase, "r0", MIX[0]), (block_phase, "b0", MIX[0]),
                             (plain_phase, "a1", MIX[0]), (route_phase, "r1", MIX[1]), (block_phase, "b1", MIX[1]),
                             (gelu_phase, "a2", MIX[1]), (route_phase, "r2", MIX[2]), (block_phase, "b2", MIX[2]),
                             (heads_phase, "a3", True, MIX[2]), (route_phase, "r3", MIX[3]), (block_phase, "b3", MIX[3]),
                             (end_phase, "end", MIX[3])):
            with nc.cleanup_on_exit():
                phase(*args)


def lay_out(inputs):
    import numpy as np

    def f32(name):
        return np.ascontiguousarray(inputs[name])

    a = {}
    xs, cs = f32("x"), f32("ctx_1024")
    a["x"] = xs.transpose(1, 0, 2).reshape(P, B * D)
    a["ctxT"] = cs.transpose(2, 0, 1).reshape(D, B * KV)
    a["ctxk"] = cs.transpose(1, 0, 2).reshape(KV, B * D)
    a["mask"] = f32("mask_1x1xSxS2_ik0").reshape(P, KV)
    const = np.zeros((P, C_N), np.float32)
    const[:, C_ID:C_ID + P] = np.eye(P)
    const[:, C_TRI:C_TRI + P] = np.triu(np.ones((P, P)))
    const[:, C_IOTA:C_IOTA + NE] = np.arange(NE)
    const[:, C_TRASH:] = Y_ROWS + P * np.arange(2 * B) + np.arange(P)[:, None]
    const[:, C_STEP:C_STEP + 16] = BLK * np.arange(16)
    const[:, C_BLK:C_BLK + NBLK] = np.arange(NBLK)
    a["const"] = const
    spread = np.zeros((D, 2, 2, HQ, P), np.float32)
    for side, parts in enumerate(((0, 1, 0, 1), (0, 0, 1, 1))):
        for t in range(HQ):
            for r in range(P):
                j, u, w = r // 32, r % 32 // HD, r % HD
                spread[HD * (HQ * t + j) + w, side, parts[u], t, r] = 1.0
    a["spread"] = spread.reshape(D, 16 * P)
    small = np.zeros((P, SMALL_N), np.float32)

    def put(name, v):
        o, w = SMALL[name]
        small[0:v.shape[0], o:o + w] = v
    put("bq3", f32("L3_xattn_bq")[:, None])
    put("bk3", f32("L3_xattn_bk")[:, None])
    put("bv3", np.broadcast_to(f32("L3_xattn_bv")[None], (P, D)))
    put("bo3", np.broadcast_to(f32("L3_xattn_bo")[None], (P, D)))
    put("bias0", np.broadcast_to(f32("L0_ffn_bias").reshape(1, D), (P, D)))
    put("ebias2", np.broadcast_to(f32("L2_ffn_expert_bias")[None], (P, NE)))
    put("rw0", f32("L0_ffn_router_w"))
    put("rw1", f32("L1_ffn_gate_w"))
    put("rw2", f32("L2_ffn_router_w").T)
    put("rw3", f32("L3_ffn_wg"))
    a["small"] = small
    a["aw"] = np.concatenate([f32(f"L{n[1]}_xattn_W{n[0]}").T for n in AW], axis=1)

    def packed(up, down, *more):
        e, h = down.shape[0], down.shape[1]
        c = -(-h // P)
        dn = np.zeros((e, c * P, D), np.float32)
        dn[:, :h] = down
        return np.concatenate([up, dn.reshape(e, c, P, D).transpose(0, 2, 1, 3).reshape(e, P, -1), *more], axis=2)

    def gated(names):
        return np.concatenate([f32(n).transpose(0, 2, 1) for n in names], axis=2)

    a["w0"] = packed(f32("L0_ffn_w1"), f32("L0_ffn_w2"))
    a["w1"] = packed(f32("L1_ffn_exp_wgu"), f32("L1_ffn_exp_wd"))
    a["w2"] = packed(gated(("L2_ffn_w1", "L2_ffn_w3")), f32("L2_ffn_w2").transpose(0, 2, 1))
    a["w3"] = packed(f32("L3_ffn_W1"), f32("L3_ffn_W2"), f32("L3_ffn_b1").reshape(NE, 4, P).transpose(0, 2, 1),
                     np.broadcast_to(f32("L3_ffn_b2")[:, None], (NE, P, D)))
    plain = [packed(f32("L1_ffn_base_wgu")[None], f32("L1_ffn_base_wd")[None]),
             packed(gated(("L2_ffn_sw1", "L2_ffn_sw3")), f32("L2_ffn_sw2").transpose(0, 2, 1))]
    a["plain"] = np.concatenate([w for p in plain for w in p], axis=1)
    return {k: np.ascontiguousarray(v) for k, v in a.items()}


def kernel(**inputs):
    import concourse.bacc as _bacc
    from concourse.bass_utils import run_bass_kernel_spmd as _run

    arrays = lay_out(inputs)
    nc = _bacc.Bacc("TRN2", target_bir_lowering=False, num_devices=1)
    ins = {k: nc.dram_tensor(f"in_{k}", v.shape, mybir.dt.from_np(v.dtype), kind="ExternalInput").ap()
           for k, v in arrays.items()}
    out = nc.dram_tensor("out_0", (P, B * D), F32, kind="ExternalOutput").ap()
    build(nc, ins, out)
    r = _run(nc, [{f"in_{k}": v for k, v in arrays.items()}], core_ids=[0])
    return r.results[0]["out_0"].reshape(P, B, D).transpose(1, 0, 2)
```

```python
from contextlib import ExitStack

import concourse.bass as bass
from concourse import mybir

F32 = mybir.dt.float32
F32R = mybir.dt.float32r
BF16 = mybir.dt.bfloat16
I32 = mybir.dt.int32
U32 = mybir.dt.uint32
ALU = mybir.AluOpType
ACT = mybir.ActivationFunctionType
AX = mybir.AxisListType

P = 128
B, D, KV = 32, 128, 77
KE = 78
TG = 4
NG = B // TG
GT = TG * P
GK = TG * KV
NH, HD = 16, 8
HQ = 32 // HD
NE = 8
EPS = 1e-5
MASKED = -1e30
CAP0 = B * P // NE
CAP3 = int(B * P / NE * 1.25) + 1

C_ID, C_TRI, C_IOTA, C_ZERO, C_STEP, C_BLK, C_TRASH = 0, 128, 256, 264, 265, 281, 321
C_LOW = C_TRASH + 2 * B
C_QUAD = C_LOW + 2
C_N = C_QUAD + HQ

BLK = 256
NBLK = 2 * B * P // BLK + NE
WS = 4
R_ALL = B * P + BLK
R_CAP3 = -(-CAP3 // BLK) * BLK
X_ROWS = NE * R_ALL
Y_ROWS = NBLK * BLK
TRASH = Y_ROWS - P
assert 2 * NE * CAP0 <= TRASH and NE * R_CAP3 <= TRASH and Y_ROWS + 2 * B * P <= X_ROWS
SMALL = {}
_at = 0
for _n, _w in (("bq3", HQ), ("bk3", HQ), ("bq3m", HQ), ("bk3m", HQ), ("bv3", D), ("bo3", D), ("bias0", D), ("ebias2", NE),
               ("rw0", NE), ("rw1", NE), ("rw2", NE), ("rw3", NE)):
    SMALL[_n] = (_at, _w)
    _at += _w
SMALL_N = _at

AW = {}
_at = 0
for _n in ("q0", "k0", "v0", "o0", "q3", "k3", "v3", "o3"):
    AW[_n] = _at
    _at += (HQ if _n[0] in "qk" else 1) * D
AW_N = _at


STEPS = {"a0": 8, "r0": 33, "a1": 17, "r1": 30, "a2": 13, "r2": 30, "a3": 29, "r3": 30, "end": 1}


class Steps:

    def __init__(self, eng, sem, base):
        self.eng, self.sem, self.base, self.n = eng, sem, base, 0

    def do(self, ins):
        ins.then_inc(self.sem, 1)
        self.n += 1

    def settle(self, apart=False):
        self.eng.wait_ge(self.sem, self.base + self.n)
        if apart:
            self.eng.nop(nofuse=True)


class Mixture:

    def __init__(self, layer, hidden, glu, plain, topk, cap, region, rows, blocks, renorm, act_fn):
        self.layer, self.hidden, self.glu, self.plain = layer, hidden, glu, plain
        self.topk, self.cap, self.region, self.rows, self.blocks = topk, cap, region, rows, blocks
        self.renorm, self.act_fn = renorm, act_fn
        self.chunks = [(at, min(P, hidden - at)) for at in range(0, hidden, P)]
        self.C = len(self.chunks)
        self.up = hidden * (2 if glu else 1)
        self.down = self.C * D
        self.parts = 2 if glu else 1
        self.U = self.C * self.parts
        self.banks = 3 if self.U % 4 else 4
        self.bias = layer == 3
        self.width = self.up + self.down + (self.C + D if self.bias else 0)


MIX = (Mixture(0, 512, False, 0, 2, CAP0, 2 * CAP0, 2 * BLK, 2 * NE * CAP0 // (2 * BLK), False, ACT.Gelu_apprx_tanh),
       Mixture(1, 352, True, 1, 2, 0, R_ALL, BLK, NBLK, True, ACT.Silu),
       Mixture(2, 256, True, 2, 2, 0, R_ALL, BLK, NBLK, True, ACT.Silu),
       Mixture(3, 512, False, 0, 1, CAP3, R_CAP3, BLK, NE * R_CAP3 // BLK, False, ACT.Gelu))
W_MAX = max(m.width for m in MIX)
PLAIN = [m.plain * (m.up + m.down) for m in MIX]


def build(nc, ins, out):
    ctx = ExitStack()
    with ctx:
        def sb(name, shape, dt=F32):
            return ctx.enter_context(nc.sbuf_tensor(name, shape, dt))

        def sem(name):
            return ctx.enter_context(nc.semaphore(name))

        def signal(name):
            return nc.alloc_semaphore(name)

        x = sb("x", [P, B * D])
        ctxT = sb("ctxT", [P, B * KV])
        ctxk = sb("ctxk", [KV, B * D])
        const = sb("const", [P, C_N])
        small = sb("small", [P, SMALL_N])
        aw = sb("aw", [P, AW_N])
        w_plain = sb("w_plain", [P, sum(PLAIN)])
        w_exp = sb("w_exp", [P, WS, W_MAX])
        z = sb("z", [P, GT])
        z_out = sb("z_out", [P, 2, GT])
        xT = sb("xT", [P, 2, 2 * BLK])
        y_out = sb("y_out", [P, 2, 2 * BLK])
        y_in = sb("y_in", [P, 2, 2 * TG, D])
        zT = sb("zT", [P, GT])
        bn = sb("bn", [P, TG, 6])
        mv = sb("mv", [P, TG, 2])
        ve = sb("ve", [P, TG])
        rstd = sb("rstd", [P, TG])
        mhalf = sb("mhalf", [P, TG])
        id_bf = sb("id_bf", [P, P], BF16)
        tri_bf = sb("tri_bf", [P, P], BF16)
        one_bf = sb("one_bf", [P, P], BF16)
        mask_i = sb("mask_i", [P, KV], I32)
        mask_b = sb("mask_b", [P, KE], BF16)
        mask_v = sb("mask_v", [P, KV])
        rowok = sb("rowok", [P, 1])
        hid = sb("hid", [P, 2, 4, GT])
        aux = sb("aux", [P, 4, GT])
        high = sb("high", [P, HQ, GT], F32R)
        xin = high[:, :, :].bitcast(F32)
        qR = sb("qR", [P, HQ, GT], F32R)
        kR = sb("kR", [P, HQ, TG, KE], F32R)
        kD = sb("kD", [P, HQ, TG, HQ, KE], F32R)
        vS = sb("vS", [P, TG, HQ, HQ, 32])
        ctxg = sb("ctxg", [P, GK])
        oneS = sb("oneS", [P, HQ, 32])
        oT = sb("oT", [P, 2, D])
        mx = sb("mx", [P, NH])
        rs = sb("rs", [P, P])
        tmp = sb("tmp", [P, D])
        pt = sb("pt", [P, 2, NH, P])
        lg = sb("lg", [P, TG, NE])
        ls_all = sb("ls_all", [P, B, NE])
        el_all = sb("el_all", [P, B, NE])
        den_all = sb("den_all", [P, B])
        rden_all = sb("rden_all", [P, B])
        mx8 = sb("mx8", [P, TG, 8])
        ix8 = sb("ix8", [P, TG, 8], U32)
        ixf = sb("ixf", [P, TG, 2])
        oh = sb("oh", [P, TG, 2, NE], BF16)
        ohc = sb("ohc", [P, TG, NE], BF16)
        rank = sb("rank", [P, TG, 2 * NE])
        picked = sb("picked", [P, TG, 2, NE])
        rk = sb("rk", [P, TG, 2])
        row = sb("row", [P, TG, 2])
        within = sb("within", [P, TG, 2])
        count = sb("count", [P, 2 * NE])
        den = sb("den", [P, TG])
        rden = sb("rden", [P, TG])
        idx_out = sb("idx_out", [P, 2, 2 * TG], U32)
        idx_in = sb("idx_in", [P, 2, 2 * TG], U32)
        wt_in = sb("wt_in", [P, 2 * TG])
        idx_all = sb("idx_all", [P, 2 * B], U32)
        wt_all = sb("wt_all", [P, 2 * B])
        rk_all = sb("rk_all", [P, 2 * B])
        ix_all = sb("ix_all", [P, 2 * B])
        pos = sb("pos", [P, 2 * B])
        ok_all = sb("ok_all", [P, 2 * B])
        nblk = sb("nblk", [P, 3, NE])
        first = sb("first", [P, NE])
        tab = sb("tab", [1, 3, NBLK])
        tab_e = sb("tab_e", [1, NBLK], I32)
        tab_r = sb("tab_r", [1, NBLK], I32)
        x_rows = nc.dram_tensor("x_rows", (X_ROWS, D), F32, kind="Internal").ap()
        y_rows = nc.dram_tensor("y_rows", (Y_ROWS, D), F32, kind="Internal").ap()
        banks = ctx.enter_context(nc.psum_tensor("banks", [P, 8, 512], F32))

        ident = const[:, C_ID:C_ID + P]
        iota8 = const[:, C_IOTA:C_IOTA + NE]
        zero1 = const[:, C_ZERO:C_ZERO + 1]

        def sm(name):
            a, w = SMALL[name]
            return small[:, a:a + w]

        def weight(name):
            return aw[:, AW[name]:AW[name] + D]

        def spread_weight(name, t):
            return aw[:, AW[name] + t * D:AW[name] + (t + 1) * D]

        def takes_low(side):
            c = C_LOW + "qk".index(side)
            return const[:, c:c + 1]

        loaded = sem("loaded")
        rest_loaded = sem("rest_loaded")
        zeros_ready = sem("zeros_ready")
        cleared = sem("cleared")
        var_ready = sem("var_ready")
        rstd_ready = sem("rstd_ready")
        z_ready = sem("z_ready")
        zt_ready = sem("zt_ready")
        zT_ready = sem("zT_ready")
        dve_step = sem("dve_step")
        pool_step = sem("pool_step")
        stored = sem("stored")

        def norm_stats(dve, st, at):
            dve.nop(nofuse=True)
            for i in range(TG):
                st.do(nc.vector.bn_stats(bn[:, i, :], x[:, bass.ds(at + i * D, D)]))
            st.settle(apart=True)
            for i in range(TG):
                st.do(nc.vector.bn_aggr(mv[:, i, :], bn[:, i, :]))
            st.settle()
            nc.vector.tensor_scalar(ve[:, :], mv[:, :, 1], EPS, None, ALU.add).then_inc(var_ready, 1)

        def norm_apply(dve, n, at, first=False):
            dve.wait_ge(rstd_ready, n)
            if not first:
                dve.wait_ge(zt_ready, n - 1)
            for i in range(TG):
                r = nc.vector.tensor_scalar(z[:, i * D:(i + 1) * D], x[:, bass.ds(at + i * D, D)],
                                            mv[:, i, 0:1], rstd[:, i:i + 1], ALU.subtract, ALU.mult)
            r.then_inc(z_ready, 1)

        def norm_power(pool, n):
            pool.wait_ge(var_ready, n)
            nc.gpsimd.tensor_tensor(rstd[:, :], ve[:, :], mhalf[:, :], ALU.pow).then_inc(rstd_ready, 1)

        def norm_transpose(pe, n, bank):
            pe.wait_ge(z_ready, n)
            for i in range(TG):
                r = nc.tensor.transpose(banks[:, bank, i * P:(i + 1) * P], z[:, i * D:(i + 1) * D], ident)
            r.then_inc(zt_ready, 1)

        def norm_store(act, n, bank):
            act.wait_ge(zt_ready, n)
            nc.scalar.copy(zT[:, :], banks[:, bank, :]).then_inc(zT_ready, 1)

        dve_base = [0]
        pool_base = [6 + HQ]
        norms = [1]
        clears = 16 * (-(-X_ROWS // 4096) - (-Y_ROWS // 4096))

        with nc.Block() as block:
            @block.sync
            def _(sp):
                sp.dma_start(x[:, 0:GT], ins["x"][:, 0:GT]).then_inc(loaded, 16)
                sp.dma_start(const[:], ins["const"]).then_inc(loaded, 16)
                sp.dma_start(aw[:], ins["aw"]).then_inc(loaded, 16)
                sp.dma_start(ctxT[:], ins["ctxT"]).then_inc(loaded, 16)
                sp.dma_start(mask_i[:], ins["mask"]).then_inc(loaded, 16)
                sp.dma_start(x[:, GT:], ins["x"][:, GT:]).then_inc(rest_loaded, 16)
                sp.dma_start(small[:], ins["small"]).then_inc(rest_loaded, 16)
                sp.dma_start(ctxk[:], ins["ctxk"]).then_inc(rest_loaded, 16)
                sp.dma_start(w_plain[:], ins["plain"]).then_inc(rest_loaded, 16)
                sp.wait_ge(zeros_ready, 1)
                zero_rows = hid[:, :, :, :].rearrange("p s a b -> p (s a b)")
                per_dma = 4096 // D * P
                for rows, total in ((x_rows, X_ROWS), (y_rows, Y_ROWS)):
                    for r0 in range(0, total, per_dma):
                        n = min(per_dma, total - r0)
                        sp.dma_start(rows[r0:r0 + n, :].rearrange("(p a) d -> p (a d)", p=P),
                                     zero_rows[:, 0:n // P * D]).then_inc(cleared, 16)
                sp.wait_ge(loaded, 16 * 5)

            @block.gpsimd
            def _(pool):
                nc.gpsimd.memset(hid[:], 0.0).then_inc(zeros_ready, 1)
                nc.gpsimd.memset(mhalf[:], -0.5).then_inc(pool_step, 1)
                nc.gpsimd.memset(one_bf[:], 1.0).then_inc(pool_step, 1)
                nc.gpsimd.memset(count[:], 0.0).then_inc(pool_step, 1)
                nc.gpsimd.memset(vS[:], 0.0).then_inc(pool_step, 1)
                nc.gpsimd.memset(oneS[:], 0.0).then_inc(pool_step, 1)
                nc.gpsimd.memset(pt[:], 0.0).then_inc(pool_step, 1)
                pool.wait_ge(pool_step, 6)
                for i in range(HQ):
                    nc.gpsimd.memset(oneS[:, i, HD * i:HD * i + HD], 1.0).then_inc(pool_step, 1)
                pool.wait_ge(pool_step, 6 + HQ)
                norm_power(pool, 1)

            @block.vector
            def _(dve):
                dve.wait_ge(loaded, 16 * 5)
                st = Steps(dve, dve_step, 0)
                norm_stats(dve, st, 0)
                st.do(nc.vector.tensor_copy(id_bf[:], const[:, C_ID:C_ID + P]))
                st.do(nc.vector.tensor_copy(tri_bf[:], const[:, C_TRI:C_TRI + P]))
                st.do(nc.vector.memset(mask_b[:, KV:KE], 0.0))
                st.do(nc.vector.tensor_scalar(mask_b[:, 0:KV], mask_i[:], 0.0, MASKED, ALU.is_equal, ALU.mult))
                st.do(nc.vector.tensor_copy(kR[:, :, :, KV:KE], const[:, C_ZERO:C_ZERO + 1].unsqueeze(1).unsqueeze(1)
                                            .to_broadcast([P, HQ, TG, 1])))
                st.do(nc.vector.tensor_scalar(mask_v[:], mask_i[:], 0.0, None, ALU.not_equal))
                st.settle()
                st.do(nc.vector.tensor_reduce(rowok[:], mask_v[:], AX.X, ALU.max))
                norm_apply(dve, 1, 0, first=True)
                st.settle()
                dve_base[0] = st.n

            @block.tensor
            def _(pe):
                pe.wait_ge(loaded, 16 * 5)
                norm_transpose(pe, 1, 7)

            @block.scalar
            def _(act):
                norm_store(act, 1, 7)

        class Combine:

            def __init__(self, tag, mix, depth=1):
                self.mix = mix
                if mix is not None:
                    self.K = mix.topk
                    self.ahead = (depth - 1) * TG + 1
                    self.landed = [[signal(f"{tag}_landed{s}{i}") for i in range(TG)] for s in range(depth)]
                    self.added = signal(f"{tag}_added")
                    self.idx = signal(f"{tag}_idx")

            def start(self, dve):
                if self.mix is not None:
                    dve.sem_inc(self.added, self.ahead)

            def gather(self, pool, g, slot, nth, tiles=(0, 1, 2, 3)):
                if self.mix is None:
                    return
                n = TG * self.K
                if 0 in tiles:
                    pool.wait_ge(self.added, g * TG + 1)
                    nc.gpsimd.tensor_copy(idx_in[:, slot, 0:n], idx_all[:, bass.ds(g * n, n)]).then_inc(self.idx, 1)
                    pool.wait_ge(self.idx, g + 1)
                    pool.nop(nofuse=True)
                for i in tiles:
                    for k in range(self.K):
                        c = i * self.K + k
                        pool.indirect_dma_start(y_in[:, slot, c, :], None, y_rows[:, :],
                                                bass.IndirectOffsetOnAxis(ap=idx_in[:, slot, c:c + 1], axis=0))\
                            .then_inc(self.landed[slot][i], 16)

            def add(self, dve, st, g, slot, nth, choices=(0, 1)):
                if self.mix is None:
                    return
                K = self.K
                n = TG * K
                if 0 in choices:
                    st.do(nc.vector.tensor_copy(wt_in[:, 0:n], wt_all[:, bass.ds(g * n, n)]))
                    st.settle()
                for k in [k for k in choices if k < K]:
                    for i in range(TG):
                        at = bass.ds(g * GT + i * D, D)
                        if k == 0:
                            dve.wait_ge(self.landed[slot][i], nth * (16 * K) + 16 * K)
                        r = nc.vector.scalar_tensor_tensor(out=x[:, at], in0=y_in[:, slot, i * K + k, :],
                                                           scalar=wt_in[:, i * K + k:i * K + k + 1], in1=x[:, at],
                                                           op0=ALU.mult, op1=ALU.add)
                        if k == K - 1:
                            r.then_inc(self.added, 1)
                        else:
                            st.do(r)
                    if k < K - 1:
                        st.settle()
                if K - 1 in choices:
                    dve.wait_ge(self.added, g * TG + (TG + self.ahead))

            def first_norm(self, dve, st):
                if self.mix is not None:
                    self.add(dve, st, 0, 0, 0)
                    if self.mix.layer == 0:
                        add_bias0(st, 0)
                    norm_stats(dve, st, 0)

        def add_bias0(st, g):
            at = bass.ds(g * GT, GT)
            xv = x[:, at].rearrange("p (i d) -> p i d", d=D)
            st.do(nc.vector.tensor_tensor(xv, xv, sm("bias0").unsqueeze(1).to_broadcast([P, TG, D]), ALU.add))
            st.settle()

        def over_groups(eng, body):
            with eng.Fori(0, NG - 1) as g:
                body(g, False)
            body(NG - 1, True)

        def over_pairs(eng, body):
            with eng.Fori(0, NG // 2 - 1) as i:
                for half in range(2):
                    body(i * 2 + half, False, half, i)
            for half in range(2):
                body(NG - 2 + half, half == 1, half, NG // 2 - 1)

        def over_slots(eng, body):
            body(0, False, 0, 0)
            with eng.Fori(0, NG // 2 - 1) as i:
                body(i * 2 + 1, False, 1, i)
                body(i * 2 + 2, False, 0, i + 1)
            body(NG - 1, True, 1, NG // 2 - 1)

        def next_add(dve, st, comb, g, last, half, pair, choice):
            if not last:
                comb.add(dve, st, g + 1, 1 - half, pair + half, (choice,))
                if choice == 1 and comb.mix.layer == 0:
                    add_bias0(st, g + 1)

        def next_rows(g, last):
            return 0 if last else (g + 1) * GT

        def heads_phase(tag, softmax, comb_mix):
            k_mm, q_mm, v_mm = signal(f"{tag}_k_mm"), signal(f"{tag}_q_mm"), signal(f"{tag}_v_mm")
            hi_done = signal(f"{tag}_hi")
            split_done = signal(f"{tag}_split")
            v_done = signal(f"{tag}_v_done")
            kd_done = signal(f"{tag}_kd")
            ctx_ready = signal(f"{tag}_ctx")
            s_mm = signal(f"{tag}_s_mm")
            s_free = signal(f"{tag}_s_free")
            p_done = signal(f"{tag}_p_done")
            pt_mm = signal(f"{tag}_pt_mm")
            pt_done = signal(f"{tag}_pt_done")
            o_mm = signal(f"{tag}_o_mm")
            oT_done = signal(f"{tag}_oT")
            out_mm = signal(f"{tag}_out_mm")
            x_added = signal(f"{tag}_x_added")
            layer = "3" if softmax else "0"
            wv, wo = weight("v" + layer), weight("o" + layer)
            scale = float(HD) ** -0.5
            comb = Combine(tag, comb_mix)
            LN0 = norms[0] - (0 if comb_mix is not None else 1)
            norms[0] = LN0 + 1 + NG
            cen = aux[:, :, :].rearrange("p a b -> p (a b)")[:, 0:NH * KV].rearrange("p (h k) -> p h k", k=KV)
            prob = hid[:, :, :, :].rearrange("p s a b -> p s (a b)")[:, :, 0:NH * KV]\
                .rearrange("p s (h k) -> p s h k", k=KV)
            base = dve_base[0]
            PER = STEPS[tag]
            ORDER = (3, 2, 1, 0)
            VB = 7

            def k_bank(n):
                return 7 if softmax else 6 + n % 2

            def o_bank(b):
                return 6 if softmax else 4 + b % 2

            def slot_of(t, j):
                return HQ * t + j if softmax else HQ * j + t

            def bias_of(side, t, masked):
                return sm(f"b{side}3{'m' if masked else ''}")[:, t:t + 1] if softmax else zero1

            with nc.Block() as block:
                @block.gpsimd
                def _(pool):
                    def spread_heads(g):
                        for n in range(4):
                            t = ORDER[n]
                            pool.wait_ge(split_done, g * 8 + (n + 1))
                            nc.gpsimd.tensor_tensor(kD[:, t], kR[:, t].bitcast(F32).unsqueeze(2).to_broadcast([P, TG, HQ, KE]),
                                                    const[:, C_QUAD:C_QUAD + HQ].unsqueeze(1).unsqueeze(3)
                                                    .to_broadcast([P, TG, HQ, KE]), ALU.mult).then_inc(kd_done, 1)

                    nc.gpsimd.tensor_copy(ctxg[:, :], ctxT[:, 0:GK]).then_inc(ctx_ready, 1)
                    if comb_mix is not None:
                        comb.gather(pool, 0, 0, 0)
                        norm_power(pool, LN0 + 1)
                    if softmax:
                        spread_heads(0)

                    def body(g, last):
                        if not last:
                            pool.wait_ge(v_mm, g + 1)
                            nc.gpsimd.tensor_copy(ctxg[:, :], ctxT[:, bass.ds(g * GK + GK, GK)]).then_inc(ctx_ready, 1)
                            comb.gather(pool, g + 1, 0, g + 1)
                        norm_power(pool, g + (LN0 + 2))
                        if softmax and not last:
                            spread_heads(g + 1)
                    over_groups(pool, body)

                @block.tensor
                def _(pe):
                    pe.sem_inc(o_mm, 2)
                    pe.sem_inc(out_mm, 2)
                    if softmax:
                        pe.sem_inc(pt_mm, 8)

                    def k_tile(g, n):
                        if n >= 1 and (softmax or n >= 2):
                            pe.wait_ge(split_done, g * 8 + (n if softmax else n - 1))
                        nc.tensor.matmul(banks[:, k_bank(n), 0:GK], spread_weight("k" + layer, ORDER[n]),
                                         ctxT[:, bass.ds(g * GK, GK)], start=True, stop=True).then_inc(k_mm, 1)

                    def rows_transpose(g):
                        pe.wait_ge(split_done, g * 8 + 4)
                        norm_transpose(pe, g + (LN0 + 1), VB)

                    def q_tile(g, n):
                        t = ORDER[n]
                        pe.wait_ge(s_free, g * 8 + (t // 2 + 1))
                        pe.wait_ge(zT_ready, g + (LN0 + 1))
                        nc.tensor.matmul(banks[:, t, :], spread_weight("q" + layer, t), zT[:, :],
                                         start=True, stop=True).then_inc(q_mm, 1)

                    def make_values(g):
                        pe.wait_ge(ctx_ready, g + 1)
                        for b in range(TG):
                            r = nc.tensor.matmul(banks[0:KV, VB, b * P:(b + 1) * P], ctxg[:, b * KV:(b + 1) * KV], wv,
                                                 start=True, stop=True)
                        r.then_inc(v_mm, 1)

                    def scores(g, b):
                        for half in range(2):
                            pe.wait_ge(s_free, g * 8 + (2 * b + half + 1))
                            if b == 0 and half == 0:
                                pe.wait_ge(split_done, g * 8 + 8)
                                if softmax:
                                    pe.wait_ge(kd_done, g * 4 + 4)
                            for bank in (2 * half, 2 * half + 1):
                                if softmax:
                                    nc.tensor.matmul(banks[:, bank, 0:HQ * KE], id_bf[:, :],
                                                     mask_b[:, :].unsqueeze(1).to_broadcast([P, HQ, KE]),
                                                     start=True, stop=False)
                                    r = nc.tensor.matmul(banks[:, bank, 0:HQ * KE], qR[:, bank, b * P:(b + 1) * P],
                                                         kD[:, bank, b, :, :].rearrange("p j k -> p (j k)"),
                                                         start=False, stop=True)
                                    continue
                                rows = slice(32 * bank, 32 * bank + 32)
                                for t in range(HQ):
                                    r = nc.tensor.matmul(banks[0:KV, bank, t * P:(t + 1) * P], kR[rows, t, b, 0:KV],
                                                         qR[rows, t, b * P:(b + 1) * P], start=True, stop=True)
                            r.then_inc(s_mm, 1)

                    def turn_probs(g, b, half):
                        pe.wait_ge(p_done, g * 8 + (2 * b + half + 1))
                        for quad in (2 * half, 2 * half + 1):
                            pe.wait_ge(pt_done, g * 16 + (4 * b + quad + 1))
                            for n in range(4):
                                r = nc.tensor.transpose(banks[0:KV, 4 + quad % 2, n * P:(n + 1) * P],
                                                        prob[:, b % 2, 4 * quad + n, :], ident)
                            r.then_inc(pt_mm, 1)

                    def values(g, b):
                        if softmax:
                            pe.wait_ge(x_added, g * 4 + (b + 2))
                        else:
                            pe.wait_ge(s_free, g * 8 + (2 * b + 4))
                            pe.wait_ge(x_added, g * 4 + (b + 1))
                        if b == 0:
                            pe.wait_ge(v_done, g + 1)
                        for t in range(HQ):
                            if softmax:
                                pe.wait_ge(pt_done, g * 16 + (4 * b + t + 3))
                            for j in range(HQ):
                                r = nc.tensor.matmul(banks[32 * t:32 * t + 32, o_bank(b), 0:P], vS[:, b, t, j, :],
                                                     pt[:, b % 2, slot_of(t, j), :], start=(j == 0), stop=(j == HQ - 1))
                            for j in range(HQ if softmax else 0):
                                r = nc.tensor.matmul(banks[32 * t:32 * t + 32, o_bank(b), P:2 * P], oneS[:, j, :],
                                                     pt[:, b % 2, slot_of(t, j), :], start=(j == 0), stop=(j == HQ - 1))
                        r.then_inc(o_mm, 1)

                    def project(g, b):
                        pe.wait_ge(oT_done, g * 4 + (b + 3))
                        nc.tensor.matmul(banks[:, o_bank(b), 2 * P:3 * P], oT[:, b % 2, :], wo,
                                         start=True, stop=True).then_inc(out_mm, 1)

                    for n in range(4):
                        k_tile(0, n)
                    if comb_mix is not None:
                        rows_transpose(0)
                    for n in range(4):
                        q_tile(0, n)
                    if comb_mix is None:
                        pe.wait_ge(split_done, 4)
                    make_values(0)
                    scores(0, 0)

                    def body(g, last):
                        for b in range(TG - 1):
                            ahead = b == TG - 2 and not last
                            scores(g, b + 1)
                            if ahead:
                                k_tile(g + 1, 0)
                                if not softmax:
                                    k_tile(g + 1, 1)
                            if softmax:
                                if b >= 1:
                                    project(g, b - 1)
                                turn_probs(g, b, 0)
                                if ahead:
                                    k_tile(g + 1, 1)
                                turn_probs(g, b, 1)
                                if ahead:
                                    k_tile(g + 1, 2)
                            values(g, b)
                            if not softmax:
                                if b >= 1:
                                    project(g, b - 1)
                                if ahead:
                                    k_tile(g + 1, 2)
                                    k_tile(g + 1, 3)
                        b = TG - 1
                        if softmax:
                            if not last:
                                k_tile(g + 1, 3)
                            project(g, b - 1)
                            turn_probs(g, b, 0)
                            if last:
                                norm_transpose(pe, g + (LN0 + 2), VB)
                            else:
                                rows_transpose(g + 1)
                            turn_probs(g, b, 1)
                            if not last:
                                q_tile(g + 1, 0)
                                q_tile(g + 1, 1)
                            values(g, b)
                        else:
                            if last:
                                norm_transpose(pe, g + (LN0 + 2), VB)
                            else:
                                rows_transpose(g + 1)
                            values(g, b)
                            project(g, b - 1)
                            if not last:
                                q_tile(g + 1, 0)
                                q_tile(g + 1, 1)
                        if not last:
                            q_tile(g + 1, 2)
                            q_tile(g + 1, 3)
                        project(g, b)
                        if not last:
                            make_values(g + 1)
                            scores(g + 1, 0)
                    over_groups(pe, body)

                @block.scalar
                def _(act):
                    if softmax:
                        act.sem_inc(pt_done, 2)
                    else:
                        act.sem_inc(oT_done, 2)
                        act.sem_inc(s_free, 2)

                    def high_parts(g, side, n):
                        t = ORDER[n]
                        if side == "k":
                            bank, width = k_bank(n), GK
                            act.wait_ge(k_mm, g * 4 + (n + 1))
                        else:
                            bank, width = t, GT
                            act.wait_ge(q_mm, g * 4 + (n + 1))
                            act.wait_ge(split_done, g * 8 + (n + 1))
                        nc.scalar.activation(high[:, n, 0:width], banks[:, bank, 0:width], ACT.Identity,
                                             bias=bias_of(side, t, True), scale=takes_low(side)).then_inc(hi_done, 1)

                    def weigh(g, b, half):
                        if softmax:
                            act.wait_ge(s_free, g * 8 + (2 * b + half + 3))
                            if half == 0:
                                act.wait_ge(pt_mm, g * 16 + (4 * b + 4))
                            nc.scalar.activation(prob[:, b % 2, 8 * half:8 * half + 8, :], cen[:, 8 * half:8 * half + 8, :],
                                                 ACT.Exp, scale=scale).then_inc(p_done, 1)
                        else:
                            act.wait_ge(s_mm, g * 8 + (2 * b + half + 1))
                            if half == 0:
                                act.wait_ge(o_mm, g * 4 + (b + 1))
                            nc.scalar.activation(pt[0:KV, b % 2, 8 * half:8 * half + 8, :].rearrange("p h k -> p (h k)"),
                                                 banks[0:KV, 2 * half:2 * half + 2, :].rearrange("p h k -> p (h k)"),
                                                 ACT.Sigmoid, scale=scale).then_inc(s_free, 1)

                    def probs_copy(g, b, half):
                        if half == 0:
                            act.wait_ge(o_mm, g * 4 + (b + 1))
                        for quad in (2 * half, 2 * half + 1):
                            act.wait_ge(pt_mm, g * 16 + (4 * b + quad + 9))
                            nc.scalar.copy(pt[0:KV, b % 2, 4 * quad:4 * quad + 4, :].rearrange("p h k -> p (h k)"),
                                           banks[0:KV, 4 + quad % 2, :]).then_inc(pt_done, 1)

                    def keep_outputs(g, b):
                        act.wait_ge(out_mm, g * 4 + (b + 1))
                        act.wait_ge(o_mm, g * 4 + (b + 3))
                        nc.scalar.copy(oT[:, b % 2, :], banks[:, o_bank(b), 0:P]).then_inc(oT_done, 1)

                    for n in range(4):
                        high_parts(0, "k", n)
                    if comb_mix is not None:
                        norm_store(act, LN0 + 1, VB)
                    for n in range(4):
                        high_parts(0, "q", n)
                    weigh(0, 0, 0)
                    weigh(0, 0, 1)

                    def body(g, last):
                        for b in range(TG - 1):
                            ahead = b == TG - 2 and not last
                            if softmax:
                                if ahead:
                                    high_parts(g + 1, "k", 0)
                                probs_copy(g, b, 0)
                                weigh(g, b + 1, 0)
                                if ahead:
                                    high_parts(g + 1, "k", 1)
                                probs_copy(g, b, 1)
                                weigh(g, b + 1, 1)
                            else:
                                weigh(g, b + 1, 0)
                                if ahead:
                                    high_parts(g + 1, "k", 0)
                                    high_parts(g + 1, "k", 1)
                                weigh(g, b + 1, 1)
                                keep_outputs(g, b)
                            if ahead:
                                high_parts(g + 1, "k", 2)
                                high_parts(g + 1, "k", 3)
                        b = TG - 1
                        if softmax:
                            probs_copy(g, b, 0)
                        norm_store(act, g + (LN0 + 2), VB)
                        if softmax:
                            probs_copy(g, b, 1)
                        else:
                            keep_outputs(g, b)
                        if not last:
                            for n in range(4):
                                high_parts(g + 1, "q", n)
                            weigh(g + 1, 0, 0)
                            weigh(g + 1, 0, 1)
                    over_groups(act, body)

                @block.vector
                def _(dve):
                    dve.sem_inc(x_added, 2)
                    if softmax:
                        dve.sem_inc(oT_done, 2)
                        dve.sem_inc(s_free, 2)

                    def split_tile(g, side, n):
                        t = ORDER[n]
                        dve.wait_ge(hi_done, g * 8 + (n + 1 + (4 if side == "q" else 0)))
                        if side == "k":
                            dst, src, h = kR[:, t, :, 0:KV], banks[:, k_bank(n), 0:GK], high[:, n, 0:GK].bitcast(F32)
                            src, h = (a.rearrange("p (b k) -> p b k", k=KV) for a in (src, h))
                        else:
                            dst, src, h = qR[:, t, :], banks[:, t, :], high[:, n, :].bitcast(F32)
                        nc.vector.scalar_tensor_tensor(out=dst, in0=src, scalar=bias_of(side, t, False), in1=h,
                                                       op0=ALU.add, op1=ALU.subtract).then_inc(split_done, 1)

                    def keep_values(g):
                        dve.wait_ge(v_mm, g + 1)
                        vin = banks[0:KV, VB, :].rearrange("p (b c i w) -> p b c i w", b=TG, c=HQ, w=HD)
                        bv = sm("bv3")[0:KV, :].rearrange("p (c i w) -> p c i w", c=HQ, w=HD)
                        for i in range(HQ):
                            dst = vS[0:KV, :, :, i, HD * i:HD * i + HD]
                            if softmax:
                                r = nc.vector.tensor_tensor(dst, vin[:, :, :, i, :], bv[:, :, i, :].unsqueeze(1)
                                                            .to_broadcast([KV, TG, HQ, HD]), ALU.add)
                            else:
                                r = nc.vector.tensor_copy(dst, vin[:, :, :, i, :])
                        r.then_inc(v_done, 1)

                    def centre(st, g, b, half):
                        s = banks[:, 2 * half:2 * half + 2, 0:HQ * KE].rearrange("p q (j k) -> p q j k", k=KE)[:, :, :, 0:KV]
                        m = mx[:, 8 * half:8 * half + 8].rearrange("p (q j) -> p q j", j=HQ)
                        dve.wait_ge(s_mm, g * 8 + (2 * b + half + 1))
                        st.do(nc.vector.tensor_reduce(m, s, AX.X, ALU.max))
                        st.settle()
                        if b > 0:
                            dve.wait_ge(p_done, g * 8 + (2 * b + half - 1))
                        nc.vector.tensor_tensor(cen[:, 8 * half:8 * half + 8, :].rearrange("p (q j) k -> p q j k", j=HQ),
                                                s, m.unsqueeze(3).to_broadcast([P, 2, HQ, KV]),
                                                ALU.subtract).then_inc(s_free, 1)

                    def normalise(st, g, b):
                        dve.wait_ge(o_mm, g * 4 + (b + 3))
                        st.do(nc.vector.reciprocal(rs[:, :], banks[:, o_bank(b), P:2 * P]))
                        st.settle()
                        dve.wait_ge(out_mm, g * 4 + (b + 1))
                        nc.vector.tensor_tensor(oT[:, b % 2, :], banks[:, o_bank(b), 0:P], rs[:, :],
                                                ALU.mult).then_inc(oT_done, 1)

                    def add(st, g, b):
                        at = bass.ds(g * GT + b * P, P)
                        y = banks[:, o_bank(b), 2 * P:3 * P]
                        dve.wait_ge(out_mm, g * 4 + (b + 3))
                        if softmax:
                            st.do(nc.vector.scalar_tensor_tensor(out=tmp[:, :], in0=y, scalar=rowok[:, 0:1], in1=sm("bo3"),
                                                                 op0=ALU.mult, op1=ALU.add))
                            st.settle()
                            y = tmp[:, :]
                        nc.vector.tensor_tensor(x[:, at], x[:, at], y, ALU.add).then_inc(x_added, 1)

                    comb.start(dve)
                    pre = Steps(dve, dve_step, base)
                    for n in range(4):
                        split_tile(0, "k", n)
                    if comb_mix is not None:
                        comb.first_norm(dve, pre)
                        norm_apply(dve, LN0 + 1, 0)
                    for n in range(4):
                        split_tile(0, "q", n)
                    keep_values(0)
                    if comb_mix is None:
                        dve.wait_ge(rest_loaded, 16 * 4)
                    if softmax:
                        centre(pre, 0, 0, 0)
                        centre(pre, 0, 0, 1)

                    def body(g, last):
                        st = Steps(dve, dve_step, g * PER + (base + pre.n))
                        nxt = 0 if last else (g + 1) * GT
                        for b in range(TG - 1):
                            ahead = b == TG - 2 and not last
                            if softmax:
                                if b >= 1:
                                    normalise(st, g, b - 1)
                                centre(st, g, b + 1, 0)
                            if ahead:
                                split_tile(g + 1, "k", 0)
                            if softmax:
                                centre(st, g, b + 1, 1)
                            if ahead:
                                split_tile(g + 1, "k", 1)
                            if b >= 1:
                                add(st, g, b - 1)
                            if b < 2 and not last:
                                comb.add(dve, st, g + 1, 0, g + 1, (b,))
                            if b == 2:
                                norm_stats(dve, st, nxt)
                            if ahead:
                                split_tile(g + 1, "k", 2)
                                if not softmax:
                                    split_tile(g + 1, "k", 3)
                        b = TG - 1
                        if softmax:
                            normalise(st, g, b - 1)
                        norm_apply(dve, g + (LN0 + 2), nxt)
                        if softmax and not last:
                            split_tile(g + 1, "k", 3)
                        add(st, g, b - 1)
                        if not last:
                            split_tile(g + 1, "q", 0)
                            split_tile(g + 1, "q", 1)
                        if softmax:
                            normalise(st, g, b)
                        if not last:
                            split_tile(g + 1, "q", 2)
                            split_tile(g + 1, "q", 3)
                        add(st, g, b)
                        if not last:
                            dve.wait_ge(o_mm, g * 4 + 6)
                            keep_values(g + 1)
                            if softmax:
                                centre(st, g + 1, 0, 0)
                                centre(st, g + 1, 0, 1)
                        assert last or st.n == PER, (tag, st.n)
                        dve_base[0] = base + pre.n + (NG - 1) * PER + st.n
                    over_groups(dve, body)

        def plain_phase(tag, comb_mix):
            e_mm, cen_done, p_done = signal(f"{tag}_e_mm"), signal(f"{tag}_cen"), signal(f"{tag}_p")
            pt_mm, pt_done, out_mm = signal(f"{tag}_pt_mm"), signal(f"{tag}_pt"), signal(f"{tag}_out_mm")
            x_added = signal(f"{tag}_x")
            comb = Combine(tag, comb_mix, depth=2)
            LN0 = norms[0]
            norms[0] = LN0 + 1 + NG
            base = dve_base[0]
            cen = aux[:, 0, 0:GK].rearrange("p (b k) -> p b k", k=KV)
            prob = aux[:, 1, 0:GK].rearrange("p (b k) -> p b k", k=KV)
            pT = aux[0:KV, 2, :]

            with nc.Block() as block:
                @block.gpsimd
                def _(pool):
                    comb.gather(pool, 0, 0, 0)
                    comb.gather(pool, 1, 1, 0, (0, 1))
                    norm_power(pool, LN0 + 1)
                    comb.gather(pool, 1, 1, 0, (2, 3))

                    def body(g, last, half, pair):
                        if not isinstance(g, int):
                            comb.gather(pool, g + 2, half, pair + 1, (0, 1))
                        norm_power(pool, g + (LN0 + 2))
                        if not isinstance(g, int):
                            comb.gather(pool, g + 2, half, pair + 1, (2, 3))
                    over_pairs(pool, body)

                @block.tensor
                def _(pe):
                    norm_transpose(pe, LN0 + 1, 3)
                    with pe.Fori(0, NG) as g:
                        pe.wait_ge(zT_ready, g + (LN0 + 1))
                        for b in range(TG):
                            r = nc.tensor.matmul(banks[:, 0, b * KV:(b + 1) * KV], zT[:, b * P:(b + 1) * P],
                                                 ctxT[:, bass.ds(g * GK + b * KV, KV)], start=True, stop=True)
                        r.then_inc(e_mm, 1)
                        pe.wait_ge(p_done, g + 1)
                        for b in range(TG):
                            r = nc.tensor.transpose(banks[0:KV, 1, b * P:(b + 1) * P], prob[:, b, :], ident)
                        r.then_inc(pt_mm, 1)
                        norm_transpose(pe, g + (LN0 + 2), 3)
                        pe.wait_ge(pt_done, g + 1)
                        pe.wait_ge(x_added, g + 1)
                        for b in range(TG):
                            r = nc.tensor.matmul(banks[:, 2, b * P:(b + 1) * P], pT[:, b * P:(b + 1) * P],
                                                 ctxk[:, bass.ds(g * GT + b * D, D)], start=True, stop=True)
                        r.then_inc(out_mm, 1)

                @block.scalar
                def _(act):
                    norm_store(act, LN0 + 1, 3)
                    with act.Fori(0, NG) as g:
                        act.wait_ge(cen_done, g + 1)
                        nc.scalar.activation(prob, cen, ACT.Exp).then_inc(p_done, 1)
                        act.wait_ge(pt_mm, g + 1)
                        nc.scalar.copy(pT, banks[0:KV, 1, :]).then_inc(pt_done, 1)
                        norm_store(act, g + (LN0 + 2), 3)

                @block.vector
                def _(dve):
                    dve.sem_inc(x_added, 1)
                    comb.start(dve)
                    pre = Steps(dve, dve_step, base)
                    comb.first_norm(dve, pre)
                    norm_apply(dve, LN0 + 1, 0)
                    PER = STEPS[tag]

                    def body(g, last, half, pair):
                        st = Steps(dve, dve_step, g * PER + (base + pre.n))
                        s = banks[:, 0, 0:GK].rearrange("p (b k) -> p b k", k=KV)
                        next_add(dve, st, comb, g, last, half, pair, 0)
                        dve.wait_ge(e_mm, g + 1)
                        st.do(nc.vector.tensor_reduce(mx[:, 0:TG], s, AX.X, ALU.max))
                        st.settle()
                        nc.vector.tensor_tensor(cen, s, mx[:, 0:TG].unsqueeze(2).to_broadcast([P, TG, KV]),
                                                ALU.subtract).then_inc(cen_done, 1)
                        next_add(dve, st, comb, g, last, half, pair, 1)
                        norm_stats(dve, st, next_rows(g, last))
                        dve.wait_ge(p_done, g + 1)
                        st.do(nc.vector.tensor_reduce(den[:, :], prob, AX.X, ALU.add))
                        norm_apply(dve, g + (LN0 + 2), next_rows(g, last))
                        st.settle()
                        st.do(nc.vector.reciprocal(rden[:, :], den[:, :]))
                        st.settle()
                        dve.wait_ge(out_mm, g + 1)
                        for b in range(TG):
                            at = bass.ds(g * GT + b * P, P)
                            r = nc.vector.scalar_tensor_tensor(out=x[:, at], in0=banks[:, 2, b * P:(b + 1) * P],
                                                               scalar=rden[:, b:b + 1], in1=x[:, at],
                                                               op0=ALU.mult, op1=ALU.add)
                        r.then_inc(x_added, 1)
                        assert last or st.n == PER, (tag, st.n)
                        dve_base[0] = base + pre.n + (NG - 1) * PER + st.n
                    over_pairs(dve, body)

        def gelu_phase(tag, comb_mix):
            ctx_ready, h_mm, g_done = signal(f"{tag}_ctx"), signal(f"{tag}_h_mm"), signal(f"{tag}_g")
            out_mm, x_added = signal(f"{tag}_out_mm"), signal(f"{tag}_x")
            comb = Combine(tag, comb_mix, depth=2)
            LN0 = norms[0]
            norms[0] = LN0 + 1 + NG
            base = dve_base[0]
            gT = aux[0:KV, 0, :]

            with nc.Block() as block:
                @block.gpsimd
                def _(pool):
                    comb.gather(pool, 0, 0, 0)
                    comb.gather(pool, 1, 1, 0, (0, 1))
                    norm_power(pool, LN0 + 1)
                    comb.gather(pool, 1, 1, 0, (2, 3))

                    def body(g, last, half, pair):
                        pool.wait_ge(h_mm, g + 1)
                        nc.gpsimd.tensor_copy(ctxg[:, :], ctxT[:, bass.ds(g * GK, GK)]).then_inc(ctx_ready, 1)
                        if not isinstance(g, int):
                            comb.gather(pool, g + 2, half, pair + 1, (0, 1))
                        norm_power(pool, g + (LN0 + 2))
                        if not isinstance(g, int):
                            comb.gather(pool, g + 2, half, pair + 1, (2, 3))
                    over_pairs(pool, body)

                @block.tensor
                def _(pe):
                    pe.sem_inc(h_mm, 1)
                    norm_transpose(pe, LN0 + 1, 3)
                    with pe.Fori(0, NG) as g:
                        pe.wait_ge(zT_ready, g + (LN0 + 1))
                        pe.wait_ge(ctx_ready, g + 1)
                        for b in range(TG):
                            r = nc.tensor.matmul(banks[0:KV, 0, b * P:(b + 1) * P], ctxg[:, b * KV:(b + 1) * KV],
                                                 zT[:, b * P:(b + 1) * P], start=True, stop=True)
                        r.then_inc(h_mm, 1)
                        norm_transpose(pe, g + (LN0 + 2), 3)
                        pe.wait_ge(g_done, g + 1)
                        pe.wait_ge(x_added, g + 1)
                        for b in range(TG):
                            r = nc.tensor.matmul(banks[:, 2, b * P:(b + 1) * P], gT[:, b * P:(b + 1) * P],
                                                 ctxk[:, bass.ds(g * GT + b * D, D)], start=True, stop=True)
                        r.then_inc(out_mm, 1)

                @block.scalar
                def _(act):
                    norm_store(act, LN0 + 1, 3)
                    with act.Fori(0, NG) as g:
                        act.wait_ge(h_mm, g + 2)
                        nc.scalar.activation(gT, banks[0:KV, 0, :], ACT.Gelu_apprx_tanh).then_inc(g_done, 1)
                        norm_store(act, g + (LN0 + 2), 3)

                @block.vector
                def _(dve):
                    dve.sem_inc(x_added, 1)
                    comb.start(dve)
                    pre = Steps(dve, dve_step, base)
                    comb.first_norm(dve, pre)
                    norm_apply(dve, LN0 + 1, 0)
                    PER = STEPS[tag]

                    def body(g, last, half, pair):
                        st = Steps(dve, dve_step, g * PER + (base + pre.n))
                        for choice in range(2):
                            next_add(dve, st, comb, g, last, half, pair, choice)
                        norm_stats(dve, st, next_rows(g, last))
                        norm_apply(dve, g + (LN0 + 2), next_rows(g, last))
                        dve.wait_ge(out_mm, g + 1)
                        at = bass.ds(g * GT, GT)
                        nc.vector.tensor_tensor(x[:, at], x[:, at], banks[:, 2, :], ALU.add).then_inc(x_added, 1)
                        assert last or st.n == PER, (tag, st.n)
                        dve_base[0] = base + pre.n + (NG - 1) * PER + st.n
                    over_pairs(dve, body)

        def route_phase(tag, mix):
            chunks, C, EX, hidden = mix.chunks, mix.C, mix.plain, mix.hidden
            K, cap = mix.topk, mix.cap
            NB, NU, NC = mix.banks, EX * mix.U, EX * mix.C
            per_choice = mix.layer == 0
            nk = K * NE if per_choice else NE
            CR = 4
            Y0, RT, TP = 4, 6, 7
            w0 = sum(PLAIN[0:mix.layer])
            wide = mix.up + mix.down
            plain_w = [w_plain[:, w0 + e * wide:w0 + (e + 1) * wide] for e in range(EX)]
            l_mm = signal(f"{tag}_l_mm")
            sub_done = signal(f"{tag}_sub")
            e_done = signal(f"{tag}_exp")
            oh_done = signal(f"{tag}_oh")
            r_mm = signal(f"{tag}_r_mm")
            h_mm = signal(f"{tag}_h_mm")
            a_done = signal(f"{tag}_a_done")
            m_done = signal(f"{tag}_m_done")
            y_mm = signal(f"{tag}_y_mm")
            y_used = signal(f"{tag}_y_used")
            idx_ready = signal(f"{tag}_idx")
            z_copied = signal(f"{tag}_z")
            sent = [signal(f"{tag}_sent{i}") for i in range(2)]
            out_free = signal(f"{tag}_out_free")
            LN0 = norms[0] - 1
            norms[0] += NG - 1
            base = dve_base[0]
            odd = EX % 2
            SENT = 16 * TG * K

            with nc.Block() as block:
                @block.gpsimd
                def _(pool):
                    pool.sem_inc(out_free, 2)
                    pool.wait_ge(cleared, clears)
                    if mix.layer:
                        nc.gpsimd.memset(count[:], 0.0).then_inc(pool_step, 1)
                        pool_base[0] += 1
                        pool.wait_ge(pool_step, pool_base[0])

                    def body(g, last, slot, nth):
                        if not last:
                            norm_power(pool, g + (LN0 + 2))
                        pool.wait_ge(idx_ready, g + 2)
                        pool.wait_ge(z_copied, g + 1)
                        pool.nop(nofuse=True)
                        for i in range(TG):
                            for k in range(K):
                                c = i * K + k
                                pool.indirect_dma_start(x_rows[:, :],
                                                        bass.IndirectOffsetOnAxis(ap=idx_out[:, slot, c:c + 1], axis=0),
                                                        z_out[:, slot, i * D:(i + 1) * D], None).then_inc(sent[slot], 16)
                        if not (isinstance(g, int) and g == 0):
                            pool.wait_ge(sent[1 - slot], (nth + slot) * SENT)
                            pool.sem_inc(out_free, 1)
                    over_slots(pool, body)
                    pool.wait_ge(sent[1], NG // 2 * SENT)

                @block.tensor
                def _(pe):
                    if EX:
                        pe.sem_inc(y_mm, 2)

                    def rise(g, e):
                        n = e * mix.U
                        for c, (at, w) in enumerate(chunks):
                            for part in range(2):
                                q = n - NB
                                pe.wait_ge(m_done if q % 2 else a_done, g * NC + (q // 2 + 1 + CR))
                                up = plain_w[e][:, part * hidden + at:part * hidden + at + w]
                                nc.tensor.matmul(banks[0:w, n % NB, :], up, zT[:, :], start=True, stop=True).then_inc(h_mm, 1)
                                n += 1

                    def fall(g, e):
                        pe.wait_ge(m_done, g * NC + ((e + 1) * C + CR))
                        pe.wait_ge(y_used, g * EX + (e + 1 + (odd if e == 0 else 0)))
                        for i in range(TG):
                            for c, (_, w) in enumerate(chunks):
                                r = nc.tensor.matmul(banks[:, Y0 + e % 2, i * D:(i + 1) * D],
                                                     hid[0:w, e % 2, c, i * P:(i + 1) * P],
                                                     plain_w[e][0:w, mix.up + c * D:mix.up + (c + 1) * D],
                                                     start=(c == 0), stop=(c == C - 1))
                        r.then_inc(y_mm, 1)

                    def body(g, last):
                        pe.wait_ge(zT_ready, g + (LN0 + 1))
                        pe.wait_ge(idx_ready, g + 1)
                        for i in range(TG):
                            r = nc.tensor.matmul(banks[:, RT, i * NE:(i + 1) * NE], zT[:, i * P:(i + 1) * P],
                                                 sm(f"rw{mix.layer}"), start=True, stop=True)
                        r.then_inc(l_mm, 1)
                        if EX:
                            rise(g, 0)
                        pe.wait_ge(oh_done, g + 1)
                        chosen = oh[:, :, 0:K, :].rearrange("p i k n -> p i (k n)") if per_choice or K == 1 else ohc[:, :, :]
                        R = banks[:, RT, 64:64 + TG * nk].rearrange("p (i n) -> p i n", n=nk)
                        T = banks[:, RT, 160:160 + nk]
                        nc.tensor.matmul(R, tri_bf[:, :], chosen, start=True, stop=False)
                        for i in range(TG - 1):
                            nc.tensor.matmul(R[:, i + 1:TG, :], one_bf[:, :],
                                             chosen[:, i:i + 1, :].to_broadcast([P, TG - 1 - i, nk]),
                                             start=False, stop=(i == TG - 2))
                        for i in range(TG):
                            r = nc.tensor.matmul(T, one_bf[:, :], chosen[:, i, :], start=(i == 0), stop=(i == TG - 1))
                        r.then_inc(r_mm, 1)
                        for e in range(EX):
                            if e + 1 < EX:
                                rise(g, e + 1)
                            elif not last and EX > 1:
                                norm_transpose(pe, g + (LN0 + 2), TP)
                            fall(g, e)
                        if not last and EX <= 1:
                            norm_transpose(pe, g + (LN0 + 2), TP)
                    over_groups(pe, body)

                @block.scalar
                def _(act):
                    act.sem_inc(a_done, CR)

                    def body(g, last, slot, nth):
                        act.wait_ge(z_ready, g + (LN0 + 1))
                        act.wait_ge(out_free, g + 1)
                        nc.scalar.copy(z_out[:, slot, :], z[:, :]).then_inc(z_copied, 1)
                        for e in range(EX):
                            for c, (_, w) in enumerate(chunks):
                                n = e * C + c
                                act.wait_ge(h_mm, g * NU + (2 * n + 1))
                                act.wait_ge(m_done, g * NC + (n - NC + 1 + CR))
                                nc.scalar.activation(aux[0:w, n, :], banks[0:w, (2 * n) % NB, :],
                                                     mix.act_fn).then_inc(a_done, 1)
                        if not last:
                            norm_store(act, g + (LN0 + 2), TP)
                    over_slots(act, body)
                    act.wait_ge(sub_done, NG)
                    nc.scalar.activation(el_all[:, :, :], ls_all[:, :, :], ACT.Exp).then_inc(e_done, 1)

                @block.vector
                def _(dve):
                    dve.sem_inc(idx_ready, 1)
                    if EX:
                        dve.sem_inc(y_used, 2)
                        dve.sem_inc(m_done, CR)
                    dve.wait_ge(pool_step, pool_base[0])
                    PER = STEPS[tag]

                    def gate(g, e):
                        dve.wait_ge(y_mm, g * EX + (e + 1 + (odd if e == 0 else 0)))
                        for c, (_, w) in enumerate(chunks):
                            n = e * C + c
                            dve.wait_ge(a_done, g * NC + (n + 1 + CR))
                            dve.wait_ge(h_mm, g * NU + (2 * n + 2))
                            nc.vector.tensor_tensor(hid[0:w, e % 2, c, :], aux[0:w, n, :],
                                                    banks[0:w, (2 * n + 1) % NB, :], ALU.mult).then_inc(m_done, 1)

                    def next_rows_ready(g):
                        dve.wait_ge(z_copied, g + 1)
                        norm_apply(dve, g + (LN0 + 2), (g + 1) * GT)

                    def choose(st, g):
                        dve.wait_ge(l_mm, g + 1)
                        L = banks[:, RT, 0:TG * NE].rearrange("p (i n) -> p i n", n=NE)
                        if mix.layer == 2:
                            st.do(nc.vector.tensor_tensor(lg[:, :, :], L, sm("ebias2").unsqueeze(1).to_broadcast([P, TG, NE]), ALU.add))
                        else:
                            st.do(nc.vector.tensor_copy(lg[:, :, :], L))
                        st.settle(apart=True)
                        for i in range(TG):
                            st.do(nc.vector.max(mx8[:, i, :], lg[:, i, :]))
                        st.settle()
                        nc.vector.tensor_tensor(ls_all[:, bass.ds(g * TG, TG), :], mx8[:, :, :],
                                                mx8[:, :, 0:1].to_broadcast([P, TG, NE]),
                                                ALU.subtract).then_inc(sub_done, 1)
                        for i in range(TG):
                            st.do(nc.vector.max_index(ix8[:, i, :], mx8[:, i, :], lg[:, i, :]))
                        st.settle()
                        st.do(nc.vector.tensor_copy(ixf[:, :, :], ix8[:, :, 0:2]))
                        st.settle()
                        for k in range(K):
                            r = nc.vector.tensor_tensor(oh[:, :, k, :], iota8.unsqueeze(1).to_broadcast([P, TG, NE]),
                                                        ixf[:, :, k:k + 1].to_broadcast([P, TG, NE]), ALU.is_equal)
                            if k < K - 1 or not (per_choice or K == 1):
                                st.do(r)
                        if not (per_choice or K == 1):
                            st.settle()
                            r = nc.vector.tensor_tensor(ohc[:, :, :], oh[:, :, 0, :], oh[:, :, 1, :], ALU.add)
                        r.then_inc(oh_done, 1)

                    def place(st, g, slot):
                        n = TG * K
                        R = banks[:, RT, 64:64 + TG * nk].rearrange("p (i n) -> p i n", n=nk)
                        dve.wait_ge(r_mm, g + 1)
                        st.do(nc.vector.tensor_tensor(rank[:, :, 0:nk], R, count[:, 0:nk].unsqueeze(1).to_broadcast([P, TG, nk]), ALU.add))
                        st.settle()
                        st.do(nc.vector.tensor_tensor(count[:, 0:nk], count[:, 0:nk], banks[:, RT, 160:160 + nk], ALU.add))
                        for k in range(K):
                            a = k * NE if per_choice else 0
                            st.do(nc.vector.tensor_tensor(picked[:, :, k, :], oh[:, :, k, :], rank[:, :, a:a + NE], ALU.mult))
                        st.settle()
                        st.do(nc.vector.tensor_reduce(rk[:, :, 0:K], picked[:, :, 0:K, :], AX.X, ALU.add))
                        st.settle()
                        for k in range(K):
                            st.do(nc.vector.tensor_scalar(row[:, :, k], ixf[:, :, k], float(mix.region),
                                                          float((k * CAP0 if per_choice else 0) - 1), ALU.mult, ALU.add))
                        st.settle()
                        st.do(nc.vector.tensor_tensor(row[:, :, 0:K], row[:, :, 0:K], rk[:, :, 0:K], ALU.add))
                        st.settle()
                        if cap:
                            st.do(nc.vector.tensor_scalar(within[:, :, 0:K], rk[:, :, 0:K], float(cap), None, ALU.is_le))
                            st.settle()
                            aside = const[:, bass.ds(g * n + C_TRASH, n)].rearrange("p (i k) -> p i k", k=K)
                            for other, op in ((aside, ALU.subtract), (within[:, :, 0:K], ALU.mult), (aside, ALU.add)):
                                st.do(nc.vector.tensor_tensor(row[:, :, 0:K], row[:, :, 0:K], other, op))
                                st.settle()
                        here = bass.ds(g * n, n)
                        if per_choice:
                            st.do(nc.vector.tensor_scalar(idx_all[:, here].rearrange("p (i k) -> p i k", k=K), row[:, :, 0:K],
                                                          float(TRASH), None, ALU.min))
                        else:
                            st.do(nc.vector.tensor_copy(ix_all[:, here].rearrange("p (i k) -> p i k", k=K), ixf[:, :, 0:K]))
                        st.do(nc.vector.tensor_copy(rk_all[:, here].rearrange("p (i k) -> p i k", k=K), rk[:, :, 0:K]))
                        dve.wait_ge(out_free, g + 1)
                        nc.vector.tensor_copy(idx_out[:, slot, 0:n].rearrange("p (i k) -> p i k", k=K), row[:, :, 0:K])\
                            .then_inc(idx_ready, 1)

                    def weigh(st):
                        v, n = nc.vector, B * K
                        wts = wt_all[:, 0:n].rearrange("p (b k) -> p b k", k=K)
                        if cap:
                            st.do(v.tensor_scalar(ok_all[:, 0:n], rk_all[:, 0:n], float(cap), None, ALU.is_le))
                        dve.wait_ge(e_done, 1)
                        st.do(v.tensor_reduce(den_all[:, :], el_all[:, :, 0:2] if mix.renorm else el_all[:, :, :], AX.X, ALU.add))
                        st.settle()
                        st.do(v.reciprocal(rden_all[:, :], den_all[:, :]))
                        st.settle()
                        st.do(v.tensor_tensor(wts, el_all[:, :, 0:K], rden_all[:, :].unsqueeze(2).to_broadcast([P, B, K]), ALU.mult))
                        st.settle()
                        if cap:
                            st.do(v.tensor_tensor(wt_all[:, 0:n], wt_all[:, 0:n], ok_all[:, 0:n], ALU.mult))
                            st.settle()

                    def body(g, last, slot, nth):
                        st = Steps(dve, dve_step, g * PER + base)
                        if not last:
                            norm_stats(dve, st, (g + 1) * GT)
                        choose(st, g)
                        if not last and K == 1:
                            next_rows_ready(g)
                        if EX:
                            gate(g, 0)
                        place(st, g, slot)
                        if not last and K > 1:
                            next_rows_ready(g)
                        for e in range(EX):
                            if e + 1 < EX:
                                gate(g, e + 1)
                            dve.wait_ge(y_mm, g * EX + (e + 3))
                            dve.wait_ge(y_used, g * EX + (e + 2))
                            at = bass.ds(g * GT, GT)
                            nc.vector.tensor_tensor(x[:, at], x[:, at], banks[:, Y0 + e % 2, :], ALU.add).then_inc(y_used, 1)
                        assert last or st.n == PER, (tag, st.n)
                        dve_base[0] = base + (NG - 1) * PER + st.n
                    over_slots(dve, body)
                    st = Steps(dve, dve_step, dve_base[0])
                    st.settle()
                    weigh(st)
                    if not per_choice:
                        plan_blocks(st, mix)
                    dve_base[0] += st.n

        def plan_blocks(st, mix):
            v, K, NBK = nc.vector, mix.topk, mix.blocks
            if mix.cap:
                st.do(v.tensor_scalar(count[:, 0:NE], count[:, 0:NE], float(mix.cap), None, ALU.min))
                st.settle()
            over = hid[:, 0, 0, 0:NE * 16].rearrange("p (e m) -> p e m", m=16)
            st.do(v.tensor_tensor(over, count[:, 0:NE].unsqueeze(2).to_broadcast([P, NE, 16]),
                                  const[:, C_STEP:C_STEP + 16].unsqueeze(1).to_broadcast([P, NE, 16]), ALU.is_gt))
            st.settle()
            st.do(v.tensor_reduce(nblk[:, 0, :], over, AX.X, ALU.add))
            st.settle()
            src = 0
            for d, dst in ((1, 1), (2, 2), (4, 1)):
                st.do(v.tensor_copy(nblk[:, dst, 0:d], nblk[:, src, 0:d]))
                st.do(v.tensor_tensor(nblk[:, dst, d:NE], nblk[:, src, d:NE], nblk[:, src, 0:NE - d], ALU.add))
                st.settle()
                src = dst
            ends = nblk[:, src, :]
            st.do(v.tensor_tensor(first[:, :], ends, nblk[:, 0, :], ALU.subtract))
            st.settle()
            blk = const[0:1, C_BLK:C_BLK + NBK]
            past = hid[0:1, 1, 0, 0:NBK * NE].rearrange("p (j e) -> p j e", e=NE)
            held = hid[0:1, 1, 1, 0:NBK * NE].rearrange("p (j e) -> p j e", e=NE)
            st.do(v.tensor_tensor(past, ends[0:1].unsqueeze(1).to_broadcast([1, NBK, NE]),
                                  blk.unsqueeze(2).to_broadcast([1, NBK, NE]), ALU.is_le))
            st.settle()
            st.do(v.tensor_tensor(held, past, nblk[0:1, 0, :].unsqueeze(1).to_broadcast([1, NBK, NE]), ALU.mult))
            st.do(v.tensor_reduce(tab[:, 0, 0:NBK], past, AX.X, ALU.add))
            st.settle()
            st.do(v.tensor_reduce(tab[:, 1, 0:NBK], held, AX.X, ALU.add))
            st.do(v.tensor_scalar(tab_e[:, 0:NBK], tab[:, 0, 0:NBK], float(NE - 1), None, ALU.min))
            st.settle()
            st.do(v.tensor_tensor(tab[:, 1, 0:NBK], blk, tab[:, 1, 0:NBK], ALU.subtract))
            st.do(v.tensor_scalar(tab[:, 2, 0:NBK], tab[:, 0, 0:NBK], float(mix.region), None, ALU.mult))
            st.settle()
            st.do(v.scalar_tensor_tensor(out=tab[:, 0, 0:NBK], in0=tab[:, 1, 0:NBK], scalar=float(BLK), in1=tab[:, 2, 0:NBK],
                                         op0=ALU.mult, op1=ALU.add))
            st.settle()
            st.do(v.tensor_scalar(tab_r[:, 0:NBK], tab[:, 0, 0:NBK], float(NE * mix.region - BLK), None, ALU.min))
            n = B * K
            eq = hid[:, 0, 1, 0:n * NE].rearrange("p (n e) -> p n e", e=NE)
            st.do(v.tensor_tensor(eq, iota8.unsqueeze(1).to_broadcast([P, n, NE]),
                                  ix_all[:, 0:n].unsqueeze(2).to_broadcast([P, n, NE]), ALU.is_equal))
            st.settle()
            st.do(v.tensor_tensor(eq, eq, first[:, :].unsqueeze(1).to_broadcast([P, n, NE]), ALU.mult))
            st.settle()
            st.do(v.tensor_reduce(pos[:, 0:n], eq, AX.X, ALU.add))
            st.settle()
            st.do(v.tensor_scalar(pos[:, 0:n], pos[:, 0:n], float(BLK), -1.0, ALU.mult, ALU.add))
            st.settle()
            st.do(v.tensor_tensor(pos[:, 0:n], pos[:, 0:n], rk_all[:, 0:n], ALU.add))
            st.settle()
            if mix.cap:
                st.do(v.scalar_tensor_tensor(out=pos[:, 0:n], in0=pos[:, 0:n], scalar=float(TRASH), in1=ok_all[:, 0:n],
                                             op0=ALU.subtract, op1=ALU.mult))
                st.settle()
                st.do(v.tensor_scalar(pos[:, 0:n], pos[:, 0:n], float(TRASH), None, ALU.add))
                st.settle()
            st.do(v.tensor_copy(idx_all[:, 0:n], pos[:, 0:n]))
            st.settle()

        def block_phase(tag, mix):
            chunks, C, U, NB, N = mix.chunks, mix.C, mix.U, mix.banks, mix.rows
            T, QUADS = N // P, mix.blocks // WS
            CR = 2 * C
            w_in = [signal(f"{tag}_w_in{q}") for q in range(WS)]
            x_in = [signal(f"{tag}_x_in{q}") for q in range(WS)]
            y_st = [signal(f"{tag}_y_st{s}") for s in range(2)]
            t_mm = signal(f"{tag}_t_mm")
            xt_done = signal(f"{tag}_xt")
            h_mm = signal(f"{tag}_h_mm")
            a_done = signal(f"{tag}_a_done")
            m_done = signal(f"{tag}_m_done")
            y_mm = signal(f"{tag}_y_mm")
            y_used = signal(f"{tag}_y_used")
            hid_done = m_done if mix.glu else a_done
            w = ins[f"w{mix.layer}"]
            aux8 = aux[:, :, :].rearrange("p a (h b) -> p (a h) b", h=2)

            def over_quads(eng, body):
                with eng.Fori(0, QUADS - 1) as i:
                    body(i, False)
                body(QUADS - 1, True)

            def at_block(i, q):
                return (i + 1, q - WS) if q >= WS else (i, q)

            with nc.Block() as block:
                @block.sync
                def _(sp):
                    def load(i, q):
                        n = i * WS + q
                        if mix.layer == 0:
                            e, r0 = i * (WS // 2) + q // 2, n * N
                        else:
                            e = sp.value_load(tab_e[0:1, bass.ds(n, 1)], min_val=0, max_val=NE - 1)
                            r0 = sp.value_load(tab_r[0:1, bass.ds(n, 1)], min_val=0, max_val=X_ROWS - N)
                        sp.dma_start(xin[:, q, 0:N].rearrange("p (t d) -> p t d", d=D),
                                     x_rows[bass.ds(r0, N), :].rearrange("(t p) d -> p t d", p=P)).then_inc(x_in[q], 16)
                        sp.dma_start(w_exp[:, q, 0:mix.width].unsqueeze(1),
                                     w[bass.ds(e, 1), :, :].rearrange("e p w -> p e w")).then_inc(w_in[q], 16)

                    for q in range(WS):
                        load(0, q)

                    def body(i, last):
                        for q in range(WS):
                            s, n = q % 2, i * WS + q
                            sp.wait_ge(y_used, n + 3)
                            sp.dma_start(y_rows[bass.ds(n * N, N), :].rearrange("(t p) d -> p t d", p=P),
                                         y_out[:, s, 0:N].rearrange("p (t d) -> p t d", d=D)).then_inc(y_st[s], 16)
                            if not last:
                                load(i + 1, q)
                    over_quads(sp, body)
                    for s in range(2):
                        sp.wait_ge(y_st[s], 16 * (QUADS * WS // 2 + 1))

                @block.tensor
                def _(pe):
                    pe.sem_inc(t_mm, 2)
                    pe.sem_inc(h_mm, 2 * U)
                    pe.sem_inc(y_mm, 2)

                    def turn(i, q):
                        i, q = at_block(i, q)
                        pe.wait_ge(x_in[q], i * 16 + 16)
                        pe.wait_ge(xt_done, i * WS + (q + 1))
                        for t in range(T):
                            r = nc.tensor.transpose(banks[:, 7, t * P:(t + 1) * P], xin[:, q, t * D:(t + 1) * D], ident)
                        r.then_inc(t_mm, 1)

                    def rise(i, q):
                        i, q = at_block(i, q)
                        n = i * WS + q
                        pe.wait_ge(xt_done, n + 2)
                        pe.wait_ge(w_in[q], i * 16 + 16)
                        for u in range(U):
                            c, part = u // mix.parts, u % mix.parts
                            at, wd = chunks[c]
                            at += part * mix.hidden
                            b = u - NB
                            if not mix.glu:
                                pe.wait_ge(a_done, n * C + (b + 1 + CR))
                            else:
                                pe.wait_ge(m_done if b % 2 else a_done, n * C + (b // 2 + 1 + CR))
                            nc.tensor.matmul(banks[0:wd, u % NB, 0:N], w_exp[:, q, at:at + wd], xT[:, q % 2, 0:N],
                                             start=True, stop=True).then_inc(h_mm, 1)

                    def fall(i, q):
                        s, n = q % 2, i * WS + q
                        pe.wait_ge(hid_done, n * C + (C + CR))
                        pe.wait_ge(y_used, n + 1)
                        for t in range(T):
                            for c, (_, wd) in enumerate(chunks):
                                at = mix.up + c * D
                                r = nc.tensor.matmul(banks[:, 5 + s, t * D:(t + 1) * D], hid[0:wd, s, c, t * P:(t + 1) * P],
                                                     w_exp[0:wd, q, at:at + D], start=(c == 0), stop=(c == C - 1))
                        r.then_inc(y_mm, 1)

                    turn(0, 0)
                    turn(0, 1)
                    rise(0, 0)

                    def body(i, last):
                        for q in range(WS):
                            if not last or q + 1 < WS:
                                rise(i, q + 1)
                            if not last or q + 2 < WS:
                                turn(i, q + 2)
                            fall(i, q)
                    over_quads(pe, body)

                @block.scalar
                def _(act):
                    act.sem_inc(a_done, CR)
                    with act.Fori(0, QUADS) as i:
                        for q in range(WS):
                            s, n = q % 2, i * WS + q
                            for c, (_, wd) in enumerate(chunks):
                                act.wait_ge(h_mm, n * U + (c * mix.parts + 1 + 2 * U))
                                src = banks[0:wd, (c * mix.parts) % NB, 0:N]
                                if mix.glu:
                                    act.wait_ge(m_done, n * C + (c + 1))
                                    nc.scalar.activation(aux8[0:wd, s * C + c, 0:N], src, mix.act_fn).then_inc(a_done, 1)
                                else:
                                    if c == 0:
                                        act.wait_ge(y_mm, n + 1)
                                    at = mix.up + mix.down + c
                                    bias = w_exp[:, q, at:at + 1] if mix.bias else zero1
                                    nc.scalar.activation(hid[0:wd, s, c, 0:N], src, mix.act_fn, bias=bias).then_inc(a_done, 1)

                @block.vector
                def _(dve):
                    dve.sem_inc(xt_done, 1)
                    dve.sem_inc(y_used, 2)
                    dve.sem_inc(m_done, CR)
                    for s in range(2):
                        dve.sem_inc(y_st[s], 16)

                    def keep_xT(i, q):
                        i, q = at_block(i, q)
                        n = i * WS + q
                        dve.wait_ge(t_mm, n + 3)
                        dve.wait_ge(h_mm, n * U + U)
                        nc.vector.tensor_copy(xT[:, q % 2, 0:N], banks[:, 7, 0:N]).then_inc(xt_done, 1)

                    def gate(i, q):
                        if not mix.glu:
                            return
                        i, q = at_block(i, q)
                        s, n = q % 2, i * WS + q
                        dve.wait_ge(y_mm, n + 1)
                        for c, (_, wd) in enumerate(chunks):
                            dve.wait_ge(a_done, n * C + (c + 1 + CR))
                            dve.wait_ge(h_mm, n * U + (2 * c + 2 + 2 * U))
                            nc.vector.tensor_tensor(hid[0:wd, s, c, 0:N], aux8[0:wd, s * C + c, 0:N],
                                                    banks[0:wd, (2 * c + 1) % NB, 0:N], ALU.mult).then_inc(m_done, 1)

                    def take(i, q):
                        s, n = q % 2, i * WS + q
                        dve.wait_ge(y_mm, n + 3)
                        dve.wait_ge(y_st[s], i * (WS // 2 * 16) + 16 * (q // 2 + 1))
                        yb = banks[:, 5 + s, 0:N]
                        if mix.bias:
                            at = mix.up + mix.down + C
                            r = nc.vector.tensor_tensor(y_out[:, s, 0:N].rearrange("p (t d) -> p t d", d=D),
                                                        yb.rearrange("p (t d) -> p t d", d=D),
                                                        w_exp[:, q, at:at + D].unsqueeze(1).to_broadcast([P, T, D]), ALU.add)
                        else:
                            r = nc.vector.tensor_copy(y_out[:, s, 0:N], yb)
                        r.then_inc(y_used, 1)

                    keep_xT(0, 0)
                    keep_xT(0, 1)
                    gate(0, 0)

                    def body(i, last):
                        for q in range(WS):
                            if not last or q + 1 < WS:
                                gate(i, q + 1)
                            if not last or q + 2 < WS:
                                keep_xT(i, q + 2)
                            take(i, q)
                    over_quads(dve, body)

        def end_phase(tag, comb_mix):
            comb = Combine(tag, comb_mix, depth=2)
            base = dve_base[0]
            PER = STEPS[tag]
            with nc.Block() as block:
                @block.gpsimd
                def _(pool):
                    with pool.Fori(0, NG // 2) as pair:
                        for half in range(2):
                            comb.gather(pool, pair * 2 + half, half, pair)

                @block.vector
                def _(dve):
                    comb.start(dve)
                    with dve.Fori(0, NG // 2) as pair:
                        for half in range(2):
                            st = Steps(dve, dve_step, (pair * 2 + half) * PER + base)
                            comb.add(dve, st, pair * 2 + half, half, pair)
                            assert st.n == PER, (tag, st.n)

                @block.sync
                def _(sp):
                    with sp.Fori(0, NG) as g:
                        sp.wait_ge(comb.added, g * TG + (TG + comb.ahead))
                        sp.dma_start(out[:, bass.ds(g * GT, GT)], x[:, bass.ds(g * GT, GT)]).then_inc(stored, 16)
                    sp.wait_ge(stored, 16 * NG)

        for phase, *args in ((heads_phase, "a0", False, None), (route_phase, "r0", MIX[0]), (block_phase, "b0", MIX[0]),
                             (plain_phase, "a1", MIX[0]), (route_phase, "r1", MIX[1]), (block_phase, "b1", MIX[1]),
                             (gelu_phase, "a2", MIX[1]), (route_phase, "r2", MIX[2]), (block_phase, "b2", MIX[2]),
                             (heads_phase, "a3", True, MIX[2]), (route_phase, "r3", MIX[3]), (block_phase, "b3", MIX[3]),
                             (end_phase, "end", MIX[3])):
            with nc.cleanup_on_exit():
                phase(*args)


def lay_out(inputs):
    import numpy as np

    def f32(name):
        return np.ascontiguousarray(inputs[name])

    a = {}
    xs, cs = f32("x"), f32("ctx_1024")
    a["x"] = xs.transpose(1, 0, 2).reshape(P, B * D)
    a["ctxT"] = cs.transpose(2, 0, 1).reshape(D, B * KV)
    a["ctxk"] = cs.transpose(1, 0, 2).reshape(KV, B * D)
    a["mask"] = f32("mask_1x1xSxS2_ik0").reshape(P, KV)
    const = np.zeros((P, C_N), np.float32)
    const[:, C_ID:C_ID + P] = np.eye(P)
    const[:, C_TRI:C_TRI + P] = np.triu(np.ones((P, P)))
    const[:, C_IOTA:C_IOTA + NE] = np.arange(NE)
    const[:, C_QUAD:C_QUAD + HQ] = np.kron(np.eye(HQ), np.ones((32, 1)))
    const[:, C_TRASH:C_LOW] = Y_ROWS + P * np.arange(2 * B) + np.arange(P)[:, None]
    const[:, C_STEP:C_STEP + 16] = BLK * np.arange(16)
    const[:, C_BLK:C_BLK + NBLK] = np.arange(NBLK)
    a["const"] = const
    r = np.arange(P)
    dim = HD * (HQ * np.arange(HQ)[:, None] + r // 32) + r % HD
    low = {"q": r // HD % 2 == 1, "k": r // HD % HQ >= 2}
    for i, side in enumerate("qk"):
        const[:, C_LOW + i] = low[side]
    small = np.zeros((P, SMALL_N), np.float32)

    def put(name, v):
        o, w = SMALL[name]
        small[0:v.shape[0], o:o + w] = v
    for side in "qk":
        spread_bias = f32(f"L3_xattn_b{side}")[dim].T
        put(f"b{side}3", spread_bias)
        put(f"b{side}3m", np.where(low[side][:, None], spread_bias, np.float32(0)))
    put("bv3", np.broadcast_to(f32("L3_xattn_bv")[None], (P, D)))
    put("bo3", np.broadcast_to(f32("L3_xattn_bo")[None], (P, D)))
    put("bias0", np.broadcast_to(f32("L0_ffn_bias").reshape(1, D), (P, D)))
    put("ebias2", np.broadcast_to(f32("L2_ffn_expert_bias")[None], (P, NE)))
    put("rw0", f32("L0_ffn_router_w"))
    put("rw1", f32("L1_ffn_gate_w"))
    put("rw2", f32("L2_ffn_router_w").T)
    put("rw3", f32("L3_ffn_wg"))
    a["small"] = small
    weights = {n: f32(f"L{n[1]}_xattn_W{n[0]}").T for n in AW}
    a["aw"] = np.concatenate([w[:, dim.reshape(-1)] if n[0] in "qk" else w for n, w in weights.items()], axis=1)

    def packed(up, down, *more):
        e, h = down.shape[0], down.shape[1]
        c = -(-h // P)
        dn = np.zeros((e, c * P, D), np.float32)
        dn[:, :h] = down
        return np.concatenate([up, dn.reshape(e, c, P, D).transpose(0, 2, 1, 3).reshape(e, P, -1), *more], axis=2)

    def gated(names):
        return np.concatenate([f32(n).transpose(0, 2, 1) for n in names], axis=2)

    a["w0"] = packed(f32("L0_ffn_w1"), f32("L0_ffn_w2"))
    a["w1"] = packed(f32("L1_ffn_exp_wgu"), f32("L1_ffn_exp_wd"))
    a["w2"] = packed(gated(("L2_ffn_w1", "L2_ffn_w3")), f32("L2_ffn_w2").transpose(0, 2, 1))
    a["w3"] = packed(f32("L3_ffn_W1"), f32("L3_ffn_W2"), f32("L3_ffn_b1").reshape(NE, 4, P).transpose(0, 2, 1),
                     np.broadcast_to(f32("L3_ffn_b2")[:, None], (NE, P, D)))
    plain = [packed(f32("L1_ffn_base_wgu")[None], f32("L1_ffn_base_wd")[None]),
             packed(gated(("L2_ffn_sw1", "L2_ffn_sw3")), f32("L2_ffn_sw2").transpose(0, 2, 1))]
    a["plain"] = np.concatenate([w for p in plain for w in p], axis=1)
    return {k: np.ascontiguousarray(v) for k, v in a.items()}


def kernel(**inputs):
    import concourse.bacc as _bacc
    from concourse.bass_utils import run_bass_kernel_spmd as _run

    arrays = lay_out(inputs)
    nc = _bacc.Bacc("TRN2", target_bir_lowering=False, num_devices=1)
    ins = {k: nc.dram_tensor(f"in_{k}", v.shape, mybir.dt.from_np(v.dtype), kind="ExternalInput").ap()
           for k, v in arrays.items()}
    out = nc.dram_tensor("out_0", (P, B * D), F32, kind="ExternalOutput").ap()
    build(nc, ins, out)
    r = _run(nc, [{f"in_{k}": v for k, v in arrays.items()}], core_ids=[0])
    return r.results[0]["out_0"].reshape(P, B, D).transpose(1, 0, 2)
```
